# Optimizing a Trainium2 kernel written in Bass

```python
import numpy as np
import jax
import jax.numpy as jnp

def _softmax(x, axis=-1):
    return jax.nn.softmax(x, axis=axis)

def _gelu(x):
    return jax.nn.gelu(x, approximate=True)

def _silu(x):
    return jax.nn.silu(x)

def _sigmoid(x):
    return jax.nn.sigmoid(x)

def _layernorm(x, axis=-1, eps=1e-05):
    m = jnp.mean(x, axis=axis, keepdims=True)
    v = jnp.var(x, axis=axis, keepdims=True)
    return (x - m) / jnp.sqrt(v + eps)

def _scatter_add(tgt, idx, src, axis=0):
    return tgt.at[idx].add(src)

def _segment_sum(src, seg, n):
    return jax.ops.segment_sum(src, seg, n)
kernel_name = 'mk_adaln_attn_ffn_d2_seqx_r8_cf8cfb'

def setup_inputs(seed: int=0):
    np.random.seed(seed)
    _w = jnp.asarray

    def _rec_inputs():
        import jax
        import jax.numpy as jnp
        _rk = jax.random.key(seed)
        x = 4.136e-05 + 0.9999 * jax.random.normal(jax.random.fold_in(_rk, 1), (32, 128, 128), jnp.float32)
        _lenS = 128 - jax.random.randint(jax.random.fold_in(_rk, 7), (32,), 0, max(1, 128 // 4) + 1, jnp.int32)
        _lenS2 = 128 - jax.random.randint(jax.random.fold_in(_rk, 8), (32,), 0, max(1, 128 // 4) + 1, jnp.int32)
        cond_1024 = -0.00608245 + 1.00131 * jax.random.normal(jax.random.fold_in(_rk, 11), (32, 128), jnp.float32)
        return (x, cond_1024)
    x, cond_1024 = _rec_inputs()

    def _L0_cond_setup():
        import jax, jax.numpy as jnp
        import numpy as np
        B, T, D_IN, V_IN, E = (64, 128, 128, 128, 128)
        key = jax.random.key(seed)
        ks = jax.random.split(key, 16)
        s = 0.01
        return {'video': jax.random.normal(ks[0], (B, V_IN), jnp.float32), 'seq': jax.random.normal(ks[1], (B, T, D_IN), jnp.float32), 'W_z': jax.random.normal(ks[2], (D_IN, E), jnp.float32) * s, 'U_z': jax.random.normal(ks[3], (E, E), jnp.float32) * s, 'C_z': jax.random.normal(ks[4], (V_IN, E), jnp.float32) * s, 'b_z': jnp.zeros((E,), jnp.float32), 'W_r': jax.random.normal(ks[5], (D_IN, E), jnp.float32) * s, 'U_r': jax.random.normal(ks[6], (E, E), jnp.float32) * s, 'C_r': jax.random.normal(ks[7], (V_IN, E), jnp.float32) * s, 'b_r': jnp.zeros((E,), jnp.float32), 'W': jax.random.normal(ks[8], (D_IN, E), jnp.float32) * s, 'U': jax.random.normal(ks[9], (E, E), jnp.float32) * s, 'C': jax.random.normal(ks[10], (V_IN, E), jnp.float32) * s, 'b': jnp.zeros((E,), jnp.float32)}
    _L0_cond_all = _L0_cond_setup()
    _L0_cond_in = {k: v for k, v in _L0_cond_all.items() if k in ('W_z', 'U_z', 'C_z', 'b_z', 'W_r', 'U_r', 'C_r', 'b_r', 'W', 'U', 'C', 'b')}
    del _L0_cond_all

    def _L0_attn_setup():
        import jax, jax.numpy as jnp
        import numpy as np
        import math
        N_STATE = 64
        H_MODEL = 128
        D_CONV = 16
        EXPAND = 2
        D_INNER = EXPAND * H_MODEL
        HEADDIM = H_MODEL // 4
        NHEADS = D_INNER // HEADDIM
        NGROUPS = 1
        CONV_DIM = D_INNER + 2 * NGROUPS * N_STATE
        D_IN_PROJ = 2 * D_INNER + 2 * NGROUPS * N_STATE + NHEADS
        BATCH, SEQLEN = (4, 256)

        def _mamba2(x, W_in, conv_w, conv_b, dt_bias, A_log, D, init_states, norm_w, W_out):
            b, l, _ = x.shape
            zxbcdt = x @ W_in
            z = zxbcdt[..., :D_INNER]
            xBC = zxbcdt[..., D_INNER:D_INNER + CONV_DIM]
            dt = jax.nn.softplus(zxbcdt[..., -NHEADS:] + dt_bias)
            kernel = conv_w.T[:, None, :]
            xBC = jax.lax.conv_general_dilated(xBC, kernel, window_strides=(1,), padding=[(D_CONV - 1, 0)], dimension_numbers=('NWC', 'WIO', 'NWC'), feature_group_count=CONV_DIM) + conv_b
            xBC = jax.nn.silu(xBC)
            xs = xBC[..., :D_INNER].reshape(b, l, NHEADS, HEADDIM)
            Bm = xBC[..., D_INNER:D_INNER + N_STATE]
            Cm = xBC[..., D_INNER + N_STATE:]
            A = -jnp.exp(A_log)
            dA = jnp.exp(dt * A)
            h0 = jnp.broadcast_to(init_states, (b, NHEADS, HEADDIM, N_STATE))

            def step(h, inp):
                dA_t, x_t, dt_t, B_t, C_t = inp
                dBx = jnp.einsum('bh,bhp,bn->bhpn', dt_t, x_t, B_t)
                h = h * dA_t[:, :, None, None] + dBx
                y_t = jnp.einsum('bhpn,bn->bhp', h, C_t)
                return (h, y_t)
            scan_in = (jnp.moveaxis(dA, 1, 0), jnp.moveaxis(xs, 1, 0), jnp.moveaxis(dt, 1, 0), jnp.moveaxis(Bm, 1, 0), jnp.moveaxis(Cm, 1, 0))
            _, ys = jax.lax.scan(step, h0, scan_in)
            y = jnp.moveaxis(ys, 0, 1) + D[None, None, :, None] * xs
            y = y.reshape(b, l, D_INNER)
            y = y * jax.nn.silu(z)
            y = y * jax.lax.rsqrt(jnp.mean(y * y, axis=-1, keepdims=True) + 1e-05) * norm_w
            return y @ W_out
        key = jax.random.key(seed)
        ks = jax.random.split(key, 10)
        x = jax.random.normal(ks[0], (BATCH, SEQLEN, H_MODEL), jnp.float32)
        W_in = jax.random.normal(ks[1], (H_MODEL, D_IN_PROJ), jnp.float32) * H_MODEL ** (-0.5)
        conv_w = jax.random.normal(ks[2], (CONV_DIM, D_CONV), jnp.float32) * D_CONV ** (-0.5)
        conv_b = jnp.zeros((CONV_DIM,), jnp.float32)
        dt0 = jnp.exp(jax.random.uniform(ks[3], (NHEADS,), minval=math.log(0.001), maxval=math.log(0.1)))
        dt_bias = jnp.log(jnp.expm1(dt0))
        A_log = jnp.log(jax.random.uniform(ks[4], (NHEADS,), minval=1.0, maxval=16.0))
        D = jnp.ones((NHEADS,), jnp.float32)
        init_states = jax.random.normal(ks[5], (NHEADS, HEADDIM, N_STATE), jnp.float32) * 0.01
        norm_w = jnp.ones((D_INNER,), jnp.float32)
        W_out = jax.random.normal(ks[6], (D_INNER, H_MODEL), jnp.float32) * D_INNER ** (-0.5)
        W_nl = jax.random.normal(ks[7], (H_MODEL, H_MODEL), jnp.float32) * H_MODEL ** (-0.5)
        b_nl = jnp.zeros((H_MODEL,), jnp.float32)
        return dict(x=x, W_in=W_in, conv_w=conv_w, conv_b=conv_b, dt_bias=dt_bias, A_log=A_log, D=D, init_states=init_states, norm_w=norm_w, W_out=W_out, W_nl=W_nl, b_nl=b_nl)
    _L0_attn_all = _L0_attn_setup()
    _L0_attn_in = {k: v for k, v in _L0_attn_all.items() if k in ('W_in', 'conv_w', 'conv_b', 'dt_bias', 'A_log', 'D', 'init_states', 'norm_w', 'W_out', 'W_nl', 'b_nl')}
    del _L0_attn_all

    def _L0_cond2_setup():
        import jax, jax.numpy as jnp
        import numpy as np
        NHID = 128
        NHEAD = 16
        HEAD_DIM = 64
        B, L = (8, 512)
        key = jax.random.key(seed)
        ks = jax.random.split(key, 12)
        s_in = 1.0 / np.sqrt(NHID)
        s_o = 1.0 / np.sqrt(NHEAD * HEAD_DIM)
        return {'x': jax.random.normal(ks[0], (B, L, NHID), dtype=jnp.float32), 'ax': jax.random.normal(ks[1], (B, NHID), dtype=jnp.float32), 'WQ_w': jax.random.normal(ks[2], (NHID, NHEAD * HEAD_DIM), dtype=jnp.float32) * s_in, 'WQ_b': jnp.zeros((NHEAD * HEAD_DIM,), dtype=jnp.float32), 'WK_w': jax.random.normal(ks[3], (NHID, NHEAD * HEAD_DIM), dtype=jnp.float32) * s_in, 'WK_b': jnp.zeros((NHEAD * HEAD_DIM,), dtype=jnp.float32), 'WV_w': jax.random.normal(ks[4], (NHID, NHEAD * HEAD_DIM), dtype=jnp.float32) * s_in, 'WV_b': jnp.zeros((NHEAD * HEAD_DIM,), dtype=jnp.float32), 'WO_w': jax.random.normal(ks[5], (NHEAD * HEAD_DIM, NHID), dtype=jnp.float32) * s_o, 'WO_b': jnp.zeros((NHID,), dtype=jnp.float32)}
    _L0_cond2_all = _L0_cond2_setup()
    _L0_cond2_in = {k: v for k, v in _L0_cond2_all.items() if k in ('WQ_w', 'WQ_b', 'WK_w', 'WK_b', 'WV_w', 'WV_b', 'WO_w', 'WO_b')}
    del _L0_cond2_all

    def _L0_ffn_setup():
        import jax, jax.numpy as jnp
        import numpy as np
        TOP_K = 2
        key = jax.random.key(seed)
        k1, k2, k3, k4, k5 = jax.random.split(key, 5)
        B, S, D, F, E = (2, 128, 128, 256, 8)
        return {'x': jax.random.normal(k1, (B, S, D), dtype=jnp.float32), 'router_kernel_DE': jax.random.normal(k2, (D, E), dtype=jnp.float32) * 0.02, 'kernel_gating_EDF': jax.random.normal(k3, (E, D, F), dtype=jnp.float32) * 0.02, 'kernel_up_EDF': jax.random.normal(k4, (E, D, F), dtype=jnp.float32) * 0.02, 'kernel_down_EFD': jax.random.normal(k5, (E, F, D), dtype=jnp.float32) * 0.02}
    _L0_ffn_all = _L0_ffn_setup()
    _L0_ffn_in = {k: v for k, v in _L0_ffn_all.items() if k in ('router_kernel_DE', 'kernel_gating_EDF', 'kernel_up_EDF', 'kernel_down_EFD')}
    del _L0_ffn_all

    def _L1_cond_setup():
        import jax, jax.numpy as jnp
        import numpy as np
        key = jax.random.key(seed)
        k1, k2, k3, k4 = jax.random.split(key, 4)
        N, T, D, H = (64, 64, 128, 128)
        x = jax.random.normal(k1, (N, T, D), dtype=jnp.float32)
        h0 = jax.random.normal(k2, (N, H), dtype=jnp.float32)
        Wx = jax.random.normal(k3, (D, 4 * H), dtype=jnp.float32) / np.sqrt(D)
        Wh = jax.random.normal(k4, (H, 4 * H), dtype=jnp.float32) / np.sqrt(H)
        b = jnp.zeros((4 * H,), dtype=jnp.float32)
        return {'x': x, 'h0': h0, 'Wx': Wx, 'Wh': Wh, 'b': b}
    _L1_cond_all = _L1_cond_setup()
    _L1_cond_in = {k: v for k, v in _L1_cond_all.items() if k in ('Wx', 'Wh', 'b')}
    del _L1_cond_all

    def _L1_attn_setup():
        import jax, jax.numpy as jnp
        import numpy as np
        EMBED = 128
        HEADS = 16
        HEAD_DIM = EMBED // HEADS
        NUM_BUCKETS = 32
        MAX_DISTANCE = 128
        B, L = (4, 256)

        def relative_position_bucket(relative_position, num_buckets=NUM_BUCKETS, max_distance=MAX_DISTANCE):
            n = -relative_position
            max_exact = num_buckets // 2
            is_small = n < max_exact
            nf = jnp.maximum(n, 1).astype(jnp.float32)
            val_if_large = max_exact + (jnp.log(nf / max_exact) / np.log(max_distance / max_exact) * (num_buckets - max_exact)).astype(jnp.int32)
            val_if_large = jnp.minimum(val_if_large, num_buckets - 1)
            ret = jnp.where(is_small, n, val_if_large)
            return jnp.maximum(ret, 0)
        key = jax.random.key(seed)
        ks = jax.random.split(key, 11)
        s = 0.02
        return {'x': jax.random.normal(ks[0], (B, L, EMBED), dtype=jnp.float32), 'wq': jax.random.normal(ks[1], (EMBED, EMBED), dtype=jnp.float32) * s, 'bq': jnp.zeros((EMBED,), dtype=jnp.float32), 'wk': jax.random.normal(ks[2], (EMBED, EMBED), dtype=jnp.float32) * s, 'bk': jnp.zeros((EMBED,), dtype=jnp.float32), 'wv': jax.random.normal(ks[3], (EMBED, EMBED), dtype=jnp.float32) * s, 'bv': jnp.zeros((EMBED,), dtype=jnp.float32), 'wo': jax.random.normal(ks[4], (EMBED, EMBED), dtype=jnp.float32) * s, 'bo': jnp.zeros((EMBED,), dtype=jnp.float32), 'rel_bias': jax.random.normal(ks[5], (NUM_BUCKETS, HEADS), dtype=jnp.float32) * s}
    _L1_attn_all = _L1_attn_setup()
    _L1_attn_in = {k: v for k, v in _L1_attn_all.items() if k in ('wq', 'bq', 'wk', 'bk', 'wv', 'bv', 'wo', 'bo', 'rel_bias')}
    del _L1_attn_all

    def _L1_cond2_setup():
        import jax, jax.numpy as jnp
        import numpy as np
        import math
        D = 128
        H = 128
        key = jax.random.key(seed)
        k1, k2, k3, k4 = jax.random.split(key, 4)
        x = jax.random.normal(k1, (64, 64, D), dtype=jnp.float32)
        h0 = jax.random.normal(k2, (64, H), dtype=jnp.float32)
        Wx = jax.random.normal(k3, (D, 4 * H), dtype=jnp.float32) / math.sqrt(D)
        Wh = jax.random.normal(k4, (H, 4 * H), dtype=jnp.float32) / math.sqrt(H)
        b = jnp.zeros((4 * H,), dtype=jnp.float32)
        return {'x': x, 'h0': h0, 'Wx': Wx, 'Wh': Wh, 'b': b}
    _L1_cond2_all = _L1_cond2_setup()
    _L1_cond2_in = {k: v for k, v in _L1_cond2_all.items() if k in ('Wx', 'Wh', 'b')}
    del _L1_cond2_all

    def _L1_ffn_setup():
        import jax, jax.numpy as jnp
        import numpy as np
        D_MODEL = 128
        HIDDEN = 256
        N_EXPERTS = 8
        TOP_K = 2
        key = jax.random.key(seed)
        ks = jax.random.split(key, 9)
        s = 0.02
        x = jax.random.normal(ks[0], (4, 256, D_MODEL), dtype=jnp.float32)
        sw1 = jax.random.normal(ks[1], (D_MODEL, HIDDEN), dtype=jnp.float32) * s
        sw2 = jax.random.normal(ks[2], (D_MODEL, HIDDEN), dtype=jnp.float32) * s
        sw3 = jax.random.normal(ks[3], (HIDDEN, D_MODEL), dtype=jnp.float32) * s
        ew1 = jax.random.normal(ks[4], (N_EXPERTS, D_MODEL, HIDDEN), dtype=jnp.float32) * s
        ew2 = jax.random.normal(ks[5], (N_EXPERTS, D_MODEL, HIDDEN), dtype=jnp.float32) * s
        ew3 = jax.random.normal(ks[6], (N_EXPERTS, HIDDEN, D_MODEL), dtype=jnp.float32) * s
        rw = jax.random.normal(ks[7], (D_MODEL, N_EXPERTS), dtype=jnp.float32) * s
        rb = jax.random.normal(ks[8], (N_EXPERTS,), dtype=jnp.float32) * s
        return {'x': x, 'sw1': sw1, 'sw2': sw2, 'sw3': sw3, 'ew1': ew1, 'ew2': ew2, 'ew3': ew3, 'rw': rw, 'rb': rb}
    _L1_ffn_all = _L1_ffn_setup()
    _L1_ffn_in = {k: v for k, v in _L1_ffn_all.items() if k in ('sw1', 'sw2', 'sw3', 'ew1', 'ew2', 'ew3', 'rw', 'rb')}
    del _L1_ffn_all
    return {'x': x, 'cond_1024': cond_1024, 'L0_cond_W_z': _L0_cond_in['W_z'], 'L0_cond_U_z': _L0_cond_in['U_z'], 'L0_cond_C_z': _L0_cond_in['C_z'], 'L0_cond_b_z': _L0_cond_in['b_z'], 'L0_cond_W_r': _L0_cond_in['W_r'], 'L0_cond_U_r': _L0_cond_in['U_r'], 'L0_cond_C_r': _L0_cond_in['C_r'], 'L0_cond_b_r': _L0_cond_in['b_r'], 'L0_cond_W': _L0_cond_in['W'], 'L0_cond_U': _L0_cond_in['U'], 'L0_cond_C': _L0_cond_in['C'], 'L0_cond_b': _L0_cond_in['b'], 'L0_attn_W_in': _L0_attn_in['W_in'], 'L0_attn_conv_w': _L0_attn_in['conv_w'], 'L0_attn_conv_b': _L0_attn_in['conv_b'], 'L0_attn_dt_bias': _L0_attn_in['dt_bias'], 'L0_attn_A_log': _L0_attn_in['A_log'], 'L0_attn_D': _L0_attn_in['D'], 'L0_attn_init_states': _L0_attn_in['init_states'], 'L0_attn_norm_w': _L0_attn_in['norm_w'], 'L0_attn_W_out': _L0_attn_in['W_out'], 'L0_attn_W_nl': _L0_attn_in['W_nl'], 'L0_attn_b_nl': _L0_attn_in['b_nl'], 'L0_cond2_WQ_w': _L0_cond2_in['WQ_w'], 'L0_cond2_WQ_b': _L0_cond2_in['WQ_b'], 'L0_cond2_WK_w': _L0_cond2_in['WK_w'], 'L0_cond2_WK_b': _L0_cond2_in['WK_b'], 'L0_cond2_WV_w': _L0_cond2_in['WV_w'], 'L0_cond2_WV_b': _L0_cond2_in['WV_b'], 'L0_cond2_WO_w': _L0_cond2_in['WO_w'], 'L0_cond2_WO_b': _L0_cond2_in['WO_b'], 'L0_ffn_router_kernel_DE': _L0_ffn_in['router_kernel_DE'], 'L0_ffn_kernel_gating_EDF': _L0_ffn_in['kernel_gating_EDF'], 'L0_ffn_kernel_up_EDF': _L0_ffn_in['kernel_up_EDF'], 'L0_ffn_kernel_down_EFD': _L0_ffn_in['kernel_down_EFD'], 'L1_cond_Wx': _L1_cond_in['Wx'], 'L1_cond_Wh': _L1_cond_in['Wh'], 'L1_cond_b': _L1_cond_in['b'], 'L1_attn_wq': _L1_attn_in['wq'], 'L1_attn_bq': _L1_attn_in['bq'], 'L1_attn_wk': _L1_attn_in['wk'], 'L1_attn_bk': _L1_attn_in['bk'], 'L1_attn_wv': _L1_attn_in['wv'], 'L1_attn_bv': _L1_attn_in['bv'], 'L1_attn_wo': _L1_attn_in['wo'], 'L1_attn_bo': _L1_attn_in['bo'], 'L1_attn_rel_bias': _L1_attn_in['rel_bias'], 'L1_cond2_Wx': _L1_cond2_in['Wx'], 'L1_cond2_Wh': _L1_cond2_in['Wh'], 'L1_cond2_b': _L1_cond2_in['b'], 'L1_ffn_sw1': _L1_ffn_in['sw1'], 'L1_ffn_sw2': _L1_ffn_in['sw2'], 'L1_ffn_sw3': _L1_ffn_in['sw3'], 'L1_ffn_ew1': _L1_ffn_in['ew1'], 'L1_ffn_ew2': _L1_ffn_in['ew2'], 'L1_ffn_ew3': _L1_ffn_in['ew3'], 'L1_ffn_rw': _L1_ffn_in['rw'], 'L1_ffn_rb': _L1_ffn_in['rb']}

def reference(x, cond_1024, L0_cond_W_z, L0_cond_U_z, L0_cond_C_z, L0_cond_b_z, L0_cond_W_r, L0_cond_U_r, L0_cond_C_r, L0_cond_b_r, L0_cond_W, L0_cond_U, L0_cond_C, L0_cond_b, L0_attn_W_in, L0_attn_conv_w, L0_attn_conv_b, L0_attn_dt_bias, L0_attn_A_log, L0_attn_D, L0_attn_init_states, L0_attn_norm_w, L0_attn_W_out, L0_attn_W_nl, L0_attn_b_nl, L0_cond2_WQ_w, L0_cond2_WQ_b, L0_cond2_WK_w, L0_cond2_WK_b, L0_cond2_WV_w, L0_cond2_WV_b, L0_cond2_WO_w, L0_cond2_WO_b, L0_ffn_router_kernel_DE, L0_ffn_kernel_gating_EDF, L0_ffn_kernel_up_EDF, L0_ffn_kernel_down_EFD, L1_cond_Wx, L1_cond_Wh, L1_cond_b, L1_attn_wq, L1_attn_bq, L1_attn_wk, L1_attn_bk, L1_attn_wv, L1_attn_bv, L1_attn_wo, L1_attn_bo, L1_attn_rel_bias, L1_cond2_Wx, L1_cond2_Wh, L1_cond2_b, L1_ffn_sw1, L1_ffn_sw2, L1_ffn_sw3, L1_ffn_ew1, L1_ffn_ew2, L1_ffn_ew3, L1_ffn_rw, L1_ffn_rb):
    import jax
    import jax.numpy as jnp

    def _L0_cond_ref(video, seq, W_z, U_z, C_z, b_z, W_r, U_r, C_r, b_r, W, U, C, b):
        import jax, jax.numpy as jnp
        import numpy as np
        B, T, D_IN, V_IN, E = (64, 128, 128, 128, 128)
        vz = video @ C_z + b_z
        vr = video @ C_r + b_r
        vh = video @ C + b
        xz = jnp.einsum('btd,de->bte', seq, W_z)
        xr = jnp.einsum('btd,de->bte', seq, W_r)
        xh = jnp.einsum('btd,de->bte', seq, W)

        def step(h, xs):
            xzt, xrt, xht = xs
            z = jax.nn.sigmoid(xzt + h @ U_z + vz)
            r = jax.nn.sigmoid(xrt + h @ U_r + vr)
            hh = jnp.tanh(xht + r * h @ U + vh)
            h_new = (1.0 - z) * h + z * hh
            return (h_new, h_new)
        h0 = jnp.zeros((seq.shape[0], U.shape[0]), seq.dtype)
        xs = (jnp.swapaxes(xz, 0, 1), jnp.swapaxes(xr, 0, 1), jnp.swapaxes(xh, 0, 1))
        _, out_t = jax.lax.scan(step, h0, xs)
        return jnp.swapaxes(out_t, 0, 1)

    def _L0_attn_ref(x, W_in, conv_w, conv_b, dt_bias, A_log, D, init_states, norm_w, W_out, W_nl, b_nl):
        import jax, jax.numpy as jnp
        import numpy as np
        import math
        N_STATE = 64
        H_MODEL = 128
        D_CONV = 16
        EXPAND = 2
        D_INNER = EXPAND * H_MODEL
        HEADDIM = H_MODEL // 4
        NHEADS = D_INNER // HEADDIM
        NGROUPS = 1
        CONV_DIM = D_INNER + 2 * NGROUPS * N_STATE
        D_IN_PROJ = 2 * D_INNER + 2 * NGROUPS * N_STATE + NHEADS
        BATCH, SEQLEN = (4, 256)

        def _mamba2(x, W_in, conv_w, conv_b, dt_bias, A_log, D, init_states, norm_w, W_out):
            b, l, _ = x.shape
            zxbcdt = x @ W_in
            z = zxbcdt[..., :D_INNER]
            xBC = zxbcdt[..., D_INNER:D_INNER + CONV_DIM]
            dt = jax.nn.softplus(zxbcdt[..., -NHEADS:] + dt_bias)
            kernel = conv_w.T[:, None, :]
            xBC = jax.lax.conv_general_dilated(xBC, kernel, window_strides=(1,), padding=[(D_CONV - 1, 0)], dimension_numbers=('NWC', 'WIO', 'NWC'), feature_group_count=CONV_DIM) + conv_b
            xBC = jax.nn.silu(xBC)
            xs = xBC[..., :D_INNER].reshape(b, l, NHEADS, HEADDIM)
            Bm = xBC[..., D_INNER:D_INNER + N_STATE]
            Cm = xBC[..., D_INNER + N_STATE:]
            A = -jnp.exp(A_log)
            dA = jnp.exp(dt * A)
            h0 = jnp.broadcast_to(init_states, (b, NHEADS, HEADDIM, N_STATE))

            def step(h, inp):
                dA_t, x_t, dt_t, B_t, C_t = inp
                dBx = jnp.einsum('bh,bhp,bn->bhpn', dt_t, x_t, B_t)
                h = h * dA_t[:, :, None, None] + dBx
                y_t = jnp.einsum('bhpn,bn->bhp', h, C_t)
                return (h, y_t)
            scan_in = (jnp.moveaxis(dA, 1, 0), jnp.moveaxis(xs, 1, 0), jnp.moveaxis(dt, 1, 0), jnp.moveaxis(Bm, 1, 0), jnp.moveaxis(Cm, 1, 0))
            _, ys = jax.lax.scan(step, h0, scan_in)
            y = jnp.moveaxis(ys, 0, 1) + D[None, None, :, None] * xs
            y = y.reshape(b, l, D_INNER)
            y = y * jax.nn.silu(z)
            y = y * jax.lax.rsqrt(jnp.mean(y * y, axis=-1, keepdims=True) + 1e-05) * norm_w
            return y @ W_out
        y = _mamba2(x, W_in, conv_w, conv_b, dt_bias, A_log, D, init_states, norm_w, W_out)
        t = y / jnp.sqrt(1.0 + y * y)
        return t @ W_nl + b_nl + x

    def _L0_cond2_ref(x, ax, WQ_w, WQ_b, WK_w, WK_b, WV_w, WV_b, WO_w, WO_b):
        import jax, jax.numpy as jnp
        import numpy as np
        NHID = 128
        NHEAD = 16
        HEAD_DIM = 64
        B, L = (8, 512)
        Bx, Lx, H = x.shape
        nh, d = (NHEAD, HEAD_DIM)
        q = (x @ WQ_w + WQ_b).reshape(Bx, Lx, nh, d)
        k = (x @ WK_w + WK_b).reshape(Bx, Lx, nh, d)
        ak = (ax @ WK_w + WK_b).reshape(Bx, 1, nh, d)
        av = (ax @ WV_w + WV_b).reshape(Bx, 1, nh, d)
        pad_k = jnp.pad(k, ((0, 0), (1, 1), (0, 0), (0, 0)))
        k_shift = jnp.stack([pad_k[:, t:Lx + t] for t in range(3)], axis=3)
        akb = jnp.broadcast_to(ak, (Bx, Lx, nh, d))[:, :, :, None, :]
        avb = jnp.broadcast_to(av, (Bx, Lx, nh, d))[:, :, :, None, :]
        K = jnp.concatenate([akb, k_shift], axis=3)
        V = jnp.concatenate([avb, k_shift], axis=3)
        scores = jnp.einsum('blhd,blhjd->blhj', q, K) / jnp.sqrt(jnp.float32(d))
        alphas = jax.nn.softmax(scores, axis=-1)
        att = jnp.einsum('blhj,blhjd->blhd', alphas, V).reshape(Bx, Lx, nh * d)
        return att @ WO_w + WO_b

    def _L0_ffn_ref(x, router_kernel_DE, kernel_gating_EDF, kernel_up_EDF, kernel_down_EFD):
        import jax, jax.numpy as jnp
        import numpy as np
        TOP_K = 2
        E = router_kernel_DE.shape[-1]
        x = x.astype(jnp.float32)
        logits_BSE = jnp.einsum('BSD,DE->BSE', x, router_kernel_DE)
        probs_BSE = jax.nn.softmax(logits_BSE.astype(jnp.float32), axis=-1)
        weights_BSK, indices_BSK = jax.lax.top_k(probs_BSE, TOP_K)
        norm_weights_BSK = jax.nn.softmax(weights_BSK, axis=-1)
        one_hot_BSKE = jax.nn.one_hot(indices_BSK, num_classes=E, dtype=x.dtype)
        full_weights_BSE = jnp.sum(one_hot_BSKE * norm_weights_BSK[..., None], axis=2)
        gating_BSEF = jnp.einsum('BSD,EDF->BSEF', x, kernel_gating_EDF)
        act_BSEF = jax.nn.silu(gating_BSEF)
        up_BSEF = jnp.einsum('BSD,EDF->BSEF', x, kernel_up_EDF)
        fuse_BSEF = act_BSEF * up_BSEF
        down_BSED = jnp.einsum('BSEF,EFD->BSED', fuse_BSEF, kernel_down_EFD)
        out_BSD = jnp.einsum('BSED,BSE->BSD', down_BSED, full_weights_BSE)
        return out_BSD.astype(jnp.float32)

    def _L1_cond_ref(x, h0, Wx, Wh, b):
        import jax, jax.numpy as jnp
        import numpy as np
        H = h0.shape[1]
        xW = jnp.einsum('ntd,dg->tng', x, Wx) + b

        def step(carry, xw_t):
            prev_h, prev_c = carry
            preact = xw_t + prev_h @ Wh
            i, f, o, g = jnp.split(preact, 4, axis=1)
            i = jax.nn.sigmoid(i)
            f = jax.nn.sigmoid(f)
            o = jax.nn.sigmoid(o)
            g = jnp.tanh(g)
            next_c = f * prev_c + i * g
            next_h = o * jnp.tanh(next_c)
            return ((next_h, next_c), next_h)
        c0 = jnp.zeros_like(h0)
        _, hs = jax.lax.scan(step, (h0, c0), xW)
        return jnp.transpose(hs, (1, 0, 2))

    def _L1_attn_ref(x, wq, bq, wk, bk, wv, bv, wo, bo, rel_bias):
        import jax, jax.numpy as jnp
        import numpy as np
        EMBED = 128
        HEADS = 16
        HEAD_DIM = EMBED // HEADS
        NUM_BUCKETS = 32
        MAX_DISTANCE = 128
        B, L = (4, 256)

        def relative_position_bucket(relative_position, num_buckets=NUM_BUCKETS, max_distance=MAX_DISTANCE):
            n = -relative_position
            max_exact = num_buckets // 2
            is_small = n < max_exact
            nf = jnp.maximum(n, 1).astype(jnp.float32)
            val_if_large = max_exact + (jnp.log(nf / max_exact) / np.log(max_distance / max_exact) * (num_buckets - max_exact)).astype(jnp.int32)
            val_if_large = jnp.minimum(val_if_large, num_buckets - 1)
            ret = jnp.where(is_small, n, val_if_large)
            return jnp.maximum(ret, 0)
        Bx, Lx, C = x.shape

        def proj(w, b):
            y = jnp.einsum('blc,dc->bld', x, w) + b
            return y.reshape(Bx, Lx, HEADS, HEAD_DIM).transpose(0, 2, 1, 3)
        q = proj(wq, bq)
        k = proj(wk, bk)
        v = proj(wv, bv)
        scores = jnp.einsum('bhqd,bhkd->bhqk', q, k) / np.sqrt(HEAD_DIM)
        ctx = jnp.arange(Lx, dtype=jnp.int32)
        relative = ctx[None, :] - ctx[:, None]
        bucket_ids = relative_position_bucket(relative)
        bias = rel_bias[bucket_ids]
        bias = jnp.transpose(bias, (2, 0, 1))
        attn = jax.nn.softmax(scores + bias[None], axis=-1)
        out = jnp.einsum('bhqk,bhkd->bhqd', attn, v)
        out = out.transpose(0, 2, 1, 3).reshape(Bx, Lx, C)
        return jnp.einsum('blc,dc->bld', out, wo) + bo

    def _L1_cond2_ref(x, h0, Wx, Wh, b):
        import jax, jax.numpy as jnp
        import numpy as np
        import math
        D = 128
        H = 128
        xz = jnp.einsum('ntd,dk->ntk', x, Wx) + b
        c0 = jnp.zeros_like(h0)

        def step(carry, xz_t):
            prev_h, prev_c = carry
            z = xz_t + prev_h @ Wh
            ai, af, ao, ag = jnp.split(z, 4, axis=1)
            i = jax.nn.sigmoid(ai)
            f = jax.nn.sigmoid(af)
            o = jax.nn.sigmoid(ao)
            g = jnp.tanh(ag)
            next_c = f * prev_c + i * g
            next_h = o * jnp.tanh(next_c)
            return ((next_h, next_c), next_h)
        _, hs = jax.lax.scan(step, (h0, c0), jnp.swapaxes(xz, 0, 1))
        return jnp.swapaxes(hs, 0, 1)

    def _L1_ffn_ref(x, sw1, sw2, sw3, ew1, ew2, ew3, rw, rb):
        import jax, jax.numpy as jnp
        import numpy as np
        D_MODEL = 128
        HIDDEN = 256
        N_EXPERTS = 8
        TOP_K = 2
        shared = jnp.einsum('bth,hd->btd', jax.nn.silu(jnp.einsum('btd,dh->bth', x, sw1)) * jnp.einsum('btd,dh->bth', x, sw2), sw3)
        probs = jax.nn.softmax(jnp.einsum('btd,de->bte', x, rw) + rb, axis=-1)
        w, idx = jax.lax.top_k(probs, TOP_K)
        w = w / jnp.sum(w, axis=-1, keepdims=True)
        gates = jnp.sum(w[..., None] * jax.nn.one_hot(idx, N_EXPERTS, dtype=x.dtype), axis=-2)
        h = jax.nn.silu(jnp.einsum('btd,edh->beth', x, ew1)) * jnp.einsum('btd,edh->beth', x, ew2)
        eout = jnp.einsum('beth,ehd->betd', h, ew3)
        routed = jnp.einsum('betd,bte->btd', eout, gates)
        return shared + routed
    x = x + _L0_attn_ref(_L0_cond_ref(cond_1024, x, L0_cond_W_z, L0_cond_U_z, L0_cond_C_z, L0_cond_b_z, L0_cond_W_r, L0_cond_U_r, L0_cond_C_r, L0_cond_b_r, L0_cond_W, L0_cond_U, L0_cond_C, L0_cond_b), L0_attn_W_in, L0_attn_conv_w, L0_attn_conv_b, L0_attn_dt_bias, L0_attn_A_log, L0_attn_D, L0_attn_init_states, L0_attn_norm_w, L0_attn_W_out, L0_attn_W_nl, L0_attn_b_nl)
    x = x + _L0_ffn_ref(_L0_cond2_ref(x, cond_1024, L0_cond2_WQ_w, L0_cond2_WQ_b, L0_cond2_WK_w, L0_cond2_WK_b, L0_cond2_WV_w, L0_cond2_WV_b, L0_cond2_WO_w, L0_cond2_WO_b), L0_ffn_router_kernel_DE, L0_ffn_kernel_gating_EDF, L0_ffn_kernel_up_EDF, L0_ffn_kernel_down_EFD)
    x = x + _L1_attn_ref(_L1_cond_ref(x, cond_1024, L1_cond_Wx, L1_cond_Wh, L1_cond_b), L1_attn_wq, L1_attn_bq, L1_attn_wk, L1_attn_bk, L1_attn_wv, L1_attn_bv, L1_attn_wo, L1_attn_bo, L1_attn_rel_bias)
    x = x + _L1_ffn_ref(_L1_cond2_ref(x, cond_1024, L1_cond2_Wx, L1_cond2_Wh, L1_cond2_b), L1_ffn_sw1, L1_ffn_sw2, L1_ffn_sw3, L1_ffn_ew1, L1_ffn_ew2, L1_ffn_ew3, L1_ffn_rw, L1_ffn_rb)
    return x

_drawn_inputs = setup_inputs


def setup_inputs(seed=0):
    import zlib

    import numpy as np

    out = dict(_drawn_inputs(seed))
    spreads = {'L0_cond_b_z': (0.0, 0.1),
     'L0_cond_b_r': (0.0, 0.1),
     'L0_cond_b': (0.0, 0.1),
     'L0_attn_conv_b': (0.0, 0.1),
     'L0_attn_D': (1.0, 0.2),
     'L0_attn_norm_w': (1.0, 0.2),
     'L0_attn_b_nl': (0.0, 0.1),
     'L0_cond2_WQ_b': (0.0, 0.1),
     'L0_cond2_WK_b': (0.0, 0.1),
     'L0_cond2_WV_b': (0.0, 0.1),
     'L0_cond2_WO_b': (0.0, 0.1),
     'L1_cond_b': (0.0, 0.1),
     'L1_attn_bq': (0.0, 0.1),
     'L1_attn_bk': (0.0, 0.1),
     'L1_attn_bv': (0.0, 0.1),
     'L1_attn_bo': (0.0, 0.1),
     'L1_cond2_b': (0.0, 0.1)}
    factors = {}
    for name, (base, spread) in spreads.items():
        noise = np.random.default_rng([zlib.crc32(name.encode()), seed]).standard_normal(out[name].shape)
        drawn = base * np.exp(spread * noise) if base else spread * noise
        out[name] = jnp.asarray(drawn.astype(out[name].dtype))
    for name, factor in factors.items():
        out[name] = (out[name] * factor).astype(out[name].dtype)
    return out
```

```python
import concourse.bass as bass
from concourse import mybir
from contextlib import ExitStack

F32 = mybir.dt.float32
BF16 = mybir.dt.bfloat16
ALU = mybir.AluOpType
ACT = mybir.ActivationFunctionType
AX = mybir.AxisListType


class Tok:

    def __init__(self, sem, step):
        self.sem, self.step, self.used, self.value = sem, step, False, None


class Counter:

    def __init__(self, prog, name):
        self.h = prog.ctx.enter_context(prog.nc.semaphore(name))
        self.count = 0


class Prog:

    ENG = ("tensor", "scalar", "vector", "gpsimd", "sync")

    def __init__(self, nc, ctx):
        self.nc, self.ctx = nc, ctx
        self.q = {e: [] for e in self.ENG}

    def sb(self, name, shape, dt=F32):
        return self.ctx.enter_context(self.nc.sbuf_tensor(name, shape, dt))

    def bank(self, name):
        return self.ctx.enter_context(self.nc.psum_tensor(name, [128, 512], F32))

    def counter(self, name):
        return Counter(self, name)

    def put(self, eng, counter, fn, waits, step=1):
        tok = Tok(counter, step)
        flat = []

        def take(w):
            if isinstance(w, (list, tuple)):
                for x in w:
                    take(x)
            elif w is not None:
                w.used = True
                flat.append(w)
        take(waits)
        if step == 16:
            tok.used = True
        self.q[eng].append((fn, flat, tok))
        return tok

    def emit(self):
        for e in self.ENG:
            for fn, waits, tok in self.q[e]:
                if tok.used:
                    tok.sem.count += tok.step
                    tok.value = tok.sem.count
        block = self.ctx.enter_context(self.nc.Block())
        for e in self.ENG:
            def body(eng, e=e):
                seen = {}
                for fn, waits, tok in self.q[e]:
                    need = {}
                    for w in waits:
                        if w.value > need.get(w.sem, 0):
                            need[w.sem] = w.value
                    for s, v in need.items():
                        if v > seen.get(s, 0):
                            eng.wait_ge(s.h, v)
                            seen[s] = v
                    ins = fn(eng)
                    if tok.used:
                        ins.then_inc(tok.sem.h, tok.step)
            blocks = {"tensor": block.tensor, "scalar": block.scalar, "vector": block.vector,
                            "gpsimd": block.gpsimd, "sync": block.sync}
            blocks[e](body)


class Stage:

    def __init__(self, p, name):
        self.p, self.name, self.c, self.latest = p, name, {}, {}

    def put(self, eng, fn, waits):
        if eng not in self.c:
            self.c[eng] = self.p.counter(f"s_{self.name}_{eng}")
        t = self.latest[eng] = self.p.put(eng, self.c[eng], fn, waits)
        return t

    def end(self):
        return list(self.latest.values())

    def mm(self, out, lhsT, rhs, start, stop, *waits):
        return self.put("tensor", lambda e: e.matmul(out, lhsT, rhs, start=start, stop=stop, skip_group_check=True), waits)

    def tr(self, out, in_, ident, *waits):
        return self.put("tensor", lambda e: e.transpose(out, in_, ident), waits)

    def act(self, out, in_, func, *waits, bias=0.0, scale=1.0):
        return self.put("scalar", lambda e: e.activation(out, in_, func, bias=bias, scale=scale), waits)

    def actsum(self, out, in_, func, total, *waits):
        return self.put("scalar", lambda e: e.activation(out, in_, func, accum_out=total), waits)

    def tt(self, out, a, b, op, *waits, eng="vector"):
        return self.put(eng, lambda e: e.tensor_tensor(out, a, b, op), waits)

    def ts(self, out, a, s1, s2, op0, op1, *waits, eng="vector"):
        if op1 is None:
            return self.put(eng, lambda e: e.tensor_scalar(out, a, s1, None, op0), waits)
        return self.put(eng, lambda e: e.tensor_scalar(out, a, s1, s2, op0, op1), waits)

    def stt(self, out, a, s, b, op0, op1, *waits):
        return self.put("vector", lambda e: e.scalar_tensor_tensor(out=out, in0=a, scalar=s, in1=b, op0=op0, op1=op1), waits)

    def cp(self, out, a, *waits, eng="vector"):
        return self.put(eng, lambda e: e.tensor_copy(out, a), waits)

    def red(self, out, a, op, *waits):
        return self.put("vector", lambda e: e.tensor_reduce(out, a, axis=AX.X, op=op), waits)

    def recip(self, out, a, *waits):
        return self.put("vector", lambda e: e.reciprocal(out, a), waits)

    def memset(self, out, v, *waits, eng="gpsimd"):
        return self.put(eng, lambda e: e.memset(out, v), waits)

    def sel(self, out, in_, op, fill, base, pattern, cm, *waits):
        return self.put("gpsimd", lambda e: e.affine_select(out=out, in_=in_, compare_op=op, fill=fill, base=base,
                                                            pattern=pattern, channel_multiplier=cm), waits)


def run(*lanes):
    lanes = [list(x) if isinstance(x, tuple) else [x, 1] for x in lanes]
    while lanes:
        for l in list(lanes):
            for _ in range(l[1]):
                try:
                    next(l[0])
                except StopIteration:
                    lanes.remove(l)
                    break

NB, T, D = 32, 128, 128
N = NB * T


def bc(ap, axis, n):
    a = ap.unsqueeze(axis)
    shape = list(a.shape)
    shape[axis] = n
    return a.broadcast_to(shape)


def program(nc, I, out, only=None, dbg=None):
    ctx = ExitStack()
    with ctx:
        p = Prog(nc, ctx)
        K = Kernel(p, I, out)
        K.consts()
        if only is None:
            K.all()
        else:
            K.one(only, dbg)
        p.emit()


class Kernel:
    def __init__(self, p, I, out):
        self.p, self.I, self.out = p, I, out
        sb = p.sb
        self.X = sb("X", [128, NB, T])
        self.G = sb("G", [128, NB, T])
        self.bank = [p.bank(f"B{i}") for i in range(8)]
        self.tX = None
        self.tG = None
        self.ndma = 0
        self.open = []
        self.moefree = None
        self.cattfree = None
        self.final = False
        self.cout = p.counter('s_out')
        self.tGfree = None
        self.work = sb("work", [128, 78 * 256])
        self.moew = sb("moew", [128, 27 * 256])
        self.catt = sb("catt", [128, 36 * 256])
        self.wfree = []
        self.wtop = 0

    def area(self, base, shape, dt=F32):
        n = 1
        for s in shape[1:]:
            n *= s
        words = n if dt == F32 else (n + 1) // 2
        t, at = base
        assert at + words <= t.shape[1], (at, words, t.shape)
        base[1] = at + words
        v = t[0:shape[0], at:at + words]
        if dt != F32:
            v = v.bitcast(dt)
        if len(shape) == 3:
            v = v.rearrange("p (a b) -> p a b", b=shape[2])
        elif len(shape) == 4:
            v = v.rearrange("p (a b c) -> p a b c", b=shape[2], c=shape[3])
        return v

    def load(self, dst, src, *waits, eng="sync", counter=None):
        if counter is None:
            self.ndma += 1
            counter = self.p.counter(f"s_ld{self.ndma}")
        return self.p.put(eng, counter, lambda e: e.dma_start(dst, src), waits, 16)

    def loads(self, pairs, *waits, eng="sync"):
        self.ndma += 1
        c = self.p.counter(f"s_ld{self.ndma}")
        for d, s in pairs:
            t = self.load(d, s, *waits, eng=eng, counter=c)
        return t

    def consts(self):
        p, I = self.p, self.I
        S = self.S0 = Stage(p, "const")
        sb = p.sb
        self.ident = sb("ident", [128, 128])
        self.identb = sb("identb", [128, 128], BF16)
        t = S.memset(self.ident[:], 0.0)
        self.tI = S.sel(self.ident[:], self.ident[:], ALU.not_equal, 1.0, 0, [[-1, 128]], 1, t)
        self.tIb = S.cp(self.identb[:], self.ident[:], self.tI, eng="gpsimd")
        self.tri = sb("tri", [128, 128])
        self.triq = sb("triq", [128, 128])
        self.low = sb("low", [128, 128])
        self.ones = sb("ones", [128, 128])
        t1 = S.memset(self.ones[:], 1.0)
        t = S.sel(self.tri[:], self.ones[:], ALU.is_ge, 0.0, 0, [[1, 128]], -1, t1)
        t2 = S.sel(self.low[:], self.ones[:], ALU.is_gt, 0.0, 0, [[-1, 128]], 1, t1)
        t3 = S.ts(self.triq[:], self.tri[:], 0.25, None, ALU.mult, None, t, eng="gpsimd")
        self.tTri = t3
        self.cond = sb("condt", [32, 128])
        self.condT = sb("condT", [128, 32])
        self.condT2 = sb("condT2", [128, 32])
        tl = self.load(self.cond[:], I["cond_1024"])
        B = self.bank[0]
        t = S.tr(B[:, 0:32], self.cond[:], self.ident[0:32, 0:32], tl, self.tI)
        self.tcond = S.act(self.condT[:], B[:, 0:32], ACT.Copy, t)
        self.tcond2 = S.act(self.condT2[:], B[:, 0:32], ACT.Copy, t, scale=2.0)
        self.tcond = self.tcond2
        self.gw = sb("gw", [128, 9, 128])
        self.gb = sb("gb", [128, 3])
        ws = ["L0_cond_W_z", "L0_cond_W_r", "L0_cond_W", "L0_cond_U_z", "L0_cond_U_r", "L0_cond_U",
              "L0_cond_C_z", "L0_cond_C_r", "L0_cond_C"]
        self.lgw = self.loads([(self.gw[:, i, :], I[n]) for i, n in enumerate(ws)] +
                              [(self.gb[:, i:i + 1], I[n].rearrange("(p o) -> p o", o=1))
                               for i, n in enumerate(["L0_cond_b_z", "L0_cond_b_r", "L0_cond_b"])])

    def load_x(self):
        S, I = self.S0, self.I
        w = [self.work, 0]
        xt = self.area(w, [128, NB, D])
        tok = []
        for u in range(4):
            tok.append(self.load(xt[:, u * 8:u * 8 + 8, :], I["x"][u * 8:u * 8 + 8].rearrange("b t d -> t b d"),
                                 eng="sync" if u % 2 else "scalar"))
        cur = {}
        for u in range(8):
            B = self.bank[2 + u % 4]
            for j in range(4):
                t = S.tr(B[:, j * 128:(j + 1) * 128], xt[:, 4 * u + j, :], self.ident[:], tok[u // 2], self.tI, cur.get(u % 4))
            dst = self.X[:, 4 * u:4 * u + 4, :].rearrange("p b t -> p (b t)")
            if u % 2:
                cur[u % 4] = S.cp(dst, B[:], t)
            else:
                cur[u % 4] = S.act(dst, B[:], ACT.Copy, t)
        self.tX = list(cur.values())
        self.wfree = self.tX

    def gru(self, banks=(6, 7)):
        p, I = self.p, self.I
        S = Stage(p, "gru")
        gw, gb = self.gw, self.gb
        V = p.sb("gV", [128, 3, 32])
        tw = []
        for i in (0, 1, 3, 4, 5, 6, 7):
            tw.append(S.ts(gw[:, i, :], gw[:, i, :], 0.5, None, ALU.mult, None, self.lgw))
        tw = [tw[-1], S.ts(gb[:, 0:2], gb[:, 0:2], 0.5, None, ALU.mult, None, self.lgw)]
        B = self.bank[banks[0]]
        for g in range(3):
            t = S.mm(B[:, g * 32:g * 32 + 32], gw[:, 6 + g, :], self.condT[:], True, True, tw, self.tcond)
        for g in range(3):
            tV = S.act(V[:, g, :], B[:, g * 32:g * 32 + 32], ACT.Identity, t, bias=gb[:, g:g + 1])
        h = [p.sb(f"gh{i}", [128, 32]) for i in range(2)]
        th = p.sb("gth", [128, 2, 32])
        hh = p.sb("ghh", [128, 32])
        rh = p.sb("grh", [128, 32])
        zz = p.sb("gz", [128, 32])
        aa = p.sb("ga", [128, 32])
        zh = p.sb("gzh", [128, 32])
        th_ = S.memset(h[1][:], 0.0)
        free = {banks[0]: tV, banks[1]: None}
        ready = {}

        def pre(q):
            b = banks[q % 2]
            B = self.bank[b]
            S.mm(B[:, 0:384].rearrange("p (s c) -> p s c", s=4), self.ident[:],
                 bc(V[:, :, :].rearrange("p g b -> p (g b)"), 1, 4), True, False, tV, self.tI, free[b])
            for g in range(3):
                o = B[:, 0:384].rearrange("p (s g b) -> p s g b", s=4, g=3)[:, :, g, :]
                S.mm(o, gw[:, g, :], self.X[:, :, 4 * q:4 * q + 4].rearrange("p b s -> p s b"), False, False,
                     tw, self.tX)
        pre(0)
        thm = th_
        tz_ = None
        trh = tcopy = tzh = None
        gcopy = [None, None]
        for t in range(T):
            if t % 4 == 1 and t + 3 < T:
                pre(t // 4 + 1)
            b = banks[(t // 4) % 2]
            B = self.bank[b]
            o = (t % 4) * 96
            hp, hn = h[(t + 1) % 2], h[t % 2]
            S.mm(B[:, o + 32:o + 64], gw[:, 4, :], hp[:], False, True, thm)
            m = S.mm(B[:, o:o + 32], gw[:, 3, :], hp[:], False, True)
            a1 = S.act(th[:, :, :].rearrange("p g b -> p (g b)"), B[:, o:o + 64], ACT.Tanh, m, tz_)
            trh = S.stt(rh[:], th[:, 1, :], 1.0, hp[:], ALU.add, ALU.mult, a1, thm)
            m = S.mm(B[:, o + 64:o + 96], gw[:, 5, :], rh[:], False, True, trh)
            a2 = S.act(hh[:], B[:, o + 64:o + 96], ACT.Tanh, m, tzh)
            tz_ = S.ts(zz[:], th[:, 0, :], 0.5, 0.5, ALU.mult, ALU.add)
            t1 = S.tt(aa[:], zz[:], hp[:], ALU.mult, tz_)
            t1 = S.tt(aa[:], hp[:], aa[:], ALU.subtract, t1)
            tzh = S.tt(zh[:], zz[:], hh[:], ALU.mult, a2)
            thm = S.tt(hn[:], zh[:], aa[:], ALU.add, tzh, t1, gcopy[t % 2])
            free[b] = a2
            gcopy[t % 2] = S.cp(self.G[:, :, t], hn[:], thm, self.tGfree, eng="gpsimd")
            self.gru_tok = gcopy[t % 2]
            yield
        self.tG = gcopy

    def lstm(self, li, banks=(6, 7)):
        p, I = self.p, self.I
        S = Stage(p, f"lstm{li}")
        pre_ = "L1_cond" if li == 0 else "L1_cond2"
        if not hasattr(self, "lt"):
            self.lt = dict(lw=p.sb("lw", [128, 8, 128]), b3=p.sb("lb3", [128, 128], BF16), b4=p.sb("lb4", [4, 128]),
                           r4=p.sb("lr4", [4, 128]), q4=p.sb("lq4", [4, 128], BF16),
                           ind=p.sb("lind", [128, 4, 4, 32], BF16), H=[p.sb(f"lH{i}", [128, 32]) for i in range(2)],
                           Dc=p.sb("lD", [128, 32]), th=p.sb("lth", [128, 4, 32]), tc=p.sb("ltc", [128, 32]),
                           pp=p.sb("lp", [128, 32]), qq=p.sb("lq", [128, 32]))
            self.lfree = None
        lt, lfree = self.lt, self.lfree
        lw, b3, b4, r4, q4, ind, H = lt["lw"], lt["b3"], lt["b4"], lt["r4"], lt["q4"], lt["ind"], lt["H"]
        Dc, th, tc, pp, qq = lt["Dc"], lt["th"], lt["tc"], lt["pp"], lt["qq"]
        ld = self.loads([(lw[:, 0:4, :], I[pre_ + "_Wx"].rearrange("k (g e) -> k g e", g=4)),
                         (lw[:, 4:8, :], I[pre_ + "_Wh"].rearrange("k (g e) -> k g e", g=4)),
                         (b4[:, :], I[pre_ + "_b"].rearrange("(g e) -> g e", g=4))], lfree)
        tw = [S.ts(lw[:, 0:3, :], lw[:, 0:3, :], 0.5, None, ALU.mult, None, ld, eng="gpsimd"),
              S.ts(lw[:, 4:7, :], lw[:, 4:7, :], 0.25, None, ALU.mult, None, ld, eng="gpsimd"),
              S.ts(lw[:, 7, :], lw[:, 7, :], 0.5, None, ALU.mult, None, ld, eng="gpsimd")]
        t = S.ts(b4[:], b4[:], self.half3(S), None, ALU.mult, None, ld, self.thalf)
        z = S.memset(b3[:], 0.0, lfree)
        t1 = S.cp(b3[0:4, :], b4[:], t, z)
        t2 = S.tt(r4[:], b4[:], b3[0:4, :], ALU.subtract, t1)
        t3 = S.cp(b3[32:36, :], r4[:], t2)
        t4 = S.cp(q4[:], r4[:], t2)
        t5 = S.tt(r4[:], r4[:], q4[:], ALU.subtract, t4, t3)
        t6 = S.cp(b3[64:68, :], r4[:], t5)
        z = S.memset(ind[:], 0.0, lfree)
        for base in (0, 32, 64):
            v = ind[base:base + 4]
            z = S.sel(v, v, ALU.not_equal, 1.0, 0, [[0, 4], [-1, 4], [0, 32]], 1, z)
        tb = [t3, t6, z]
        h0 = self.condT2
        tD = S.memset(Dc[:], 0.0, z)
        free = {banks[0]: None, banks[1]: None}

        def pre(q):
            b = banks[q % 2]
            B = self.bank[b]
            S.mm(B[:, :], b3[0:68, :], ind[0:68].rearrange("p s g b -> p (s g b)"), True, False, tb, free[b])
            for g in range(4):
                o = B[:, :].rearrange("p (s g b) -> p s g b", s=4, g=4)[:, :, g, :]
                S.mm(o, lw[:, g, :], self.X[:, :, 4 * q:4 * q + 4].rearrange("p b s -> p s b"), False, False,
                     tw, self.tX)
        yield
        pre(0)
        thm = self.tcond2
        tth = None
        ttc = None
        gcopy = [None, None]
        for t in range(T):
            if t % 4 == 1 and t + 3 < T:
                pre(t // 4 + 1)
            b = banks[(t // 4) % 2]
            B = self.bank[b]
            o = (t % 4) * 128
            hp = h0 if t == 0 else H[(t + 1) % 2]
            hn = H[t % 2]
            for g in range(4):
                m = S.mm(B[:, o + 32 * g:o + 32 * g + 32], lw[:, 4 + g, :], hp[:], False, True, thm)
            a1 = S.act(th[:, :, :].rearrange("p g b -> p (g b)"), B[:, o:o + 128], ACT.Tanh, m, thm)
            t1 = S.stt(pp[:], th[:, 0, :], 1.0, th[:, 3, :], ALU.add, ALU.mult, a1)
            t2 = S.stt(qq[:], th[:, 1, :], 1.0, Dc[:], ALU.add, ALU.mult, tD, a1)
            tD = S.stt(Dc[:], qq[:], 0.5, pp[:], ALU.mult, ALU.add, t1, t2, ttc)
            ttc = S.act(tc[:], Dc[:], ACT.Tanh, tD, thm, scale=0.5)
            thm = S.stt(hn[:], th[:, 2, :], 1.0, tc[:], ALU.add, ALU.mult, ttc, gcopy[t % 2])
            free[b] = a1
            gcopy[t % 2] = S.cp(self.G[:, :, t], hn[:], thm, self.tGfree, eng="gpsimd")
            yield
        self.tG = gcopy
        self.lfree = S.end()

    def half3(self, S):
        if not hasattr(self, "h3"):
            self.h3 = self.p.sb("h3", [4, 1])
            t = self.S0.memset(self.h3[:], 0.5)
            self.thalf = self.S0.sel(self.h3[:], self.h3[:], ALU.not_equal, 1.0, -3, [[0, 1]], 1, t)
        return self.h3[:]

    def mamba_prep(self):
        p, I = self.p, self.I
        sb = p.sb
        S = Stage(p, "mprep")
        self.win = sb("win", [128, 648])
        self.wout = sb("wout", [128, 2, 128])
        self.wnl = sb("wnl", [128, 128])
        self.bnl = sb("bnl", [128, 1])
        self.nw = sb("nw", [128, 2])
        self.cw = sb("cw", [128, 3, 16])
        self.cb = sb("cb", [128, 3])
        self.dtb = sb("dtb", [128, 8])
        self.alog = sb("alog", [128, 8])
        self.dcol = sb("dcol", [128, 2])
        self.dg = sb("dg", [128, 2, 128])
        self.h0 = sb("h0", [128, 2, 64])
        self.h0T = sb("h0T", [64, 256])
        pairs = [(self.win[:], I["L0_attn_W_in"]),
                 (self.wout[:], I["L0_attn_W_out"].rearrange("(c p) n -> p c n", p=128)),
                 (self.wnl[:], I["L0_attn_W_nl"]),
                 (self.bnl[:], I["L0_attn_b_nl"].rearrange("(p o) -> p o", o=1)),
                 (self.cw[:], I["L0_attn_conv_w"].rearrange("(c p) k -> p c k", p=128)),
                 (self.dtb[:], bc(I["L0_attn_dt_bias"], 0, 128)),
                 (self.alog[:], bc(I["L0_attn_A_log"], 0, 128)),
                 (self.h0[:], I["L0_attn_init_states"].rearrange("(c h) q n -> (h q) c n", c=2))]
        for c in range(2):
            pairs.append((self.nw[:, c:c + 1], I["L0_attn_norm_w"][c * 128:c * 128 + 128].rearrange("(p o) -> p o", o=1)))
            for j in range(4):
                pairs.append((self.dcol[32 * j:32 * j + 32, c:c + 1],
                              bc(I["L0_attn_D"][4 * c + j:4 * c + j + 1], 0, 32)))
        for c in range(3):
            pairs.append((self.cb[:, c:c + 1], I["L0_attn_conv_b"][c * 128:c * 128 + 128].rearrange("(p o) -> p o", o=1)))
        ld = self.loads(pairs, eng="scalar")
        for c in range(2):
            t = S.ts(self.wout[:, c, :], self.wout[:, c, :], self.nw[:, c:c + 1], None, ALU.mult, None, ld)
        t = S.ts(self.dcol[:], self.dcol[:], 0.5, None, ALU.mult, None, ld)
        for c in range(2):
            t = S.ts(self.dg[:, c, :], self.ident[:], self.dcol[:, c:c + 1], None, ALU.mult, None, t, self.tI)
        B = self.bank[1]
        for c in range(2):
            tm = S.tr(B[0:64, c * 128:c * 128 + 128], self.h0[:, c, :], self.ident[:], ld, self.tI)
        t2 = S.act(self.h0T[:], B[0:64, 0:256], ACT.Copy, tm, scale=0.5)
        t3 = S.act(self.alog[:], self.alog[:], ACT.Exp, ld)
        t4 = S.ts(self.alog[:], self.alog[:], -1.0, None, ALU.mult, None, t3)
        self.tmw = [t, t2, t4, ld]
        self.tb1 = t2

    def mamba_dt(self, bs=range(NB)):
        p = self.p
        S = Stage(p, "mdt")
        n0, n = bs[0], len(bs)
        if not hasattr(self, "adt"):
            self.adt = p.sb("adt", [128, NB, 8])
            self.dth = p.sb("dth", [128, NB, 8])
            self.ec = p.sb("ec", [128, NB, 8])
            self.q1 = p.sb("mq1", [128, NB, 8])
            self.q2 = p.sb("mq2", [128, NB, 8])
            self.q3 = p.sb("mq3", [128, NB, 8])
        B = self.bank[0]
        s = slice(n0, n0 + n)
        P = B[:, 0:8 * n].rearrange("p (b h) -> p b h", h=8)
        for i, b in enumerate(bs):
            tm = S.mm(P[:, i, :], self.G[:, b, :], self.win[:, 640:648], True, True, self.tG, self.tmw)
        x, e, z, q = self.dth[:, s, :], self.q1[:, s, :], self.q2[:, s, :], self.q3[:, s, :]
        t = S.tt(x, P, bc(self.dtb[:], 1, n), ALU.add, tm)
        t = S.stt(e, x, -1.0, x, ALU.mult, ALU.min, t)
        t = S.act(e, e, ACT.Exp, t)
        t = S.ts(z, e, 2.0, None, ALU.add, None, t)
        t = S.recip(z, z, t)
        t = S.tt(z, z, e, ALU.mult, t)
        t = S.tt(e, z, z, ALU.mult, t)
        t = S.ts(q, e, 1 / 19, 1 / 17, ALU.mult, ALU.add, t)
        for k in (15, 13, 11, 9, 7, 5, 3, 1):
            t = S.tt(q, q, e, ALU.mult, t)
            t = S.ts(q, q, 1.0 / k, None, ALU.add, None, t)
        t = S.tt(q, q, z, ALU.mult, t)
        t = S.ts(x, x, 0.0, 0.5, ALU.max, ALU.mult, t)
        t = S.tt(x, x, q, ALU.add, t)
        a = self.adt[:, s, :]
        t = S.tt(a, x, bc(self.alog[:], 1, n), ALU.mult, t)
        t = S.ts(a, a, 2.0, None, ALU.mult, None, t)
        P2 = B[:, 256:256 + 8 * n].rearrange("p (b h) -> p b h", h=8)
        tm = S.mm(P2, self.tri[:], a, True, True, t, self.tTri)
        t2 = S.act(self.ec[:, s, :], P2, ACT.Exp, tm)
        self.tdt = [t, t2]

    def mamba(self, bs=range(NB), workers=2):
        self.mamba_dt(bs)
        w = [self.work, 0]
        units = [list(bs)[i:i + 4] for i in range(0, len(bs), 4)]
        gens = [self.mamba_worker(k, units[k::workers], w) for k in range(workers)]
        self.done = []
        return gens

    def mamba_worker(self, wk, units, w):
        p = self.p
        S = Stage(p, f"mamba{wk}")
        self.open.append(S)
        ar = lambda *s, dt=F32: self.area(w, list(s), dt)
        B0, B1, B2 = self.bank[3 * wk:3 * wk + 3]
        XP = ar(128, 3, 4, 144)
        cv = ar(128, 3, 512)
        th = ar(128, 3, 512)
        C0 = ar(128, 512)
        RT = ar(128, 8, 128)
        xdt = ar(128, 256)
        cbm = ar(128, 128)
        zt = ar(128, 256)
        y4 = ar(128, 4, 256)
        sq = ar(128, 256)
        ss = ar(128, 4)
        yT = ar(128, 2, 512)
        tm1 = ar(128, 512)
        zpad = S.memset(XP[:, :, :, 0:16], 0.0, self.wfree)
        fb = [[self.tdt, self.wfree], [self.tb1, self.wfree], self.wfree]
        tconv = t_y = tE = txd = tcbm = tCx = None
        tXP = tth = tC0 = tyT = ttm = tz = trs = t_yT = tss = None
        for un in units:
            ub = slice(un[0], un[0] + 4)
            Gu = self.G[:, ub, :].rearrange("p b t -> p (b t)")
            tc = []
            for c, Bk in enumerate((B0, B1, B2)):
                t = S.mm(Bk[:], self.win[:, 256 + c * 128:384 + c * 128], Gu, True, True, fb[c], self.tG, self.tmw)
                t = S.act(XP[:, c, :, 16:144], Bk[:].rearrange("p (b t) -> p b t", b=4), ACT.Copy, t, tconv, zpad)
                fb[c] = t
                tc.append(t)
            yield
            for c in range(3):
                acc = cv[:, c, :].rearrange("p (b t) -> p b t", b=4)
                t = S.ts(acc, XP[:, c, :, 1:129], self.cw[:, c, 0:1], self.cb[:, c:c + 1], ALU.mult, ALU.add,
                         tc[c], tCx, tth, self.tmw)
                for k in range(1, 16):
                    t = S.stt(acc, XP[:, c, :, 1 + k:129 + k], self.cw[:, c, k:k + 1], acc, ALU.mult, ALU.add, t)
                    if k % 5 == 0:
                        yield
                ta = S.act(th[:, c, :], cv[:, c, :], ACT.Tanh, t, tth, tC0, scale=0.5)
                if c < 2:
                    tth = S.stt(cv[:, c, :], th[:, c, :], 1.0, cv[:, c, :], ALU.add, ALU.mult, ta)
                else:
                    tth = S.stt(C0[0:64, :], th[64:128, c, :], 1.0, cv[64:128, c, :], ALU.add, ALU.mult, ta, tE)
                    tth = S.stt(cv[0:64, c, :], th[0:64, c, :], 1.0, cv[0:64, c, :], ALU.add, ALU.mult, ta)
                yield
            tconv = tth
            for j, b in enumerate(un):
                ts_ = slice(j * 128, j * 128 + 128)
                a = self.adt[:, b, :]
                tr_ = S.tt(RT[:], bc(self.tri[:], 1, 8), bc(a, 2, 128), ALU.mult, self.tdt, txd, tcbm, eng="gpsimd")
                S.mm(B0[:, 256:384], cv[0:64, 2, ts_], C0[0:64, ts_], True, True, tth, fb[0])
                for c in range(2):
                    t = S.tr(B0[:, c * 128:c * 128 + 128], cv[:, c, ts_], self.ident[:], tth, self.tI)
                tcbm = S.tt(cbm[:], B0[:, 256:384], self.triq[:], ALU.mult, t, tE, self.tTri)
                txd0 = S.tt(xdt[:].rearrange("p (h q) -> p h q", h=8), B0[:, 0:256].rearrange("p (h q) -> p h q", h=8),
                            bc(self.dth[:, b, :], 2, 32), ALU.mult, t, tCx)
                yield
                t1 = S.mm(B1[:], self.low[:], RT[:, 0:4, :].rearrange("p h t -> p (h t)"), True, True, tr_, fb[1])
                t2 = S.mm(B2[:], self.low[:], RT[:, 4:8, :].rearrange("p h t -> p (h t)"), True, True, fb[2])
                yield
                e1 = S.act(RT[:, 0:4, :].rearrange("p h t -> p (h t)"), B1[:], ACT.Exp, t1)
                e2 = S.act(RT[:, 4:8, :].rearrange("p h t -> p (h t)"), B2[:], ACT.Exp, t2)
                tE = S.tt(RT[:], RT[:], bc(cbm[:], 1, 8), ALU.mult, e1, e2, tcbm, eng="gpsimd")
                yield
                tzm = S.mm(B1[:, 0:256], self.G[:, b, :], self.win[:, 0:256], True, True, e1)
                tza = S.act(zt[:], B1[:, 0:256], ACT.Tanh, tzm, t_y, scale=0.5)
                tz = S.stt(zt[:], zt[:], 1.0, B1[:, 0:256], ALU.add, ALU.mult, tza)
                for c in range(2):
                    S.mm(B0[:, c * 128:c * 128 + 128], cv[:, c, ts_], self.dg[:, c, :], c == 0, False, txd0, tcbm)
                S.mm(B0[:, 256:512], C0[0:64, ts_], self.h0T[:], False, False)
                for h in range(8):
                    t = S.mm(B0[:, h * 32:h * 32 + 32], RT[:, h, :], xdt[:, h * 32:h * 32 + 32], False, True, tE, txd0)
                tCx = txd = t
                yield
                y = y4[:, j, :]
                y3 = y.rearrange("p (h q) -> p h q", h=8)
                t = S.tt(y3, B0[:, 256:512].rearrange("p (h q) -> p h q", h=8), bc(self.ec[:, b, :], 2, 32), ALU.mult,
                         t, self.tdt, t_yT)
                t = S.tt(y, y, B0[:, 0:256], ALU.add, t)
                fb[0] = t
                fb[1] = tz
                fb[2] = e2
                t_y = S.tt(y, y, zt[:], ALU.mult, t, tz)
                tss = S.actsum(sq[:], y, ACT.Square, ss[:, j:j + 1], t_y, trs)
                yield
            t = S.ts(ss[:], ss[:], 1 / 256, 4e-5, ALU.mult, ALU.add, tss)
            t = S.recip(ss[:], ss[:], t)
            t = S.act(ss[:], ss[:], ACT.Sqrt, t)
            for j in range(4):
                trs = S.ts(y4[:, j, :], y4[:, j, :], ss[:, j:j + 1], None, ALU.mult, None, t, t_y)
            yield
            for h in range(2):
                for j in (2 * h, 2 * h + 1):
                    for c in range(2):
                        t = S.tr(B2[:, (j % 2) * 256 + c * 128:(j % 2) * 256 + c * 128 + 128], y4[:, j, c * 128:c * 128 + 128],
                                 self.ident[:], trs, fb[2])
                t_yT = t
                fb[2] = S.act(yT[:, :, h * 256:h * 256 + 256].rearrange("p c (j t) -> p j c t", j=2),
                              B2[:].rearrange("p (j c t) -> p j c t", j=2, c=2), ACT.Copy, t, tyT)
            t = fb[2]
            tC0 = tCx
            for c in range(2):
                tw_ = S.mm(B0[:], self.wout[:, c, :], yT[:, c, :], c == 0, c == 1, t, fb[0], self.tmw)
            tyT = tw_
            t1 = S.act(tm1[:], B0[:], ACT.Square, tw_, ttm)
            t1 = S.ts(tm1[:], tm1[:], 1.0, None, ALU.add, None, t1)
            t1 = S.recip(tm1[:], tm1[:], t1)
            t1 = S.act(tm1[:], tm1[:], ACT.Sqrt, t1)
            yield
            t1 = S.tt(tm1[:], tm1[:], B0[:], ALU.mult, t1)
            fb[0] = t1
            t2 = S.mm(B1[:], self.wnl[:], tm1[:], True, True, t1, fb[1])
            ttm = t2
            Xu = self.X[:, ub, :].rearrange("p b t -> p (b t)")
            t3 = S.stt(Xu, B1[:], self.bnl[:], Xu, ALU.add, ALU.add, t2, self.tX)
            fb[1] = t3
            t4 = S.tt(Xu, Xu, Gu, ALU.add, t3, eng="gpsimd")
            self.done.append(t4)
            yield

    def cond2_prep(self, banks=(0, 1)):
        p, I = self.p, self.I
        S = Stage(p, "cprep")
        ca = [self.catt, 0]
        ar = lambda *s, dt=F32: self.area(ca, list(s), dt)
        self.WQ, self.WK, self.WO = ar(128, 8, 128), ar(128, 8, 128), ar(128, 8, 128)
        self.ckc = ar(128, 2, 8)
        self.bo = ar(128, 1)
        self.Gak = ar(128, NB, 16)
        self.cak = ar(128, NB, 16)
        self.avo = ar(16, NB, 128)
        w = [self.work, 78 * 256 - 20 * 256]
        WV = self.area(w, [128, 8, 128])
        akb = self.area(w, [128, 8, 2, 32])
        avb = self.area(w, [128, 8, 2, 32])
        wqT = self.area(w, [128, 8, 128])
        bqb = self.area(w, [128, 8, 128])
        avt = self.area([self.work, w[1] - 1024], [64, 8, 128])
        bv = p.sb("cbv", [128, 8])
        self.blk = p.sb("blk", [128, 2])
        self.selc = p.sb("selc", [48, 16, 64], BF16)
        self.wprep = None
        W = lambda n: I[n].rearrange("k (c m) -> k c m", c=8)
        col = lambda n: I[n].rearrange("(c p) -> p c", p=128)
        ld = self.loads([(self.WQ, W("L0_cond2_WQ_w")), (self.WK, W("L0_cond2_WK_w")), (WV, W("L0_cond2_WV_w")),
                         (self.WO, I["L0_cond2_WO_w"].rearrange("(c p) n -> p c n", p=128)),
                         (self.bo, I["L0_cond2_WO_b"].rearrange("(p o) -> p o", o=1))] +
                        [(d[:, c:c + 1], I[n][c * 128:c * 128 + 128].rearrange("(p o) -> p o", o=1))
                         for c in range(8) for d, n in ((self.ckc[:, 0, :], "L0_cond2_WQ_b"),
                                                        (self.ckc[:, 1, :], "L0_cond2_WK_b"), (bv, "L0_cond2_WV_b"))],
                        self.wfree, eng="scalar")
        z = S.memset(akb, 0.0, self.wfree)
        z2 = S.memset(avb, 0.0, self.wfree)
        t = S.sel(self.blk[:], self.ones[:, 0:2], ALU.is_ge, 0.0, 0, [[-64, 2]], 1, self.tI, self.tIb, self.tTri)
        self.tblk = S.sel(self.blk[:], self.blk[:], ALU.is_ge, 0.0, 63, [[64, 2]], -1, t)
        t = S.memset(self.selc[:], 0.0)
        for part in range(3):
            t = S.sel(self.selc[:], self.selc[:], ALU.not_equal, 1.0, -16 * part, [[-1, 16], [0, 64]], 1, t)
        self.tsel = t
        B0, B1 = self.bank[banks[0]], self.bank[banks[1]]
        for c in range(8):
            S.mm(B0[:, c * 32:c * 32 + 32], self.WK[:, c, :], self.condT[:], True, True, ld, self.tcond, self.wfree)
            t = S.mm(B0[:, 256 + c * 32:288 + c * 32], WV[:, c, :], self.condT[:], True, True)
        for c in range(8):
            for i in range(2):
                r = slice(64 * i, 64 * i + 64)
                t1 = S.act(akb[r, c, i, :], B0[r, c * 32:c * 32 + 32], ACT.Identity, t, z, bias=self.ckc[r, 1, c:c + 1])
                t1 = S.act(avb[r, c, i, :], B0[r, 256 + c * 32:288 + c * 32], ACT.Identity, t, z2, bias=bv[r, c:c + 1])
        f0 = t1
        f1 = None
        for g in range(2):
            for i in range(4):
                t = S.tr(B1[:, i * 128:i * 128 + 128], self.WQ[:, 4 * g + i, :], self.ident[:], ld, self.tI, f1, self.wfree)
            f1 = S.act(wqT[:, 4 * g:4 * g + 4, :].rearrange("p c m -> p (c m)"), B1[:], ACT.Copy, t)
        tb = S.cp(bqb, bc(self.ckc[:, 0, :], 2, 128), ld)
        for c in range(8):
            t = S.mm(B0[:, c * 64:c * 64 + 64], wqT[:, c, :], akb[:, c].rearrange("p i b -> p (i b)"), True, True, f0, f1)
        t2 = S.act(self.Gak.rearrange("p b (c i) -> p c i b", c=8), B0[:].rearrange("p (c i b) -> p c i b", c=8, i=2),
                   ACT.Copy, t)
        for c in range(8):
            t = S.mm(B1[:, c * 64:c * 64 + 64], bqb[:, c, :], akb[:, c].rearrange("p i b -> p (i b)"), True, True, f1, tb)
        t3 = S.act(self.cak.rearrange("p b (c i) -> p c i b", c=8), B1[:].rearrange("p (c i b) -> p c i b", c=8, i=2),
                   ACT.Copy, t)
        f = [t2, t3]
        for g in range(2):
            Bk = (B0, B1)[g]
            for i in range(4):
                c = 4 * g + i
                t = S.mm(Bk[0:64, i * 128:i * 128 + 128], avb[:, c].rearrange("p i b -> p (i b)"), self.WO[:, c, :],
                         True, True, f[g], f0)
            f[g] = S.act(avt[:, 4 * g:4 * g + 4, :].rearrange("p c m -> p (c m)"), Bk[0:64, :], ACT.Copy, t)
        t = self.loads([(self.avo[2 * c + i:2 * c + i + 1, :, :], avt[32 * i:32 * i + 32, c, :])
                        for c in range(8) for i in range(2)], f)
        self.tcw = [ld, t2, t3, t]
        self.wfree = [t, t2, t3]
        self.tb0, self.tb1 = f

    def cond2(self, bs=range(NB), workers=2):
        w = [self.work, 0]
        units = [list(bs)[i:i + 4] for i in range(0, len(bs), 4)]
        self.done = []
        return [self.cond2_worker(k, units[k::workers], w) for k in range(workers)]

    def cond2_worker(self, wk, units, w):
        S = Stage(self.p, f"cond2{wk}")
        self.open.append(S)
        ar = lambda *s, dt=F32: self.area(w, list(s), dt)
        Bq, Bk, Bs = self.bank[3 * wk:3 * wk + 3]
        KP = ar(128, 8, 4, 130)
        pr = [ar(128, 512) for i in range(3)]
        sc = ar(128, 64, 4)
        m = ar(128, 64)
        sm = ar(128, 64)
        R = ar(128, 64, 4)
        A = ar(128, 4 * 3, 48, dt=BF16)
        AT = ar(48, 3, 512, dt=BF16)
        a0 = ar(16, 512)
        att = [ar(128, 512) for i in range(2)]
        tpad = S.memset(KP[:, :, :, 0:1], 0.0, self.wfree)
        tpad = S.memset(KP[:, :, :, 129:130], 0.0, self.wfree, tpad)
        fq = fk = fs = [self.tb0, self.tb1, self.tcw, self.wfree]
        fKP = [self.wfree] * 8
        fpr = [self.wfree] * 3
        tex = tA = tAT = ta0 = None
        fatt = [None, None]
        for un in units:
            ub = slice(un[0], un[0] + 4)
            Xu = self.X[:, ub, :].rearrange("p b t -> p (b t)")
            S3 = Bs[:, 0:256].rearrange("p (b h j) -> p b h j", b=4, h=16)
            for i, b in enumerate(un):
                t = S.mm(S3[:, i, :, 0], self.X[:, b, :], self.Gak[:, b, :], i == 0, False, fs, self.tcw, self.tX)
            for c in range(8):
                tq = S.mm(Bq[:], self.WQ[:, c, :], Xu, True, True, fq, self.tcw, self.tX)
                tk = S.mm(Bk[:], self.WK[:, c, :], Xu, True, True, fk)
                fk = tk = S.act(KP[:, c, :, 1:129], Bk[:].rearrange("p (b t) -> p b t", b=4), ACT.Identity, tk, fKP[c],
                                bias=self.ckc[:, 1, c:c + 1])
                yield
                for j in range(3):
                    fq = S.stt(pr[j].rearrange("p (b t) -> p b t", b=4), Bq[:].rearrange("p (b t) -> p b t", b=4),
                               self.ckc[:, 0, c:c + 1], KP[:, c, :, j:j + 128], ALU.add, ALU.mult, tq, tk, fpr[j], tpad)
                    for i in range(4):
                        ts = S.mm(S3[:, i, 2 * c:2 * c + 2, j + 1], pr[j][:, i * 128:i * 128 + 128], self.blk[:],
                                  False, False, fq, self.tblk)
                    fpr[j] = ts
                yield
            S4 = sc.rearrange("p (b h) j -> p b h j", b=4)
            t = S.act(sc, S3.rearrange("p b h j -> p (b h) j"), ACT.Copy, ts, tA)
            t = S.tt(S4[:, :, :, 0], S4[:, :, :, 0], self.cak[:, ub, :], ALU.add, t)
            fs = t
            t = S.red(m, sc, ALU.max, t)
            t = S.tt(sc, sc, bc(m, 2, 4), ALU.subtract, t)
            t = S.act(sc, sc, ACT.Exp, t, scale=0.125)
            t = S.red(sm, sc, ALU.add, t)
            t = S.recip(sm, sm, t)
            t = S.tt(sc, sc, bc(sm, 2, 4), ALU.mult, t)
            Av = A.rearrange("p (b j) (q h) -> p b j q h", b=4, q=3)
            Sv = sc.rearrange("p (b h) j -> p b j h", b=4)
            Rb = R.rearrange("p x y -> p (x y)").rearrange("p (b j h) -> p b j h", b=4, j=4)
            for j in range(1, 4):
                ta = S.cp(Av[:, :, j - 1, 0, :], Sv[:, :, j, :], t, tAT, eng="gpsimd")
                tb = S.tt(Rb[:, :, j, :], Sv[:, :, j, :], Av[:, :, j - 1, 0, :], ALU.subtract, ta, eng="gpsimd")
                ta = S.cp(Av[:, :, j - 1, 1, :], Rb[:, :, j, :], tb, eng="gpsimd")
                tb = S.tt(Rb[:, :, j, :], Rb[:, :, j, :], Av[:, :, j - 1, 1, :], ALU.subtract, ta, eng="gpsimd")
                tA = S.cp(Av[:, :, j - 1, 2, :], Rb[:, :, j, :], tb, eng="gpsimd")
            yield
            for i in range(4):
                t1 = S.tr(Bs[0:16, i * 128:i * 128 + 128], Sv[:, i, 0, :], self.ident[:], t, self.tI)
            ta0 = S.act(a0, Bs[0:16, :], ACT.Copy, t1, ta0)
            fs = ta0
            for j in range(3):
                Bt = (Bq, Bq, Bk)[j][:].bitcast(BF16)
                o = (0, 512, 0)[j]
                for i in range(4):
                    t1 = S.tr(Bt[0:48, o + i * 128:o + i * 128 + 128], Av[:, i, j, :, :].rearrange("p q h -> p (q h)"),
                              self.identb[:], tA, self.tIb, fq if j < 2 else fk)
                if j == 1:
                    fq = S.act(AT[:, 0:2, :].rearrange("p j t -> p (j t)"), Bt[0:48, :], ACT.Copy, t1, tAT)
                if j == 2:
                    fk = S.act(AT[:, 2, :], Bt[0:48, 0:512], ACT.Copy, t1, tAT)
            tAT_r = [fq, fk]
            yield
            for i, b in enumerate(un):
                to = S.mm(Bs[:, i * 128:i * 128 + 128], self.avo[:, b, :], a0[:, i * 128:i * 128 + 128], i == 0, False,
                          ta0, fs)
            tex = to
            n = 0
            for c in range(8):
                prods = []
                for j in range(3):
                    Bb = (Bq, Bk)[n % 2]
                    fb = (fq, fk)[n % 2]
                    t1 = S.mm(Bb[:], self.selc[:, 2 * c:2 * c + 2, :].rearrange("p h d -> p (h d)"), AT[:, j, :], True, True,
                              tAT_r, self.tsel, fb)
                    tAT = t1
                    t2 = S.tt(pr[j].rearrange("p (b t) -> p b t", b=4), Bb[:].rearrange("p (b t) -> p b t", b=4),
                              KP[:, c, :, j:j + 128], ALU.mult, t1, fpr[j])
                    prods.append(t2)
                    if n % 2:
                        fk = t2
                    else:
                        fq = t2
                    n += 1
                yield
                fKP[c] = t2
                av = att[c % 2]
                t3 = S.tt(av, pr[0], pr[1], ALU.add, prods[1], fatt[c % 2], eng="gpsimd")
                fpr[0] = fpr[1] = t3
                t3 = S.tt(av, av, pr[2], ALU.add, t3, prods[2], eng="gpsimd")
                fpr[2] = t3
                yield
                to = S.mm(Bs[:], self.WO[:, c, :], av, False, c == 7, t3)
                fatt[c % 2] = to
            t = S.act(self.G[:, ub, :].rearrange("p b t -> p (b t)"), Bs[:], ACT.Identity, to, self.tGfree, bias=self.bo)
            fs = t
            self.done.append(t)
            yield

    def moe_load(self, li):
        I, w = self.I, [self.moew, 0]
        E = 8 + li
        self.wg, self.wu, self.wd = (self.area(w, [128, E, 256]), self.area(w, [128, E, 256]),
                                     self.area(w, [128, E * 2, 128]))
        ng, nu, nd = (("L0_ffn_kernel_gating_EDF", "L0_ffn_kernel_up_EDF", "L0_ffn_kernel_down_EFD"),
                      ("L1_ffn_ew1", "L1_ffn_ew2", "L1_ffn_ew3"))[li]
        self.rw = self.p.sb(f"rw{li}", [128, 8])
        self.rb = self.p.sb(f"rb{li}", [128, 8])
        pairs = [(self.rw[:], I[("L0_ffn_router_kernel_DE", "L1_ffn_rw")[li]]),
                 (self.wg[:, 0:8, :], I[ng].rearrange("e d f -> d e f")),
                 (self.wu[:, 0:8, :], I[nu].rearrange("e d f -> d e f")),
                 (self.wd[:, 0:16, :], I[nd].rearrange("e (c f) d -> f (e c) d", c=2))]
        if li:
            pairs += [(self.wg[:, 8, :], I["L1_ffn_sw1"]), (self.wu[:, 8, :], I["L1_ffn_sw2"]),
                      (self.wd[:, 16:18, :], I["L1_ffn_sw3"].rearrange("(c f) d -> f c d", c=2)),
                      (self.rb[:], bc(I["L1_ffn_rb"], 0, 128))]
        self.tmoe = self.loads(pairs, self.moefree)

    def moe_route(self, li, bs, bank, w):
        p = self.p
        S = Stage(p, f"route{li}")
        self.open.append(S)
        n = len(bs)
        ar = lambda *s, dt=F32: self.area(w, list(s), dt)
        if not hasattr(self, "rev"):
            self.rev = p.sb("rev", [128, 8])
            for e in range(8):
                self.trev = self.S0.memset(self.rev[:, e:e + 1], float(8 - e), eng="vector")
            self.selw = p.sb("selw", [24, 8, 128], BF16)
            t = self.S0.memset(self.selw[:], 0.0, self.tI)
            for part in range(3):
                t = self.S0.sel(self.selw[:], self.selw[:], ALU.not_equal, 1.0, -8 * part, [[-1, 8], [0, 128]], 1, t)
            self.tselw = t
        pr, f1, f2, mk = (ar(128, n, 8) for _ in range(4))
        m1, m2, q1, q2 = (ar(128, n) for _ in range(4))
        Wp = ar(128, n, 24, dt=BF16)
        WT = ar(24, n * 128, dt=BF16)
        B = self.bank[bank]
        P = B[:, 0:8 * n].rearrange("p (b e) -> p b e", e=8)
        for i, b in enumerate(bs):
            t = S.mm(P[:, i, :], self.G[:, b, :], self.rw[:], True, True, self.tG, self.tmoe, self.wfree)
        if li:
            t = S.stt(pr, P, 0.5, bc(self.rb[:], 1, n), ALU.mult, ALU.add, t, self.wfree)
        else:
            t = S.cp(pr, P, t, self.wfree)
        t = S.red(m1, pr, ALU.max, t)
        t = S.tt(pr, pr, bc(m1, 2, 8), ALU.subtract, t)
        t = S.act(pr, pr, ACT.Exp, t)
        t = S.red(m1, pr, ALU.add, t)
        t = S.recip(m1, m1, t)
        t = S.tt(pr, pr, bc(m1, 2, 8), ALU.mult, t)
        for k, (m, f, q) in enumerate(((m1, f1, q1), (m2, f2, q2))):
            t = S.red(m, pr, ALU.max, t)
            t = S.tt(mk, pr, bc(m, 2, 8), ALU.is_equal, t)
            t = S.tt(mk, mk, bc(self.rev[:], 1, n), ALU.mult, t, self.trev)
            t = S.red(q, mk, ALU.max, t)
            t = S.tt(f, mk, bc(q, 2, 8), ALU.is_equal, t)
            if k == 0:
                t = S.stt(pr, f, -4.0, pr, ALU.mult, ALU.add, t)
        if li:
            t = S.tt(q1, m1, m2, ALU.add, t)
            t = S.recip(q1, q1, t)
            t1 = S.tt(m1, m1, q1, ALU.mult, t)
            t2 = S.tt(m2, m2, q1, ALU.mult, t)
        else:
            t = S.tt(q1, m2, m1, ALU.subtract, t)
            t = S.act(q1, q1, ACT.Exp, t)
            t = S.ts(q2, q1, 1.0, None, ALU.add, None, t)
            t1 = S.recip(m1, q2, t)
            t2 = S.tt(m2, q1, m1, ALU.mult, t1)
        t = S.tt(f1, f1, bc(m1, 2, 8), ALU.mult, t1, t2)
        t = S.tt(f2, f2, bc(m2, 2, 8), ALU.mult, t)
        t = S.tt(f1, f1, f2, ALU.add, t)
        t = S.cp(Wp[:, :, 0:8], f1, t)
        t = S.tt(f1, f1, Wp[:, :, 0:8], ALU.subtract, t)
        t = S.cp(Wp[:, :, 8:16], f1, t)
        t = S.tt(f1, f1, Wp[:, :, 8:16], ALU.subtract, t)
        t = S.cp(Wp[:, :, 16:24], f1, t)
        Bb = B[:].bitcast(BF16)
        f = None
        for i0 in range(0, n, 8):
            for i in range(8):
                tm = S.tr(Bb[0:24, i * 128:i * 128 + 128], Wp[:, i0 + i, :], self.identb[:], t, self.tIb, f)
            f = S.act(WT[:, i0 * 128:i0 * 128 + 1024], Bb[0:24, :], ACT.Copy, tm)
        self.tWT = [f]
        return WT

    def moe(self, li, bs=range(NB), banks=(0, 1, 2, 3, 4, 5)):
        if li and not self.final:
            self.final = True
        self.moe_load(li)
        self.done = []
        return [self.moe_lane(li, bs, banks)]

    def moe_lane(self, li, bs, banks):
        w = [self.work, 0]
        ar = lambda *s, dt=F32: self.area(w, list(s), dt)
        WT = self.moe_route(li, bs, banks[5], w)
        yield
        S = Stage(self.p, f"moe{li}")
        self.open.append(S)
        xw = [ar(128, 512) for _ in range(2)]
        sg = [ar(128, 512) for _ in range(2)]
        hh = [ar(128, 512) for _ in range(2)]
        ot = ar(128, 512)
        if li:
            og = ar(128, 512)
        BG, BU = banks[0:2], banks[2:4]
        BW, BO = self.bank[banks[4]], self.bank[banks[5]]
        fG = [self.wfree, self.wfree]
        fU = [self.wfree, self.wfree]
        fW = fO = [self.wfree, self.tWT]
        fxw = [None, None]
        fh = [None, None]
        fsg = [None, None]
        tot = None
        steps = []
        E = 8 + li
        units = [list(bs)[i:i + 4] for i in range(0, len(bs), 4)]
        prev = None
        k = 0

        def down(pv):
            nonlocal fO, tot
            e, fc, kk, th, u, un = pv
            first, last = (e == 0 and fc == 0), (e == E - 1 and fc == 1)
            t = S.mm(BO[:], self.wd[:, 2 * e + fc, :], hh[kk % 2], first, last, th, fO if first else None)
            fh[kk % 2] = t
            if last:
                Xu = self.X[:, un[0]:un[0] + 4, :].rearrange("p b t -> p (b t)")
                if not li:
                    fO = S.tt(Xu, Xu, BO[:], ALU.add, t, self.tX)
                    self.done.append(fO)
                else:
                    fO = t2 = S.tt(ot, Xu, BO[:], ALU.add, t, self.tX, tot)
                    for i in range(4):
                        t3 = S.tr(BO[:, i * 128:i * 128 + 128], ot[:, i * 128:i * 128 + 128], self.ident[:], t2, self.tI)
                    tot = t3
                    fO = S.act(og, BO[:], ACT.Copy, t3, self.done[-1] if self.done else None)
                    self.done.append(self.load(self.out[un[0]:un[0] + 4].rearrange("b t d -> t b d"),
                                               og.rearrange("p (b d) -> p b d", b=4), fO, counter=self.cout))
        for u, un in enumerate(units):
            ub = slice(un[0], un[0] + 4)
            Gu = self.G[:, ub, :].rearrange("p b t -> p (b t)")
            for e in range(E):
                if e < 8:
                    t = S.mm(BW[:], self.selw[:, e, :], WT[:, u * 512:u * 512 + 512], True, True, self.tWT, self.tselw, fW)
                    txw = fW = S.tt(xw[e % 2], Gu, BW[:], ALU.mult, t, fxw[e % 2])
                    src = xw[e % 2]
                else:
                    src, txw = Gu, None
                for fc in range(2):
                    i = k % 2
                    G_, U_ = self.bank[BG[i]], self.bank[BU[i]]
                    c = slice(fc * 128, fc * 128 + 128)
                    t1 = S.mm(G_[:], self.wg[:, e, c], Gu, True, True, fG[i], self.tmoe)
                    fG[i] = t1 = S.act(sg[i], G_[:], ACT.Silu, t1, fsg[i], scale=0.5 if li else 1.0)
                    t2 = S.mm(U_[:], self.wu[:, e, c], src, True, True, fU[i], txw)
                    if e < 8:
                        fxw[e % 2] = t2
                    if li:
                        t3 = S.stt(hh[i], U_[:], 0.5, sg[i], ALU.mult, ALU.mult, t1, t2, fh[i])
                    else:
                        t3 = S.tt(hh[i], sg[i], U_[:], ALU.mult, t1, t2, fh[i])
                    fU[i] = fsg[i] = t3
                    if prev:
                        down(prev)
                    prev = (e, fc, k, t3, u, un)
                    k += 1
                    yield
        down(prev)
        yield

    def attn_prep(self, bank=0, waits=None):
        p, I = self.p, self.I
        S = Stage(p, "aprep")
        ca = [self.catt, 0]
        ar = lambda *s, dt=F32: self.area(ca, list(s), dt)
        self.awT = [ar(128, 128) for _ in range(4)]
        self.ab = ar(128, 4)
        self.bvb = ar(128, 128)
        self.bS = ar(128, 16, 128, dt=BF16)
        self.bT = [ar(128, 16, 128, dt=BF16) for _ in range(3)]
        raw = ar(128, 4, 128)
        oh = ar(32, 512)
        rel = ar(32, 16)
        bf = ar(128, 16, 32)
        col = lambda n: I[n].rearrange("(p o) -> p o", o=1)
        ld = self.loads([(raw[:, i, :], I["L1_attn_w" + c]) for i, c in enumerate("qkvo")] +
                        [(self.ab[:, 0:1], col("L1_attn_bq")), (self.ab[:, 1:2], col("L1_attn_bk")),
                         (self.ab[:, 3:4], col("L1_attn_bo")), (self.bvb, bc(I["L1_attn_bv"], 0, 128)),
                         (oh, I["onehot"]), (rel, I["L1_attn_rel_bias"])], self.cattfree, eng="scalar")
        B = self.bank[bank]
        for i in range(4):
            t = S.tr(B[:, i * 128:i * 128 + 128], raw[:, i, :], self.ident[:], ld, self.tI, waits, self.tcond)
        for i in range(4):
            f = S.act(self.awT[i], B[:, i * 128:i * 128 + 128], ACT.Copy, t)
        t0 = S.ts(self.ab[:, 0:1], self.ab[:, 0:1], 8 ** -0.5, None, ALU.mult, None, ld)
        tw = [f, t0, ld]
        tb = None
        yield
        for g in range(4):
            for q in range(32):
                o = 256 + 127 - (32 * g + q)
                t = S.mm(B[:, q * 16:q * 16 + 16], oh[:, o:o + 128], rel, True, True, ld, f)
            o3 = bf.rearrange("p h q -> p q h")
            t = S.act(o3, B[:].rearrange("p (q h) -> p q h", h=16), ACT.Copy, t, tb)
            f = t
            v = [x[:, :, 32 * g:32 * g + 32] for x in self.bT]
            t = S.cp(v[0], bf, t, eng="gpsimd")
            t = S.tt(bf, bf, v[0], ALU.subtract, t, eng="gpsimd")
            t = S.cp(v[1], bf, t, eng="gpsimd")
            t = S.tt(bf, bf, v[1], ALU.subtract, t, eng="gpsimd")
            tb = S.cp(v[2], bf, t, eng="gpsimd")
            yield
        for g in range(4):
            for k in range(32):
                o = 127 - (32 * g + k)
                t = S.mm(B[:, k * 16:k * 16 + 16], oh[:, o:o + 128], rel, True, True, f)
            f = S.act(self.bS[:, :, 32 * g:32 * g + 32].rearrange("p h k -> p k h"),
                      B[:].rearrange("p (k h) -> p k h", h=16), ACT.Copy, t)
            yield
        self.taw = tw + [tb, f]
        self.afree = f

    def attn(self, bs=range(NB), workers=2):
        w = [self.work, 0]
        self.scr = [[self.p.nc.dram_tensor(f"scr{k}{i}", [128, 3, 256], BF16, kind="Internal").ap() for i in range(2)]
                    for k in range(workers)]
        units = [list(bs)[i:i + 2] for i in range(0, len(bs), 2)]
        self.done = []
        return [self.attn_worker(k, units[k::workers], w) for k in range(workers)]

    def attn_worker(self, wk, units, w):
        S = Stage(self.p, f"attn{wk}")
        self.open.append(S)
        ar = lambda *s, dt=F32: self.area(w, list(s), dt)
        banks = self.bank[3 * wk:3 * wk + 3]
        q32 = [ar(128, 256) for _ in range(2)]
        pq, pk = ar(128, 3, 256, dt=BF16), ar(128, 3, 256, dt=BF16)
        parts = [[x[:, i, :] for i in range(3)] for x in (pq, pk)]
        cw = self.p.counter(f's_attnw{wk}')
        Q = ar(51, 16, 256, dt=BF16)
        Kt = ar(51, 16, 256, dt=BF16)
        V = ar(128, 2, 16, 9)
        nm = ar(128, 2, 16)
        nr = ar(128, 2, 16)
        np_ = ar(128, 2, 48, dt=BF16)
        nT = ar(48, 256, dt=BF16)
        P = [ar(128, 4, 128) for _ in range(2)]
        rc = ar(128, 16)
        o = ar(128, 128)
        oT = ar(128, 256)
        cdma = self.p.counter(f"s_attnq{wk}")
        cdma2 = self.p.counter(f"s_attnm{wk}")
        tone = S.memset(Kt[32:51], 1.0, self.wfree, eng="vector")
        tone2 = S.memset(V[:, :, :, 8:9], 1.0, self.wfree)
        f = [[self.afree, self.wfree], self.wfree, self.wfree]
        tQ = tV = tP = tm_ = to = toT = tnm = tpv = td = tdb = None
        fP = [None, None]
        PAIRS = [(0, 0), (0, 1), (0, 2), (1, 0), (1, 1), (2, 0)]
        for un in units:
            ub = slice(un[0], un[0] + 2)
            Gu = self.G[:, ub, :].rearrange("p b t -> p (b t)")
            B0, B1, B2 = banks
            t1 = S.mm(B0[:, 0:256], self.awT[0], Gu, True, True, f[0], self.tG, self.taw)
            t1 = S.mm(B0[:, 256:512], self.awT[1], Gu, True, True)
            t2 = None
            for i, b in enumerate(un):
                t2 = S.mm(B1[:, i * 128:i * 128 + 128], self.G[:, b, :], self.awT[2], True, True, f[1])
            for i in range(2):
                ta = S.act(q32[i], B0[:, 256 * i:256 * i + 256], ACT.Identity, t1, tQ, bias=self.ab[:, i:i + 1],
                           scale=0.5 * (8 ** -0.5 if i == 0 else 1.0))
                pa = parts[i]
                t = S.cp(pa[0], q32[i], ta, td, eng="gpsimd")
                t = S.tt(q32[i], q32[i], pa[0], ALU.subtract, t, eng="gpsimd")
                t = S.cp(pa[1], q32[i], t, eng="gpsimd")
                t = S.tt(q32[i], q32[i], pa[1], ALU.subtract, t, eng="gpsimd")
                tQ = S.cp(pa[2], q32[i], t, eng="gpsimd")
            f[0] = ta
            for i in range(2):
                tV = S.stt(V[:, i, :, 0:8], B1[:, i * 128:i * 128 + 128].rearrange("p (h d) -> p h d", h=16), 0.5,
                           self.bvb.rearrange("p (h d) -> p h d", h=16), ALU.mult, ALU.add, t2, tpv, self.taw)
            f[1] = tV
            yield
            sc = self.scr[wk]
            td = self.load(sc[0], pq[:], tQ, tdb, counter=cw)
            td = self.load(sc[1], pk[:], tQ, tdb, counter=cw, eng="sync")
            tdb = []
            for dst, s_, row, lo, hi in ((Kt, 1, 0, 0, 0), (Kt, 1, 1, 0, 0), (Kt, 1, 2, 0, 0), (Kt, 1, 3, 1, 1),
                                         (Kt, 1, 4, 1, 1), (Kt, 1, 5, 2, 2), (Q, 0, 0, 0, 2), (Q, 0, 3, 0, 1), (Q, 0, 5, 0, 0)):
                for q in range(lo, hi + 1):
                    r = row + q - lo
                    src = sc[s_].rearrange("(h d) q t -> q d h t", d=8)[q]
                    tdb = self.load(dst[8 * r:8 * r + 8], src, td, tone, tpv, counter=cdma)
            tk = tdb
            yield
            n = 0
            for i, b in enumerate(un):
                for g in range(4):
                    Bk = banks[n % 2]
                    S.mm(Bk[:], self.identb[:], self.bS[:, 4 * g:4 * g + 4, :].rearrange("p h k -> p (h k)"), True, False,
                         f[n % 2], self.taw, self.tIb)
                    for h in range(4):
                        t = S.mm(Bk[:, h * 128:h * 128 + 128], Q[0:48, 4 * g + h, i * 128:i * 128 + 128],
                                 Kt[0:48, 4 * g + h, i * 128:i * 128 + 128], False, True, tk)
                    f[n % 2] = tmx = S.red(nm[:, i, 4 * g:4 * g + 4], Bk[:].rearrange("p (h k) -> p h k", h=4), ALU.max, t, tnm)
                    n += 1
                    yield
            t = S.ts(nm, nm, -1.0, None, ALU.mult, None, tmx)
            t = S.cp(np_[:, :, 0:16], nm, t, tnm)
            t = S.tt(nr, nm, np_[:, :, 0:16], ALU.subtract, t)
            t = S.cp(np_[:, :, 16:32], nr, t)
            t = S.tt(nr, nr, np_[:, :, 16:32], ALU.subtract, t)
            t = S.cp(np_[:, :, 32:48], nr, t)
            Bb = B2[:].bitcast(BF16)
            for i in range(2):
                t1 = S.tr(Bb[0:48, i * 128:i * 128 + 128], np_[:, i, :], self.identb[:], t, f[2], self.tIb)
            tnm = t1
            f[2] = t = S.act(nT, Bb[0:48, 0:256], ACT.Copy, t1, tm_)
            for q in range(3):
                tm_ = self.load(Q[48 + q:49 + q, :, :], nT[16 * q:16 * q + 16, :], t, tpv, counter=cdma2)
            yield
            n = 0
            for i, b in enumerate(un):
                for g in range(4):
                    Bk = banks[n % 2]
                    for k in range(3):
                        S.mm(Bk[:], self.identb[:], self.bT[k][:, 4 * g:4 * g + 4, :].rearrange("p h q -> p (h q)"),
                             k == 0, False, f[n % 2])
                    for h in range(4):
                        t = S.mm(Bk[:, h * 128:h * 128 + 128], Kt[:, 4 * g + h, i * 128:i * 128 + 128],
                                 Q[:, 4 * g + h, i * 128:i * 128 + 128], False, True, tk, tm_)
                    f[n % 2] = te = S.act(P[n % 2].rearrange("p h q -> p (h q)"), Bk[:], ACT.Exp, t, fP[n % 2])
                    yield
                    for h in range(4):
                        hh = 4 * g + h
                        t = S.mm(B2[:, hh * 9:hh * 9 + 9], P[n % 2][:, h, :], V[:, i, hh, :], True, True, te, tV, tone2, f[2])
                    fP[n % 2] = t
                    n += 1
                tpv = t
                O = B2[:, 0:144].rearrange("p (h d) -> p h d", h=16)
                t = S.recip(rc, O[:, :, 8], tpv, to)
                t = S.tt(o.rearrange("p (h d) -> p h d", h=16), O[:, :, 0:8], bc(rc, 2, 8), ALU.mult, t, to)
                to = t1 = S.tr(B2[:, 256:384], o, self.ident[:], t)
                f[2] = S.act(oT[:, i * 128:i * 128 + 128], B2[:, 256:384], ACT.Copy, t1, toT)
                yield
            toT = t = S.mm(B2[:, 0:256], self.awT[3], oT, True, True, f[2])
            Xu = self.X[:, ub, :].rearrange("p b t -> p (b t)")
            f[2] = S.stt(Xu, B2[:, 0:256], self.ab[:, 3:4], Xu, ALU.add, ALU.add, t, self.tX)
            self.done.append(f[2])
            yield

    def all(self):
        self.load_x()
        self.stages = []
        self.mamba_prep()
        run(self.gru())
        self.wfree = [self.tX, self.tG]

        def go(gens):
            run(*gens)
            e = [s.end() for s in self.open]
            self.open = []
            return e
        e = go(self.mamba())
        self.tX = self.done
        self.wfree = e
        self.tGfree = e
        self.cond2_prep()
        self.wfree = self.wfree + e
        e = go(self.cond2())
        self.tG = self.done
        self.wfree = e
        self.cattfree = e
        e = go(self.moe(0))
        self.tX = self.done
        self.wfree = self.tGfree = self.moefree = e
        run((self.lstm(0), 1), (self.attn_prep(), 1))
        e = go(self.attn())
        self.tX = self.done
        self.wfree = self.tGfree = e
        run(self.lstm(1))
        e = go(self.moe(1))
        fin = Stage(self.p, "fin")
        fin.put("sync", lambda e: e.nop(), self.done)

    def one(self, stage, dbg):
        t1 = self.load(self.X[:], self.I["dX"])
        t2 = self.load(self.G[:], self.I["dG"])
        self.tX, self.tG, self.tGfree = [t1], [t2], [t2]
        if stage == "gru":
            run(self.gru())
        elif stage.startswith("lstm"):
            run(self.lstm(int(stage[-1])))
        elif stage == "mamba":
            self.mamba_prep(); run(*self.mamba()); self.tX = self.done
        elif stage == "cond2":
            self.cond2_prep(); run(*self.cond2()); self.tG = self.done
        elif stage == "moe0":
            run(*self.moe(0)); self.tX = self.done
        elif stage == "attn1":
            run(self.attn_prep()); run(*self.attn()); self.tX = self.done
        elif stage == "moe1":
            run(*self.moe(1)); self.tX = self.tX + self.done
        ts = [self.load(dbg[0], self.X[:], self.tX), self.load(dbg[1], self.G[:], self.tG)]
        fin = Stage(self.p, "fin")
        fin.put("sync", lambda e: e.nop(), ts)


def host_consts():
    import numpy as np
    oh = np.zeros((32, 512), np.float32)
    for j in range(255):
        oh[bucket(j - 127), j] = 1.0
        oh[bucket(j - 127), 256 + 254 - j] = 1.0
    return {"onehot": oh}


def bucket(n):
    import numpy as np
    if n < 16:
        return max(n, 0)
    v = np.log(np.float32(n) / np.float32(16)).astype(np.float32) / np.float32(np.log(128 / 16)) * np.float32(16)
    return min(16 + int(v), 31)


_INS = ['x', 'cond_1024', 'L0_cond_W_z', 'L0_cond_U_z', 'L0_cond_C_z', 'L0_cond_b_z', 'L0_cond_W_r', 'L0_cond_U_r',
        'L0_cond_C_r', 'L0_cond_b_r', 'L0_cond_W', 'L0_cond_U', 'L0_cond_C', 'L0_cond_b', 'L0_attn_W_in',
        'L0_attn_conv_w', 'L0_attn_conv_b', 'L0_attn_dt_bias', 'L0_attn_A_log', 'L0_attn_D', 'L0_attn_init_states',
        'L0_attn_norm_w', 'L0_attn_W_out', 'L0_attn_W_nl', 'L0_attn_b_nl', 'L0_cond2_WQ_w', 'L0_cond2_WQ_b',
        'L0_cond2_WK_w', 'L0_cond2_WK_b', 'L0_cond2_WV_w', 'L0_cond2_WV_b', 'L0_cond2_WO_w', 'L0_cond2_WO_b',
        'L0_ffn_router_kernel_DE', 'L0_ffn_kernel_gating_EDF', 'L0_ffn_kernel_up_EDF', 'L0_ffn_kernel_down_EFD',
        'L1_cond_Wx', 'L1_cond_Wh', 'L1_cond_b', 'L1_attn_wq', 'L1_attn_bq', 'L1_attn_wk', 'L1_attn_bk', 'L1_attn_wv',
        'L1_attn_bv', 'L1_attn_wo', 'L1_attn_bo', 'L1_attn_rel_bias', 'L1_cond2_Wx', 'L1_cond2_Wh', 'L1_cond2_b',
        'L1_ffn_sw1', 'L1_ffn_sw2', 'L1_ffn_sw3', 'L1_ffn_ew1', 'L1_ffn_ew2', 'L1_ffn_ew3', 'L1_ffn_rw', 'L1_ffn_rb']


def kernel(**inputs):
    import numpy as _np
    import concourse.bacc as _bacc
    from concourse import mybir as _mybir
    from concourse.bass_utils import run_bass_kernel_spmd as _run

    nc = _bacc.Bacc("TRN2", target_bir_lowering=False, num_devices=1)
    arrays, args = {}, {}
    data = {name: inputs[name] for name in _INS}
    data.update(host_consts())
    for name, v in data.items():
        a = _np.ascontiguousarray(v)
        arrays[f"in_{name}"] = a
        args[name] = nc.dram_tensor(f"in_{name}", a.shape, _mybir.dt.from_np(a.dtype), kind="ExternalInput").ap()
    out = nc.dram_tensor("out_0", (NB, T, D), F32, kind="ExternalOutput").ap()
    program(nc, args, out)
    r = _run(nc, [arrays], core_ids=[0])
    return r.results[0]["out_0"]
```

```python
import concourse.bass as bass
from concourse import mybir
from contextlib import ExitStack

F32 = mybir.dt.float32
BF16 = mybir.dt.bfloat16
ALU = mybir.AluOpType
ACT = mybir.ActivationFunctionType
AX = mybir.AxisListType


class Tok:

    def __init__(self, sem, step):
        self.sem, self.step, self.used, self.value = sem, step, False, None


class Counter:

    def __init__(self, prog, name):
        self.h = prog.ctx.enter_context(prog.nc.semaphore(name))
        self.count = 0


class Prog:

    ENG = ("tensor", "scalar", "vector", "gpsimd", "sync")

    def __init__(self, nc, ctx):
        self.nc, self.ctx = nc, ctx
        self.q = {e: [] for e in self.ENG}

    def sb(self, name, shape, dt=F32):
        return self.ctx.enter_context(self.nc.sbuf_tensor(name, shape, dt))

    def bank(self, name):
        return self.ctx.enter_context(self.nc.psum_tensor(name, [128, 512], F32))

    def counter(self, name):
        return Counter(self, name)

    def put(self, eng, counter, fn, waits, step=1):
        tok = Tok(counter, step)
        flat = []

        def take(w):
            if isinstance(w, (list, tuple)):
                for x in w:
                    take(x)
            elif w is not None:
                w.used = True
                flat.append(w)
        take(waits)
        if step == 16:
            tok.used = True
        self.q[eng].append((fn, flat, tok))
        return tok

    def emit(self):
        for e in self.ENG:
            for fn, waits, tok in self.q[e]:
                if tok.used:
                    tok.sem.count += tok.step
                    tok.value = tok.sem.count
        block = self.ctx.enter_context(self.nc.Block())
        for e in self.ENG:
            def body(eng, e=e):
                seen = {}
                for fn, waits, tok in self.q[e]:
                    need = {}
                    for w in waits:
                        if w.value > need.get(w.sem, 0):
                            need[w.sem] = w.value
                    for s, v in need.items():
                        if v > seen.get(s, 0):
                            eng.wait_ge(s.h, v)
                            seen[s] = v
                    ins = fn(eng)
                    if tok.used:
                        ins.then_inc(tok.sem.h, tok.step)
            blocks = {"tensor": block.tensor, "scalar": block.scalar, "vector": block.vector,
                            "gpsimd": block.gpsimd, "sync": block.sync}
            blocks[e](body)


class Stage:

    def __init__(self, p, name):
        self.p, self.name, self.c, self.latest = p, name, {}, {}

    def put(self, eng, fn, waits):
        if eng not in self.c:
            self.c[eng] = self.p.counter(f"s_{self.name}_{eng}")
        t = self.latest[eng] = self.p.put(eng, self.c[eng], fn, waits)
        return t

    def end(self):
        return list(self.latest.values())

    def mm(self, out, lhsT, rhs, start, stop, *waits):
        return self.put("tensor", lambda e: e.matmul(out, lhsT, rhs, start=start, stop=stop, skip_group_check=True), waits)

    def tr(self, out, in_, ident, *waits):
        return self.put("tensor", lambda e: e.transpose(out, in_, ident), waits)

    def act(self, out, in_, func, *waits, bias=0.0, scale=1.0):
        return self.put("scalar", lambda e: e.activation(out, in_, func, bias=bias, scale=scale), waits)

    def actsum(self, out, in_, func, total, *waits):
        return self.put("scalar", lambda e: e.activation(out, in_, func, accum_out=total), waits)

    def tt(self, out, a, b, op, *waits, eng="vector"):
        return self.put(eng, lambda e: e.tensor_tensor(out, a, b, op), waits)

    def ts(self, out, a, s1, s2, op0, op1, *waits, eng="vector"):
        if op1 is None:
            return self.put(eng, lambda e: e.tensor_scalar(out, a, s1, None, op0), waits)
        return self.put(eng, lambda e: e.tensor_scalar(out, a, s1, s2, op0, op1), waits)

    def stt(self, out, a, s, b, op0, op1, *waits):
        return self.put("vector", lambda e: e.scalar_tensor_tensor(out=out, in0=a, scalar=s, in1=b, op0=op0, op1=op1), waits)

    def cp(self, out, a, *waits, eng="vector"):
        return self.put(eng, lambda e: e.tensor_copy(out, a), waits)

    def red(self, out, a, op, *waits):
        return self.put("vector", lambda e: e.tensor_reduce(out, a, axis=AX.X, op=op), waits)

    def recip(self, out, a, *waits):
        return self.put("vector", lambda e: e.reciprocal(out, a), waits)

    def memset(self, out, v, *waits, eng="gpsimd"):
        return self.put(eng, lambda e: e.memset(out, v), waits)

    def sel(self, out, in_, op, fill, base, pattern, cm, *waits):
        return self.put("gpsimd", lambda e: e.affine_select(out=out, in_=in_, compare_op=op, fill=fill, base=base,
                                                            pattern=pattern, channel_multiplier=cm), waits)


def run(*lanes):
    lanes = [list(x) if isinstance(x, tuple) else [x, 1] for x in lanes]
    while lanes:
        for l in list(lanes):
            for _ in range(l[1]):
                try:
                    next(l[0])
                except StopIteration:
                    lanes.remove(l)
                    break

NB, T, D = 32, 128, 128
N = NB * T


def bc(ap, axis, n):
    a = ap.unsqueeze(axis)
    shape = list(a.shape)
    shape[axis] = n
    return a.broadcast_to(shape)


def program(nc, I, out, only=None, dbg=None):
    ctx = ExitStack()
    with ctx:
        p = Prog(nc, ctx)
        K = Kernel(p, I, out)
        K.consts()
        if only is None:
            K.all()
        else:
            K.one(only, dbg)
        p.emit()


class Kernel:
    def __init__(self, p, I, out):
        self.p, self.I, self.out = p, I, out
        sb = p.sb
        self.X = sb("X", [128, NB, T])
        self.G = sb("G", [128, NB, T])
        self.bank = [p.bank(f"B{i}") for i in range(8)]
        self.tX = None
        self.tG = None
        self.ndma = 0
        self.open = []
        self.moefree = None
        self.cattfree = None
        self.final = False
        self.cout = p.counter('s_out')
        self.tGfree = None
        self.work = sb("work", [128, 78 * 256])
        self.moew = sb("moew", [128, 27 * 256])
        self.catt = sb("catt", [128, 36 * 256])
        self.wfree = []
        self.NT = 6
        self.CY = 4
        self.VC = (1, 4, 7)
        self.R1 = 8
        self.R2 = 4
        self.R3 = 14
        self.R4 = 1
        self.R5 = 1
        self.WY = 2
        self.lag2 = 1

    def area(self, base, shape, dt=F32):
        n = 1
        for s in shape[1:]:
            n *= s
        words = n if dt == F32 else (n + 1) // 2
        t, at = base
        assert at + words <= t.shape[1], (at, words, t.shape)
        base[1] = at + words
        v = t[0:shape[0], at:at + words]
        if dt != F32:
            v = v.bitcast(dt)
        if len(shape) == 3:
            v = v.rearrange("p (a b) -> p a b", b=shape[2])
        elif len(shape) == 4:
            v = v.rearrange("p (a b c) -> p a b c", b=shape[2], c=shape[3])
        return v

    def load(self, dst, src, *waits, eng="sync", counter=None):
        if counter is None:
            self.ndma += 1
            counter = self.p.counter(f"s_ld{self.ndma}")
        return self.p.put(eng, counter, lambda e: e.dma_start(dst, src), waits, 16)

    def loads(self, pairs, *waits, eng="sync"):
        self.ndma += 1
        c = self.p.counter(f"s_ld{self.ndma}")
        for d, s in pairs:
            t = self.load(d, s, *waits, eng=eng, counter=c)
        return t

    def consts(self):
        p, I = self.p, self.I
        S = self.S0 = Stage(p, "const")
        sb = p.sb
        self.ident = sb("ident", [128, 128])
        self.identb = sb("identb", [128, 128], BF16)
        t = S.memset(self.ident[:], 0.0)
        self.tI = S.sel(self.ident[:], self.ident[:], ALU.not_equal, 1.0, 0, [[-1, 128]], 1, t)
        self.tIb = S.cp(self.identb[:], self.ident[:], self.tI, eng="gpsimd")
        self.tri = sb("tri", [128, 128])
        self.triq = sb("triq", [128, 128])
        self.low = sb("low", [128, 128])
        self.ones = sb("ones", [128, 128])
        t1 = S.memset(self.ones[:], 1.0)
        t = S.sel(self.tri[:], self.ones[:], ALU.is_ge, 0.0, 0, [[1, 128]], -1, t1)
        t2 = S.sel(self.low[:], self.ones[:], ALU.is_gt, 0.0, 0, [[-1, 128]], 1, t1)
        t3 = S.ts(self.triq[:], self.tri[:], 0.25, None, ALU.mult, None, t, eng="gpsimd")
        self.tTri = t3
        self.cond = sb("condt", [32, 128])
        self.condT = sb("condT", [128, 32])
        self.condT2 = sb("condT2", [128, 32])
        tl = self.load(self.cond[:], I["cond_1024"])
        B = self.bank[0]
        t = S.tr(B[:, 0:32], self.cond[:], self.ident[0:32, 0:32], tl, self.tI)
        self.tcond = S.act(self.condT[:], B[:, 0:32], ACT.Copy, t)
        self.tcond2 = S.act(self.condT2[:], B[:, 0:32], ACT.Copy, t, scale=2.0)
        self.tcond = self.tcond2
        self.gw = sb("gw", [128, 9, 128])
        self.gb = sb("gb", [128, 3])
        ws = ["L0_cond_W_z", "L0_cond_W_r", "L0_cond_W", "L0_cond_U_z", "L0_cond_U_r", "L0_cond_U",
              "L0_cond_C_z", "L0_cond_C_r", "L0_cond_C"]
        self.lgw = self.loads([(self.gw[:, i, :], I[n]) for i, n in enumerate(ws)] +
                              [(self.gb[:, i:i + 1], I[n].rearrange("(p o) -> p o", o=1))
                               for i, n in enumerate(["L0_cond_b_z", "L0_cond_b_r", "L0_cond_b"])])

    def load_x(self):
        S, I = self.S0, self.I
        w = [self.work, 0]
        xt = self.area(w, [128, NB, D])
        tok = []
        for u in range(4):
            tok.append(self.load(xt[:, u * 8:u * 8 + 8, :], I["x"][u * 8:u * 8 + 8].rearrange("b t d -> t b d"),
                                 eng="sync" if u % 2 else "scalar"))
        cur = {}
        for u in range(8):
            B = self.bank[2 + u % 4]
            for j in range(4):
                t = S.tr(B[:, j * 128:(j + 1) * 128], xt[:, 4 * u + j, :], self.ident[:], tok[u // 2], self.tI, cur.get(u % 4))
            dst = self.X[:, 4 * u:4 * u + 4, :].rearrange("p b t -> p (b t)")
            if u % 2:
                cur[u % 4] = S.cp(dst, B[:], t)
            else:
                cur[u % 4] = S.act(dst, B[:], ACT.Copy, t)
        self.tX = list(cur.values())
        self.wfree = self.tX

    def gru(self, banks=(6, 7), zbanks=(4, 5)):
        p, I = self.p, self.I
        S = Stage(p, "gru")
        gw, gb = self.gw, self.gb
        V = p.sb("gV", [128, 3, 32])
        tw = []
        for i in (0, 1, 3, 4, 5, 6, 7):
            tw.append(S.ts(gw[:, i, :], gw[:, i, :], 0.5, None, ALU.mult, None, self.lgw))
        tw = [tw[-1], S.ts(gb[:, 0:2], gb[:, 0:2], 0.5, None, ALU.mult, None, self.lgw)]
        B = self.bank[banks[0]]
        for g in range(3):
            t = S.mm(B[:, g * 32:g * 32 + 32], gw[:, 6 + g, :], self.condT[:], True, True, tw, self.tcond)
        for g in range(3):
            tV = S.act(V[:, g, :], B[:, g * 32:g * 32 + 32], ACT.Identity, t, bias=gb[:, g:g + 1])
        h = [p.sb(f"gh{i}", [128, 32]) for i in range(2)]
        th = p.sb("gth", [128, 2, 32])
        hh = p.sb("ghh", [128, 32])
        rh = p.sb("grh", [128, 32])
        zz = p.sb("gz", [128, 32])
        aa = p.sb("ga", [128, 32])
        zh = p.sb("gzh", [128, 32])
        th_ = S.memset(h[1][:], 0.0, eng="vector")
        free = [[tV, self.wfree], self.wfree]

        def pre(q):
            BR, BZ = self.bank[banks[q % 2]], self.bank[zbanks[q % 2]]
            R3 = BR[:, 0:256].rearrange("p (s g b) -> p s g b", s=4, g=2)
            Z3 = BZ[:, 0:128].rearrange("p (s b) -> p s b", s=4)
            xq = self.X[:, :, 4 * q:4 * q + 4].rearrange("p b s -> p s b")
            S.mm(BR[:, 0:256].rearrange("p (s c) -> p s c", s=4), self.ident[:],
                 bc(V[:, 1:3, :].rearrange("p g b -> p (g b)"), 1, 4), True, False, tV, self.tI, free[q % 2])
            S.mm(Z3, self.ident[:], bc(V[:, 0, :], 1, 4), True, False)
            yield
            for out, g in ((R3[:, :, 0, :], 1), (R3[:, :, 1, :], 2), (Z3, 0)):
                S.mm(out, gw[:, g, :], xq, False, False, tw, self.tX)
                if g:
                    yield
            yield
        for _ in pre(0):
            pass
        thm = th_
        tz0 = tz_ = tcopy = tzh = None
        gcopy = [None, None]
        for t in range(T):
            if t % 4 == 0 and t + 4 < T:
                ahead = pre(t // 4 + 1)
            q = (t // 4) % 2
            B, BZ = self.bank[banks[q]], self.bank[zbanks[q]]
            o, oz = (t % 4) * 64, (t % 4) * 32
            hp, hn = h[(t + 1) % 2][:], h[t % 2][:]
            m = self.mmh(S, B, o, gw[:, 4, :], hp, thm)
            mz = self.mmh(S, BZ, oz, gw[:, 3, :], hp)
            a1 = S.act(th[:, 1, :], B[:, o:o + 32], ACT.Tanh, m, thm)
            a0 = S.act(th[:, 0, :], BZ[:, oz:oz + 32], ACT.Tanh, mz, thm)
            trh = S.stt(rh[:], th[:, 1, :], 1.0, hp, ALU.add, ALU.mult, a1, thm)
            m = self.mmh(S, B, o + 32, gw[:, 5, :], rh[:], trh)
            if t + 4 < T or t % 4:
                next(ahead, None)
            a2 = S.act(hh[:], B[:, o + 32:o + 64], ACT.Tanh, m, tzh)
            tz_ = S.ts(zz[:], th[:, 0, :], 0.5, 0.5, ALU.mult, ALU.add, a0)
            t1 = S.tt(aa[:], zz[:], hp, ALU.mult, tz_)
            t1 = S.tt(aa[:], hp, aa[:], ALU.subtract, t1)
            tzh = S.tt(zh[:], zz[:], hh[:], ALU.mult, a2)
            thm = S.tt(hn, zh[:], aa[:], ALU.add, tzh, t1, gcopy[t % 2])
            free[q] = a2
            gcopy[t % 2] = S.cp(self.G[:, :, t], hn, thm, self.tGfree, eng="gpsimd")
            yield
        self.tG = gcopy

    def lstm(self, li, banks=(6, 7), obanks=(4, 5)):
        p, I = self.p, self.I
        S = Stage(p, f"lstm{li}")
        pre_ = "L1_cond" if li == 0 else "L1_cond2"
        if not hasattr(self, "lt"):
            self.lt = dict(lw=p.sb("lw", [128, 8, 128]), b3=p.sb("lb3", [128, 128], BF16), b4=p.sb("lb4", [4, 128]),
                           r4=p.sb("lr4", [4, 128]), q4=p.sb("lq4", [4, 128], BF16),
                           ind=p.sb("lind", [128, 4, 4, 32], BF16), H=[p.sb(f"lH{i}", [128, 32]) for i in range(2)],
                           Dc=p.sb("lD", [128, 32]), th=p.sb("lth", [128, 4, 32]), tc=p.sb("ltc", [128, 32]),
                           pp=p.sb("lp", [128, 32]), qq=p.sb("lq", [128, 32]))
            self.lfree = None
        lt, lfree = self.lt, self.lfree
        lw, b3, b4, r4, q4, ind, H = lt["lw"], lt["b3"], lt["b4"], lt["r4"], lt["q4"], lt["ind"], lt["H"]
        Dc, th, tc, pp, qq = lt["Dc"], lt["th"], lt["tc"], lt["pp"], lt["qq"]
        ld = self.loads([(lw[:, 0:4, :], I[pre_ + "_Wx"].rearrange("k (g e) -> k g e", g=4)),
                         (lw[:, 4:8, :], I[pre_ + "_Wh"].rearrange("k (g e) -> k g e", g=4)),
                         (b4[:, :], I[pre_ + "_b"].rearrange("(g e) -> g e", g=4))], lfree)
        tw = [S.ts(lw[:, 0:3, :], lw[:, 0:3, :], 0.5, None, ALU.mult, None, ld, eng="gpsimd"),
              S.ts(lw[:, 4:7, :], lw[:, 4:7, :], 0.25, None, ALU.mult, None, ld, eng="gpsimd"),
              S.ts(lw[:, 7, :], lw[:, 7, :], 0.5, None, ALU.mult, None, ld, eng="gpsimd")]
        t = S.ts(b4[:], b4[:], self.half3(S), None, ALU.mult, None, ld, self.thalf)
        z = S.memset(b3[:], 0.0, lfree)
        t1 = S.cp(b3[0:4, :], b4[:], t, z)
        t2 = S.tt(r4[:], b4[:], b3[0:4, :], ALU.subtract, t1)
        t3 = S.cp(b3[32:36, :], r4[:], t2)
        t4 = S.cp(q4[:], r4[:], t2)
        t5 = S.tt(r4[:], r4[:], q4[:], ALU.subtract, t4, t3)
        t6 = S.cp(b3[64:68, :], r4[:], t5)
        z = S.memset(ind[:], 0.0, lfree)
        for base in (0, 32, 64):
            v = ind[base:base + 4]
            z = S.sel(v, v, ALU.not_equal, 1.0, 0, [[0, 4], [-1, 4], [0, 32]], 1, z)
        tb = [t3, t6, z]
        tD = S.memset(Dc[:], 0.0, z)
        free = [self.wfree, self.wfree]

        def pre(q):
            BF, BO = self.bank[banks[q % 2]], self.bank[obanks[q % 2]]
            F3 = BF[:, 0:384].rearrange("p (s g b) -> p s g b", s=4, g=3)
            O3 = BO[:, 0:128].rearrange("p (s b) -> p s b", s=4)
            xq = self.X[:, :, 4 * q:4 * q + 4].rearrange("p b s -> p s b")
            S.mm(F3[:, :, 0:2, :], b3[0:68, :], ind[0:68, :, 0:2, :], True, False, tb, free[q % 2])
            S.mm(F3[:, :, 2, :], b3[0:68, :], ind[0:68, :, 3, :], False, False)
            S.mm(O3, b3[0:68, :], ind[0:68, :, 2, :], True, False)
            for out, g in ((F3[:, :, 0, :], 0), (F3[:, :, 1, :], 1), (F3[:, :, 2, :], 3), (O3, 2)):
                S.mm(out, lw[:, g, :], xq, False, False, tw, self.tX)
                yield
        yield
        for _ in pre(0):
            pass
        thm = S.cp(H[1][:], self.condT2[:], lfree, self.tcond2)
        ttc = None
        gcopy = [None, None]
        for t in range(T):
            if t % 4 == 0 and t + 4 < T:
                ahead = pre(t // 4 + 1)
            q = (t // 4) % 2
            B, BO = self.bank[banks[q]], self.bank[obanks[q]]
            o, oo = (t % 4) * 96, (t % 4) * 32
            hp, hn = H[(t + 1) % 2][:], H[t % 2][:]
            for i, g in enumerate((0, 1, 3)):
                m = self.mmh(S, B, o + 32 * i, lw[:, 4 + g, :], hp, thm)
            mo = self.mmh(S, BO, oo, lw[:, 6, :], hp)
            if t + 4 < T or t % 4:
                next(ahead, None)
            a1 = S.act(th[:, 0:3, :].rearrange("p g b -> p (g b)"), B[:, o:o + 96], ACT.Tanh, m, thm)
            ao = S.act(th[:, 3, :], BO[:, oo:oo + 32], ACT.Tanh, mo, thm)
            t1 = S.stt(pp[:], th[:, 0, :], 1.0, th[:, 2, :], ALU.add, ALU.mult, a1)
            t2 = S.stt(qq[:], th[:, 1, :], 1.0, Dc[:], ALU.add, ALU.mult, tD, a1)
            tD = S.stt(Dc[:], qq[:], 0.5, pp[:], ALU.mult, ALU.add, t1, t2, ttc)
            ttc = S.act(tc[:], Dc[:], ACT.Tanh, tD, thm, scale=0.5)
            thm = S.stt(hn, th[:, 3, :], 1.0, tc[:], ALU.add, ALU.mult, ttc, ao, gcopy[t % 2])
            free[q] = [a1, ao]
            gcopy[t % 2] = S.cp(self.G[:, :, t], hn, thm, self.tGfree, eng="gpsimd")
            yield
        self.tG = gcopy
        self.lfree = S.end()

    def mmh(self, S, B, o, w, h, *waits):
        for j in range(0, 128, 32):
            t = S.mm(B[j:j + 32, o:o + 32], w[:, j:j + 32], h, False, True, *waits)
        return t

    def half3(self, S):
        if not hasattr(self, "h3"):
            self.h3 = self.p.sb("h3", [4, 1])
            t = self.S0.memset(self.h3[:], 0.5)
            self.thalf = self.S0.sel(self.h3[:], self.h3[:], ALU.not_equal, 1.0, -3, [[0, 1]], 1, t)
        return self.h3[:]

    def mamba_prep(self):
        p, I = self.p, self.I
        sb = p.sb
        S = Stage(p, "mprep")
        self.win = sb("win", [128, 648])
        self.wout = sb("wout", [128, 2, 128])
        self.wnl = sb("wnl", [128, 128])
        self.bnl = sb("bnl", [128, 1])
        self.nw = sb("nw", [128, 2])
        self.cw = sb("cw", [128, 3, 16])
        self.cb = sb("cb", [128, 3])
        self.dtb = sb("dtb", [128, 8])
        self.alog = sb("alog", [128, 8])
        self.dcol = sb("dcol", [128, 2])
        self.dg = sb("dg", [128, 2, 128])
        self.h0 = sb("h0", [128, 2, 64])
        self.h0T = sb("h0T", [64, 256])
        pairs = [(self.win[:], I["L0_attn_W_in"]),
                 (self.wout[:], I["L0_attn_W_out"].rearrange("(c p) n -> p c n", p=128)),
                 (self.wnl[:], I["L0_attn_W_nl"]),
                 (self.bnl[:], I["L0_attn_b_nl"].rearrange("(p o) -> p o", o=1)),
                 (self.cw[:], I["L0_attn_conv_w"].rearrange("(c p) k -> p c k", p=128)),
                 (self.dtb[:], bc(I["L0_attn_dt_bias"], 0, 128)),
                 (self.alog[:], bc(I["L0_attn_A_log"], 0, 128)),
                 (self.h0[:], I["L0_attn_init_states"].rearrange("(c h) q n -> (h q) c n", c=2))]
        for c in range(2):
            pairs.append((self.nw[:, c:c + 1], I["L0_attn_norm_w"][c * 128:c * 128 + 128].rearrange("(p o) -> p o", o=1)))
            for j in range(4):
                pairs.append((self.dcol[32 * j:32 * j + 32, c:c + 1],
                              bc(I["L0_attn_D"][4 * c + j:4 * c + j + 1], 0, 32)))
        for c in range(3):
            pairs.append((self.cb[:, c:c + 1], I["L0_attn_conv_b"][c * 128:c * 128 + 128].rearrange("(p o) -> p o", o=1)))
        ld = self.loads(pairs, eng="scalar")
        for c in range(2):
            t = S.ts(self.wout[:, c, :], self.wout[:, c, :], self.nw[:, c:c + 1], None, ALU.mult, None, ld)
        t = S.ts(self.dcol[:], self.dcol[:], 0.5, None, ALU.mult, None, ld)
        for c in range(2):
            t = S.ts(self.dg[:, c, :], self.ident[:], self.dcol[:, c:c + 1], None, ALU.mult, None, t, self.tI)
        self.tap = self.area([self.moew, 0], [128, 3 * self.NT, 128])
        for c in range(3):
            for k in range(self.NT):
                tg = S.ts(self.tap[:, c * self.NT + k, :], self.ident[:], self.cw[:, c, k:k + 1], None, ALU.mult, None,
                          ld, self.tI)
        t = [t, tg]
        B = self.bank[1]
        for c in range(2):
            tm = S.tr(B[0:64, c * 128:c * 128 + 128], self.h0[:, c, :], self.ident[:], ld, self.tI)
        t2 = S.act(self.h0T[:], B[0:64, 0:256], ACT.Copy, tm, scale=0.5)
        t3 = S.act(self.alog[:], self.alog[:], ACT.Exp, ld)
        t4 = S.ts(self.alog[:], self.alog[:], -1.0, None, ALU.mult, None, t3)
        self.tmw = [t, t2, t4, ld]
        self.tb1 = t2

    def mamba_dt(self, bs=range(NB)):
        p = self.p
        S = Stage(p, "mdt")
        n0, n = bs[0], len(bs)
        if not hasattr(self, "adt"):
            self.adt = p.sb("adt", [128, NB, 8])
            self.dth = p.sb("dth", [128, NB, 8])
            self.ec = p.sb("ec", [128, NB, 8])
            self.q1 = p.sb("mq1", [128, NB, 8])
            self.q2 = p.sb("mq2", [128, NB, 8])
            self.q3 = p.sb("mq3", [128, NB, 8])
        B = self.bank[0]
        s = slice(n0, n0 + n)
        P = B[:, 0:8 * n].rearrange("p (b h) -> p b h", h=8)
        for i, b in enumerate(bs):
            tm = S.mm(P[:, i, :], self.G[:, b, :], self.win[:, 640:648], True, True, self.tG, self.tmw)
        x, e, z, q = self.dth[:, s, :], self.q1[:, s, :], self.q2[:, s, :], self.q3[:, s, :]
        t = S.tt(x, P, bc(self.dtb[:], 1, n), ALU.add, tm)
        t = S.stt(e, x, -1.0, x, ALU.mult, ALU.min, t)
        t = S.act(e, e, ACT.Exp, t)
        yield
        t = S.ts(z, e, 2.0, None, ALU.add, None, t)
        t = S.recip(z, z, t)
        yield
        t = S.tt(z, z, e, ALU.mult, t)
        t = S.tt(e, z, z, ALU.mult, t)
        t = S.ts(q, e, 1 / 19, 1 / 17, ALU.mult, ALU.add, t)
        for k in (15, 13, 11, 9, 7, 5, 3, 1):
            t = S.tt(q, q, e, ALU.mult, t)
            t = S.ts(q, q, 1.0 / k, None, ALU.add, None, t)
            yield
        t = S.tt(q, q, z, ALU.mult, t)
        t = S.ts(x, x, 0.0, 0.5, ALU.max, ALU.mult, t)
        t = S.tt(x, x, q, ALU.add, t)
        a = self.adt[:, s, :]
        yield
        t = S.tt(a, x, bc(self.alog[:], 1, n), ALU.mult, t)
        t = S.ts(a, a, 2.0, None, ALU.mult, None, t)
        P2 = B[:, 256:256 + 8 * n].rearrange("p (b h) -> p b h", h=8)
        yield
        tm = S.mm(P2, self.tri[:], a, True, True, t, self.tTri)
        t2 = S.act(self.ec[:, s, :], P2, ACT.Exp, tm)
        self.tdt = [t, t2]

    def mamba(self, bs=range(NB), workers=2):
        self.tdt = None
        w = [self.work, 0]
        units = [list(bs)[i:i + 4] for i in range(0, len(bs), 4)]
        self.cvb = [self.area(w, [128, 3, 512]) for _ in range(3)]
        self.c0b = [self.area(w, [128, 512]) for _ in range(3)]
        self.cvready, self.cvfree = {}, {}
        gens = [self.mamba_conv(units, w), (self.mamba_dt(bs), 2)]
        gens += [self.mamba_worker(k, units, w) for k in range(workers)]
        self.done = []
        return gens

    def mamba_conv(self, units, w):
        S = Stage(self.p, "mconv")
        self.open.append(S)
        ar = lambda *s, dt=F32: self.area(w, list(s), dt)
        XP = [ar(128, 4, 144) for _ in range(3)]
        th = [ar(128, 512) for _ in range(2)]
        NT = self.NT
        BI, BT = self.bank[6], self.bank[7]
        fI = fT = self.wfree
        fX = [S.memset(x[:, :, 0:16], 0.0, self.wfree) for x in XP]
        fth = [None, None]
        n = 0
        pend = None
        for u, un in enumerate(units):
            while u >= 3 and u - 3 not in self.cvfree:
                yield
            Gu = self.G[:, un[0]:un[0] + 4, :].rearrange("p b t -> p (b t)")
            cv, C0 = self.cvb[u % 3], self.c0b[u % 3]
            fcv = self.cvfree.get(u - 3, self.wfree)
            tks = []
            for c in range(3):
                X, th_ = XP[n % 3], th[n % 2]
                t = S.mm(BI[:], self.win[:, 256 + c * 128:384 + c * 128], Gu, True, True, fI, self.tG, self.tmw)
                fI = tx = S.act(X[:, :, 16:144], BI[:].rearrange("p (b t) -> p b t", b=4), ACT.Copy, t, fX[n % 3])
                yield
                for k in range(NT):
                    t = S.mm(BT[:], self.tap[:, c * NT + k, :], X[:, :, 1 + k:129 + k], k == 0, k == NT - 1, tx, fT)
                acc = cv[:, c, :].rearrange("p (b t) -> p b t", b=4)
                fT = t = S.act(cv[:, c, :], BT[:], ACT.Identity, t, fcv, bias=self.cb[:, c:c + 1])
                if pend:
                    pend()
                yield
                th2 = [t, t]
                for k in range(NT, 16):
                    for i in range(2):
                        b2 = slice(2 * i, 2 * i + 2)
                        th2[i] = S.stt(acc[:, b2, :], X[:, b2, 1 + k:129 + k], self.cw[:, c, k:k + 1], acc[:, b2, :],
                                       ALU.mult, ALU.add, th2[i])
                    if (k - NT) % self.CY == self.CY - 1:
                        yield
                t = th2
                fX[n % 3] = t

                def silu(t=t, c=c, th_=th_, n=n, cv=cv, C0=C0, u=u, tks=tks, fcv=fcv):
                    ta = S.act(th_, cv[:, c, :], ACT.Tanh, t, fth[n % 2], scale=0.5)
                    if c < 2:
                        t1 = S.stt(cv[:, c, :], th_, 1.0, cv[:, c, :], ALU.add, ALU.mult, ta)
                    else:
                        t1 = S.stt(C0[0:64, :], th_[64:128, :], 1.0, cv[64:128, c, :], ALU.add, ALU.mult, ta, fcv)
                        t1 = S.stt(cv[0:64, c, :], th_[0:64, :], 1.0, cv[0:64, c, :], ALU.add, ALU.mult, ta)
                    fth[n % 2] = t1
                    tks.append(t1)
                    if c == 2:
                        self.cvready[u] = tks
                pend = silu
                n += 1
            if u + 1 == len(units):
                pend()
            yield

    def mamba_worker(self, wk, units, w):
        p = self.p
        S = Stage(p, f"mamba{wk}")
        self.open.append(S)
        ar = lambda *s, dt=F32: self.area(w, list(s), dt)
        B0, B1, B2 = self.bank[3 * wk:3 * wk + 3]
        wc = [self.catt, wk * 3072]
        E = [self.area(wc, [128, 8, 128]) for _ in range(2)]
        zt = [self.area(wc, [128, 256]) for _ in range(2)]
        xdt = ar(128, 256)
        cbm = ar(128, 128)
        y4 = ar(128, 4, 256)
        sq = ar(128, 256)
        ss = ar(128, 4)
        yT = ar(128, 2, 512)
        tm1 = ar(128, 512)
        while self.tdt is None:
            yield
        fb = [[self.tdt, self.wfree], [self.tb1, self.wfree], self.wfree]
        tE = tY = None
        tyT = ttm = trs = t_yT = tss = None
        fE, fz = [None, None], [None, None]
        seq = [b for u in range(wk, len(units), 2) for b in units[u]]
        ahead = {}

        def decay(n):
            b, k = seq[n], n % 2
            e, z = E[k], zt[k]
            ef = e.rearrange("p h t -> p (h t)")
            t = S.tt(e, bc(self.tri[:], 1, 8), bc(self.adt[:, b, :], 2, 128), ALU.mult, self.tdt, fE[k], eng="gpsimd")
            yield
            t1 = S.mm(B1[:], self.low[:], ef[:, 0:512], True, True, t, fb[1])
            t2 = S.mm(B2[:], self.low[:], ef[:, 512:1024], True, True, fb[2])
            e1 = S.act(ef[:, 0:512], B1[:], ACT.Exp, t1)
            e2 = S.act(ef[:, 512:1024], B2[:], ACT.Exp, t2)
            fb[1], fb[2] = e1, e2
            yield
            t = S.mm(B1[:, 0:256], self.G[:, b, :], self.win[:, 0:256], True, True, fb[1])
            t = S.act(z, B1[:, 0:256], ACT.Tanh, t, fz[k], scale=0.5)
            fb[1] = tz = S.stt(z, z, 1.0, B1[:, 0:256], ALU.add, ALU.mult, t)
            ahead[n] = [e1, e2, tz]
            yield
        for _ in decay(0):
            yield
        n = -1
        for u in range(wk, len(units), 2):
            un = units[u]
            while u not in self.cvready:
                yield
            tth = [self.cvready[u], self.wfree]
            cv, C0 = self.cvb[u % 3], self.c0b[u % 3]
            ub = slice(un[0], un[0] + 4)
            Gu = self.G[:, ub, :].rearrange("p b t -> p (b t)")
            for j, b in enumerate(un):
                ts_ = slice(j * 128, j * 128 + 128)
                n += 1
                nxt = decay(n + 1) if n + 1 < len(seq) else iter(())
                e, k = E[n % 2], n % 2
                e1, e2, tz = ahead.pop(n)
                S.mm(B2[:, 256:384], cv[0:64, 2, ts_], C0[0:64, ts_], True, True, tth, fb[2])
                for c in range(2):
                    t = S.tr(B2[:, c * 128:c * 128 + 128], cv[:, c, ts_], self.ident[:], tth, self.tI)
                tcbm = S.tt(cbm[:], B2[:, 256:384], self.triq[:], ALU.mult, t, tE, self.tTri)
                txd = S.tt(xdt[:].rearrange("p (h q) -> p h q", h=8), B2[:, 0:256].rearrange("p (h q) -> p h q", h=8),
                           bc(self.dth[:, b, :], 2, 32), ALU.mult, t, tY)
                fb[2] = [tcbm, txd]
                next(nxt, None)
                tE = S.tt(e, e, bc(cbm[:], 1, 8), ALU.mult, e1, e2, tcbm, eng="gpsimd")
                yield
                next(nxt, None)
                yield
                for c in range(2):
                    S.mm(B0[:, c * 128:c * 128 + 128], cv[:, c, ts_], self.dg[:, c, :], c == 0, False, fb[0])
                S.mm(B0[:, 256:512], C0[0:64, ts_], self.h0T[:], False, False)
                yield
                next(nxt, None)
                for h in range(8):
                    for r in range(0, 128, 32):
                        t = S.mm(B0[r:r + 32, h * 32:h * 32 + 32], e[:, h, r:r + 32], xdt[:, h * 32:h * 32 + 32],
                                 False, True, tE, txd)
                fE[k] = tY = t
                y = y4[:, j, :]
                y3 = y.rearrange("p (h q) -> p h q", h=8)
                t = S.tt(y3, B0[:, 256:512].rearrange("p (h q) -> p h q", h=8), bc(self.ec[:, b, :], 2, 32), ALU.mult,
                         t, self.tdt, t_yT)
                t = S.tt(y, y, B0[:, 0:256], ALU.add, t)
                fb[0] = t
                fz[k] = t_y = S.tt(y, y, zt[k], ALU.mult, t, tz)
                tss = S.actsum(sq[:], y, ACT.Square, ss[:, j:j + 1], t_y, trs, tss)
                yield
            self.cvfree[u] = tY
            t = S.ts(ss[:], ss[:], 1 / 256, 4e-5, ALU.mult, ALU.add, tss)
            t = S.recip(ss[:], ss[:], t)
            t = S.act(ss[:], ss[:], ACT.Sqrt, t)
            for j in range(4):
                trs = S.ts(y4[:, j, :], y4[:, j, :], ss[:, j:j + 1], None, ALU.mult, None, t, t_y)
            yield
            yield
            for h in range(2):
                for j in (2 * h, 2 * h + 1):
                    for c in range(2):
                        t = S.tr(B2[:, (j % 2) * 256 + c * 128:(j % 2) * 256 + c * 128 + 128], y4[:, j, c * 128:c * 128 + 128],
                                 self.ident[:], trs, fb[2])
                t_yT = t
                fb[2] = S.act(yT[:, :, h * 256:h * 256 + 256].rearrange("p c (j t) -> p j c t", j=2),
                              B2[:].rearrange("p (j c t) -> p j c t", j=2, c=2), ACT.Copy, t, tyT)
            t = fb[2]
            yield
            for c in range(2):
                tw_ = S.mm(B0[:], self.wout[:, c, :], yT[:, c, :], c == 0, c == 1, t, fb[0], self.tmw)
            tyT = tw_
            t1 = S.act(tm1[:], B0[:], ACT.Square, tw_, ttm)
            t1 = S.ts(tm1[:], tm1[:], 1.0, None, ALU.add, None, t1)
            yield
            t1 = S.recip(tm1[:], tm1[:], t1)
            t1 = S.act(tm1[:], tm1[:], ACT.Sqrt, t1)
            for _ in range(self.WY):
                yield
            t1 = S.tt(tm1[:], tm1[:], B0[:], ALU.mult, t1)
            fb[0] = t1
            yield
            t2 = S.mm(B1[:], self.wnl[:], tm1[:], True, True, t1, fb[1])
            ttm = t2
            Xu = self.X[:, ub, :].rearrange("p b t -> p (b t)")
            t3 = S.stt(Xu, B1[:], self.bnl[:], Xu, ALU.add, ALU.add, t2, self.tX)
            fb[1] = t3
            t4 = S.tt(Xu, Xu, Gu, ALU.add, t3, eng="gpsimd")
            self.done.append(t4)
            yield

    def cond2_prep(self, banks=(0, 1)):
        p, I = self.p, self.I
        S = Stage(p, "cprep")
        ca = [self.catt, 0]
        ar = lambda *s, dt=F32: self.area(ca, list(s), dt)
        self.WQ, self.WK, self.WO = ar(128, 8, 128), ar(128, 8, 128), ar(128, 8, 128)
        self.ckc = ar(128, 2, 8)
        self.bo = ar(128, 1)
        self.Gak = ar(128, NB, 16)
        self.cak = ar(128, NB, 16)
        self.avo = ar(16, NB, 128)
        w = [self.work, 78 * 256 - 20 * 256]
        WV = self.area(w, [128, 8, 128])
        akb = self.area(w, [128, 8, 2, 32])
        avb = self.area(w, [128, 8, 2, 32])
        wqT = self.area(w, [128, 8, 128])
        bqb = self.area(w, [128, 8, 128])
        avt = self.area([self.work, w[1] - 1024], [64, 8, 128])
        bv = p.sb("cbv", [128, 8])
        self.blk = p.sb("blk", [128, 2])
        self.selc = p.sb("selc", [48, 16, 64], BF16)
        self.wprep = None
        W = lambda n: I[n].rearrange("k (c m) -> k c m", c=8)
        col = lambda n: I[n].rearrange("(c p) -> p c", p=128)
        ld = self.loads([(self.WQ, W("L0_cond2_WQ_w")), (self.WK, W("L0_cond2_WK_w")), (WV, W("L0_cond2_WV_w")),
                         (self.WO, I["L0_cond2_WO_w"].rearrange("(c p) n -> p c n", p=128)),
                         (self.bo, I["L0_cond2_WO_b"].rearrange("(p o) -> p o", o=1))] +
                        [(d[:, c:c + 1], I[n][c * 128:c * 128 + 128].rearrange("(p o) -> p o", o=1))
                         for c in range(8) for d, n in ((self.ckc[:, 0, :], "L0_cond2_WQ_b"),
                                                        (self.ckc[:, 1, :], "L0_cond2_WK_b"), (bv, "L0_cond2_WV_b"))],
                        self.wfree, eng="scalar")
        z = S.memset(akb, 0.0, self.wfree)
        z2 = S.memset(avb, 0.0, self.wfree)
        t = S.sel(self.blk[:], self.ones[:, 0:2], ALU.is_ge, 0.0, 0, [[-64, 2]], 1, self.tI, self.tIb, self.tTri)
        self.tblk = S.sel(self.blk[:], self.blk[:], ALU.is_ge, 0.0, 63, [[64, 2]], -1, t)
        t = S.memset(self.selc[:], 0.0)
        for part in range(3):
            t = S.sel(self.selc[:], self.selc[:], ALU.not_equal, 1.0, -16 * part, [[-1, 16], [0, 64]], 1, t)
        self.tsel = t
        B0, B1 = self.bank[banks[0]], self.bank[banks[1]]
        for c in range(8):
            S.mm(B0[:, c * 32:c * 32 + 32], self.WK[:, c, :], self.condT[:], True, True, ld, self.tcond, self.wfree)
            t = S.mm(B0[:, 256 + c * 32:288 + c * 32], WV[:, c, :], self.condT[:], True, True)
        for c in range(8):
            for i in range(2):
                r = slice(64 * i, 64 * i + 64)
                t1 = S.act(akb[r, c, i, :], B0[r, c * 32:c * 32 + 32], ACT.Identity, t, z, bias=self.ckc[r, 1, c:c + 1])
                t1 = S.act(avb[r, c, i, :], B0[r, 256 + c * 32:288 + c * 32], ACT.Identity, t, z2, bias=bv[r, c:c + 1])
        f0 = t1
        f1 = None
        for g in range(2):
            for i in range(4):
                t = S.tr(B1[:, i * 128:i * 128 + 128], self.WQ[:, 4 * g + i, :], self.ident[:], ld, self.tI, f1, self.wfree)
            f1 = S.act(wqT[:, 4 * g:4 * g + 4, :].rearrange("p c m -> p (c m)"), B1[:], ACT.Copy, t)
        tb = S.cp(bqb, bc(self.ckc[:, 0, :], 2, 128), ld)
        for c in range(8):
            t = S.mm(B0[:, c * 64:c * 64 + 64], wqT[:, c, :], akb[:, c].rearrange("p i b -> p (i b)"), True, True, f0, f1)
        t2 = S.act(self.Gak.rearrange("p b (c i) -> p c i b", c=8), B0[:].rearrange("p (c i b) -> p c i b", c=8, i=2),
                   ACT.Copy, t)
        for c in range(8):
            t = S.mm(B1[:, c * 64:c * 64 + 64], bqb[:, c, :], akb[:, c].rearrange("p i b -> p (i b)"), True, True, f1, tb)
        t3 = S.act(self.cak.rearrange("p b (c i) -> p c i b", c=8), B1[:].rearrange("p (c i b) -> p c i b", c=8, i=2),
                   ACT.Copy, t)
        f = [t2, t3]
        for g in range(2):
            Bk = (B0, B1)[g]
            for i in range(4):
                c = 4 * g + i
                t = S.mm(Bk[0:64, i * 128:i * 128 + 128], avb[:, c].rearrange("p i b -> p (i b)"), self.WO[:, c, :],
                         True, True, f[g], f0)
            f[g] = S.act(avt[:, 4 * g:4 * g + 4, :].rearrange("p c m -> p (c m)"), Bk[0:64, :], ACT.Copy, t)
        t = self.loads([(self.avo[2 * c + i:2 * c + i + 1, :, :], avt[32 * i:32 * i + 32, c, :])
                        for c in range(8) for i in range(2)], f)
        self.tcw = [ld, t2, t3]
        self.tavo = t
        self.wlow = self.wfree
        self.wfree = self.wfree + [t, t2, t3]
        self.tb0, self.tb1 = f

    def cond2(self, bs=range(NB), workers=2):
        w = [self.work, 0]
        units = [list(bs)[i:i + 4] for i in range(0, len(bs), 4)]
        self.done = []
        return [self.cond2_worker(k, units[k::workers], w) for k in range(workers)]

    def cond2_worker(self, wk, units, w):
        S = Stage(self.p, f"cond2{wk}")
        free = self.wfree if wk else self.wlow
        self.open.append(S)
        ar = lambda *s, dt=F32: self.area(w, list(s), dt)
        Bs = self.bank[3 * wk + 2]
        ring = [self.bank[i] for i in (3 * wk, 3 * wk + 1, 6 + wk)]
        KP = ar(128, 8, 4, 130)
        pr = [ar(128, 512) for i in range(5)]
        sc = ar(128, 64, 4)
        m = ar(128, 64)
        sm = ar(128, 64)
        R = ar(128, 64, 4)
        A = ar(128, 4 * 3, 48, dt=BF16)
        AT = ar(48, 3, 512, dt=BF16)
        a0 = ar(16, 512)
        att = [ar(128, 512) for i in range(2)]
        tpad = S.memset(KP[:, :, :, 0:1], 0.0, free)
        tpad = S.memset(KP[:, :, :, 129:130], 0.0, free, tpad)
        fs = [self.tb0, self.tb1, self.tcw, free]
        fr = [fs] * 3
        r_ = 0
        fKP = [free] * 8
        fpr = [free] * 5
        x = 0
        tex = tA = tAT = ta0 = None
        fatt = [None, None]
        for _ in range(self.lag2 * wk):
            yield
        for un in units:
            ub = slice(un[0], un[0] + 4)
            Xu = self.X[:, ub, :].rearrange("p b t -> p (b t)")
            S3 = Bs[:, 0:256].rearrange("p (b h j) -> p b h j", b=4, h=16)
            for i, b in enumerate(un):
                for r in range(0, 128, 32):
                    t = S.mm(S3[r:r + 32, i, :, 0], self.X[:, b, r:r + 32], self.Gak[:, b, :], i == 0, False,
                             fs, self.tcw, self.tX)
            for c in range(8):
                iq, ik = r_ % 3, (r_ + 1) % 3
                r_ += 2
                Bq, Bk = ring[iq], ring[ik]
                tk = S.mm(Bk[:], self.WK[:, c, :], Xu, True, True, fr[ik], self.tcw, self.tX)
                tq = S.mm(Bq[:], self.WQ[:, c, :], Xu, True, True, fr[iq])
                fr[ik] = tk = S.act(KP[:, c, :, 1:129], Bk[:].rearrange("p (b t) -> p b t", b=4), ACT.Identity, tk, fKP[c],
                                bias=self.ckc[:, 1, c:c + 1])
                yield
                tp, xs = [], []
                for j in range(3):
                    x = (x + 1) % 5
                    xs.append(x)
                    fr[iq] = S.stt(pr[x].rearrange("p (b t) -> p b t", b=4), Bq[:].rearrange("p (b t) -> p b t", b=4),
                               self.ckc[:, 0, c:c + 1], KP[:, c, :, j:j + 128], ALU.add, ALU.mult, tq, tk, fpr[x], tpad)
                    tp.append(fr[iq])
                yield
                for j in range(3):
                    for i in range(4):
                        for r in range(0, 128, 32):
                            ts = S.mm(S3[r:r + 32, i, 2 * c:2 * c + 2, j + 1],
                                      pr[xs[j]][:, i * 128 + r:i * 128 + r + 32], self.blk[:], False, False,
                                      tp[j], self.tblk)
                    fpr[xs[j]] = ts
                yield
            S4 = sc.rearrange("p (b h) j -> p b h j", b=4)
            t = S.act(sc, S3.rearrange("p b h j -> p (b h) j"), ACT.Copy, ts, tA)
            t = S.tt(S4[:, :, :, 0], S4[:, :, :, 0], self.cak[:, ub, :], ALU.add, t)
            fs = t
            t = S.red(m, sc, ALU.max, t)
            t = S.tt(sc, sc, bc(m, 2, 4), ALU.subtract, t)
            t = S.act(sc, sc, ACT.Exp, t, scale=0.125)
            t = S.red(sm, sc, ALU.add, t)
            t = S.recip(sm, sm, t)
            t = S.tt(sc, sc, bc(sm, 2, 4), ALU.mult, t)
            Av = A.rearrange("p (b j) (q h) -> p b j q h", b=4, q=3)
            Sv = sc.rearrange("p (b h) j -> p b j h", b=4)
            Rb = R.rearrange("p x y -> p (x y)").rearrange("p (b j h) -> p b j h", b=4, j=4)
            A3, S3_, R3 = (lambda k: Av[:, :, :, k, :]), Sv[:, :, 1:4, :], Rb[:, :, 1:4, :]
            ta = S.cp(A3(0), S3_, t, tAT)
            tb = S.tt(R3, S3_, A3(0), ALU.subtract, ta)
            ta = S.cp(A3(1), R3, tb)
            tb = S.tt(R3, R3, A3(1), ALU.subtract, ta)
            tA = S.cp(A3(2), R3, tb)
            yield
            yield
            for i in range(4):
                t1 = S.tr(Bs[0:16, i * 128:i * 128 + 128], Sv[:, i, 0, :], self.ident[:], t, self.tI)
            ta0 = S.act(a0, Bs[0:16, :], ACT.Copy, t1, ta0)
            fs = ta0
            tAT_r = []
            for j in range(3):
                k = r_ % 3
                r_ += 1
                Bt = ring[k][:].bitcast(BF16)
                for i in range(4):
                    t1 = S.tr(Bt[0:48, i * 128:i * 128 + 128], Av[:, i, j, :, :].rearrange("p q h -> p (q h)"),
                              self.identb[:], tA, self.tIb, fr[k])
                fr[k] = S.act(AT[:, j, :], Bt[0:48, 0:512], ACT.Copy, t1, tAT)
                tAT_r.append(fr[k])
            yield
            for i, b in enumerate(un):
                to = S.mm(Bs[:, i * 128:i * 128 + 128], self.avo[:, b, :], a0[:, i * 128:i * 128 + 128], i == 0, False,
                          ta0, fs, self.tavo)
            tex = to
            late = []

            def wo(c, av, t):
                def go():
                    nonlocal to
                    fatt[c % 2] = to = S.mm(Bs[:], self.WO[:, c, :], av, False, c == 7, t)
                return go
            for c in range(8):
                prods, xs = [], []
                for j in range(3):
                    x = (x + 1) % 5
                    xs.append(x)
                    k = r_ % 3
                    r_ += 1
                    Bb, fb = ring[k], fr[k]
                    t1 = S.mm(Bb[:], self.selc[:, 2 * c:2 * c + 2, :].rearrange("p h d -> p (h d)"), AT[:, j, :], True, True,
                              tAT_r, self.tsel, fb)
                    tAT = t1
                    t2 = S.tt(pr[x].rearrange("p (b t) -> p b t", b=4), Bb[:].rearrange("p (b t) -> p b t", b=4),
                              KP[:, c, :, j:j + 128], ALU.mult, t1, fpr[x])
                    prods.append(t2)
                    fr[k] = t2
                    if j < 2:
                        yield
                if len(late) > 1:
                    late.pop(0)()
                fKP[c] = t2
                av = att[c % 2]
                u0, u1, u2 = (pr[v] for v in xs)
                t3 = S.tt(av, u0, u1, ALU.add, prods[1], fatt[c % 2], eng="gpsimd")
                fpr[xs[0]] = fpr[xs[1]] = t3
                t3 = S.tt(av, av, u2, ALU.add, t3, prods[2], eng="vector" if c in self.VC else "gpsimd")
                fpr[xs[2]] = t3
                late.append(wo(c, av, t3))
                yield
            for g in late:
                g()
                yield
            t = S.act(self.G[:, ub, :].rearrange("p b t -> p (b t)"), Bs[:], ACT.Identity, to, self.tGfree, bias=self.bo)
            fs = t
            self.done.append(t)
            yield

    def moe_load(self, li):
        I, w = self.I, [self.moew, 0]
        E = 8 + li
        self.wg, self.wu, self.wd = (self.area(w, [128, E, 256]), self.area(w, [128, E, 256]),
                                     self.area(w, [128, E * 2, 128]))
        ng, nu, nd = (("L0_ffn_kernel_gating_EDF", "L0_ffn_kernel_up_EDF", "L0_ffn_kernel_down_EFD"),
                      ("L1_ffn_ew1", "L1_ffn_ew2", "L1_ffn_ew3"))[li]
        self.rw = self.p.sb(f"rw{li}", [128, 8])
        self.rb = self.p.sb(f"rb{li}", [128, 8])
        pairs = [(self.rw[:], I[("L0_ffn_router_kernel_DE", "L1_ffn_rw")[li]]),
                 (self.wg[:, 0:8, :], I[ng].rearrange("e d f -> d e f")),
                 (self.wu[:, 0:8, :], I[nu].rearrange("e d f -> d e f")),
                 (self.wd[:, 0:16, :], I[nd].rearrange("e (c f) d -> f (e c) d", c=2))]
        if li:
            pairs += [(self.wg[:, 8, :], I["L1_ffn_sw1"]), (self.wu[:, 8, :], I["L1_ffn_sw2"]),
                      (self.wd[:, 16:18, :], I["L1_ffn_sw3"].rearrange("(c f) d -> f c d", c=2)),
                      (self.rb[:], bc(I["L1_ffn_rb"], 0, 128))]
        self.tmoe = self.loads(pairs, self.moefree)

    def moe_route(self, li, bs, bank, w):
        p = self.p
        S = Stage(p, f"route{li}")
        self.open.append(S)
        n = len(bs)
        ar = lambda *s, dt=F32: self.area(w, list(s), dt)
        if not hasattr(self, "rev"):
            self.rev = p.sb("rev", [128, 8])
            for e in range(8):
                self.trev = self.S0.memset(self.rev[:, e:e + 1], float(8 - e), eng="vector")
            self.selw = p.sb("selw", [24, 8, 128], BF16)
            t = self.S0.memset(self.selw[:], 0.0, self.tI)
            for part in range(3):
                t = self.S0.sel(self.selw[:], self.selw[:], ALU.not_equal, 1.0, -8 * part, [[-1, 8], [0, 128]], 1, t)
            self.tselw = t
        pr, f1, f2, mk = (ar(128, n, 8) for _ in range(4))
        m1, m2, q1, q2 = (ar(128, n) for _ in range(4))
        Wp = ar(128, n, 24, dt=BF16)
        WT = ar(24, n * 128, dt=BF16)
        B = self.bank[bank]
        P = B[:, 0:8 * n].rearrange("p (b e) -> p b e", e=8)
        for i, b in enumerate(bs):
            t = S.mm(P[:, i, :], self.G[:, b, :], self.rw[:], True, True, self.tG, self.tmoe, self.wfree)
        if li:
            t = S.stt(pr, P, 0.5, bc(self.rb[:], 1, n), ALU.mult, ALU.add, t, self.wfree)
        else:
            t = S.cp(pr, P, t, self.wfree)
        t = S.red(m1, pr, ALU.max, t)
        t = S.tt(pr, pr, bc(m1, 2, 8), ALU.subtract, t)
        t = S.act(pr, pr, ACT.Exp, t)
        t = S.red(m1, pr, ALU.add, t)
        t = S.recip(m1, m1, t)
        t = S.tt(pr, pr, bc(m1, 2, 8), ALU.mult, t)
        for k, (m, f, q) in enumerate(((m1, f1, q1), (m2, f2, q2))):
            t = S.red(m, pr, ALU.max, t)
            t = S.tt(mk, pr, bc(m, 2, 8), ALU.is_equal, t)
            t = S.tt(mk, mk, bc(self.rev[:], 1, n), ALU.mult, t, self.trev)
            t = S.red(q, mk, ALU.max, t)
            t = S.tt(f, mk, bc(q, 2, 8), ALU.is_equal, t)
            if k == 0:
                t = S.stt(pr, f, -4.0, pr, ALU.mult, ALU.add, t)
        if li:
            t = S.tt(q1, m1, m2, ALU.add, t)
            t = S.recip(q1, q1, t)
            t1 = S.tt(m1, m1, q1, ALU.mult, t)
            t2 = S.tt(m2, m2, q1, ALU.mult, t)
        else:
            t = S.tt(q1, m2, m1, ALU.subtract, t)
            t = S.act(q1, q1, ACT.Exp, t)
            t = S.ts(q2, q1, 1.0, None, ALU.add, None, t)
            t1 = S.recip(m1, q2, t)
            t2 = S.tt(m2, q1, m1, ALU.mult, t1)
        t = S.tt(f1, f1, bc(m1, 2, 8), ALU.mult, t1, t2)
        t = S.tt(f2, f2, bc(m2, 2, 8), ALU.mult, t)
        t = S.tt(f1, f1, f2, ALU.add, t)
        t = S.cp(Wp[:, :, 0:8], f1, t)
        t = S.tt(f1, f1, Wp[:, :, 0:8], ALU.subtract, t)
        t = S.cp(Wp[:, :, 8:16], f1, t)
        t = S.tt(f1, f1, Wp[:, :, 8:16], ALU.subtract, t)
        t = S.cp(Wp[:, :, 16:24], f1, t)
        Bb = B[:].bitcast(BF16)
        f = None
        for i0 in range(0, n, 8):
            for i in range(8):
                tm = S.tr(Bb[0:24, i * 128:i * 128 + 128], Wp[:, i0 + i, :], self.identb[:], t, self.tIb, f)
            f = S.act(WT[:, i0 * 128:i0 * 128 + 1024], Bb[0:24, :], ACT.Copy, tm)
        self.tWT = [f]
        return WT

    def moe(self, li, bs=range(NB), banks=(0, 1, 2, 3, 4, 5)):
        if li and not self.final:
            self.final = True
        self.moe_load(li)
        self.done = []
        return [self.moe_lane(li, bs, banks)]

    def moe_lane(self, li, bs, banks):
        w = [self.work, 0]
        ar = lambda *s, dt=F32: self.area(w, list(s), dt)
        WT = self.moe_route(li, bs, banks[5], w)
        yield
        S = Stage(self.p, f"moe{li}")
        self.open.append(S)
        xw = [ar(128, 512) for _ in range(2)]
        sg = [ar(128, 512) for _ in range(2)]
        hh = [ar(128, 512) for _ in range(2)]
        ot = ar(128, 512)
        if li:
            og = ar(128, 512)
        BG, BU = banks[0:2], banks[2:4]
        BW, BO = self.bank[banks[4]], self.bank[banks[5]]
        fG = [self.wfree, self.wfree]
        fU = [self.wfree, self.wfree]
        fW = fO = [self.wfree, self.tWT]
        fxw = [None, None]
        fh = [None, None]
        fsg = [None, None]
        tot = None
        steps = []
        E = 8 + li
        units = [list(bs)[i:i + 4] for i in range(0, len(bs), 4)]
        prev = None
        k = 0

        def down(pv):
            nonlocal fO, tot
            e, fc, kk, th, u, un = pv
            first, last = (e == 0 and fc == 0), (e == E - 1 and fc == 1)
            t = S.mm(BO[:], self.wd[:, 2 * e + fc, :], hh[kk % 2], first, last, th, fO if first else None)
            fh[kk % 2] = t
            if last:
                Xu = self.X[:, un[0]:un[0] + 4, :].rearrange("p b t -> p (b t)")
                if not li:
                    fO = S.tt(Xu, Xu, BO[:], ALU.add, t, self.tX)
                    self.done.append(fO)
                else:
                    fO = t2 = S.tt(ot, Xu, BO[:], ALU.add, t, self.tX, tot)
                    for i in range(4):
                        t3 = S.tr(BO[:, i * 128:i * 128 + 128], ot[:, i * 128:i * 128 + 128], self.ident[:], t2, self.tI)
                    tot = t3
                    fO = S.act(og, BO[:], ACT.Copy, t3, self.done[-1] if self.done else None)
                    self.done.append(self.load(self.out[un[0]:un[0] + 4].rearrange("b t d -> t b d"),
                                               og.rearrange("p (b d) -> p b d", b=4), fO, counter=self.cout))
        for u, un in enumerate(units):
            ub = slice(un[0], un[0] + 4)
            Gu = self.G[:, ub, :].rearrange("p b t -> p (b t)")
            for e in range(E):
                if e < 8:
                    t = S.mm(BW[:], self.selw[:, e, :], WT[:, u * 512:u * 512 + 512], True, True, self.tWT, self.tselw, fW)
                    txw = fW = S.tt(xw[e % 2], Gu, BW[:], ALU.mult, t, fxw[e % 2])
                    src = xw[e % 2]
                else:
                    src, txw = Gu, None
                for fc in range(2):
                    i = k % 2
                    G_, U_ = self.bank[BG[i]], self.bank[BU[i]]
                    c = slice(fc * 128, fc * 128 + 128)
                    t1 = S.mm(G_[:], self.wg[:, e, c], Gu, True, True, fG[i], self.tmoe)
                    fG[i] = t1 = S.act(sg[i], G_[:], ACT.Silu, t1, fsg[i], scale=0.5 if li else 1.0)
                    t2 = S.mm(U_[:], self.wu[:, e, c], src, True, True, fU[i], txw)
                    if e < 8:
                        fxw[e % 2] = t2
                    if li:
                        t3 = S.stt(hh[i], U_[:], 0.5, sg[i], ALU.mult, ALU.mult, t1, t2, fh[i])
                    else:
                        t3 = S.tt(hh[i], sg[i], U_[:], ALU.mult, t1, t2, fh[i])
                    fU[i] = fsg[i] = t3
                    if prev:
                        down(prev)
                    prev = (e, fc, k, t3, u, un)
                    k += 1
                    yield
        down(prev)
        yield

    def attn_prep(self, bank=0, waits=None):
        p, I = self.p, self.I
        S = Stage(p, "aprep")
        ca = [self.catt, 0]
        ar = lambda *s, dt=F32: self.area(ca, list(s), dt)
        self.awT = [ar(128, 128) for _ in range(4)]
        self.ab = ar(128, 4)
        self.bvb = ar(128, 128)
        self.bS = ar(128, 16, 128, dt=BF16)
        self.bT = [ar(128, 16, 128, dt=BF16) for _ in range(3)]
        raw = ar(128, 4, 128)
        oh = ar(96, 512)
        ohb = ar(96, 512, dt=BF16)
        rel = ar(96, 16)
        relb = ar(96, 16, dt=BF16)
        bf = ar(128, 16, 32)
        col = lambda n: I[n].rearrange("(p o) -> p o", o=1)
        ld = self.loads([(raw[:, i, :], I["L1_attn_w" + c]) for i, c in enumerate("qkvo")] +
                        [(self.ab[:, 0:1], col("L1_attn_bq")), (self.ab[:, 1:2], col("L1_attn_bk")),
                         (self.ab[:, 3:4], col("L1_attn_bo")), (self.bvb, bc(I["L1_attn_bv"], 0, 128))] +
                         [(oh[32 * i:32 * i + 32], I["onehot"]) for i in range(3)] +
                        [(rel[32 * i:32 * i + 32], I["L1_attn_rel_bias"]) for i in range(3)], self.cattfree, eng="scalar")
        B = self.bank[bank]
        for i in range(4):
            t = S.tr(B[:, i * 128:i * 128 + 128], raw[:, i, :], self.ident[:], ld, self.tI, waits, self.tcond)
        for i in range(4):
            f = S.act(self.awT[i], B[:, i * 128:i * 128 + 128], ACT.Copy, t)
        t0 = S.ts(self.ab[:, 0:1], self.ab[:, 0:1], 8 ** -0.5, None, ALU.mult, None, ld)
        tr_ = ld
        for i in range(3):
            for j in range(i, 3):
                r = slice(32 * j, 32 * j + 32)
                tr_ = S.cp(relb[r], rel[r], tr_)
                if j > i:
                    tr_ = S.tt(rel[r], rel[r], relb[r], ALU.subtract, tr_)
        tr_ = [tr_, S.cp(ohb, oh, ld)]
        tw = [f, t0, ld]
        tb = None
        yield
        for g in range(4):
            for q in range(32):
                o = 256 + 127 - (32 * g + q)
                t = S.mm(B[:, q * 16:q * 16 + 16], ohb[:, o:o + 128], relb, True, True, tr_, f)
            o3 = bf.rearrange("p h q -> p q h")
            t = S.act(o3, B[:].rearrange("p (q h) -> p q h", h=16), ACT.Copy, t, tb)
            f = t
            v = [x[:, :, 32 * g:32 * g + 32] for x in self.bT]
            t = S.cp(v[0], bf, t)
            t = S.tt(bf, bf, v[0], ALU.subtract, t)
            t = S.cp(v[1], bf, t)
            t = S.tt(bf, bf, v[1], ALU.subtract, t)
            tb = S.cp(v[2], bf, t)
            yield
        for g in range(4):
            for k in range(32):
                o = 127 - (32 * g + k)
                t = S.mm(B[:, k * 16:k * 16 + 16], ohb[:, o:o + 128], relb, True, True, f)
            f = S.act(self.bS[:, :, 32 * g:32 * g + 32].rearrange("p h k -> p k h"),
                      B[:].rearrange("p (k h) -> p k h", h=16), ACT.Copy, t)
            yield
        self.taw = tw + [tb, f]
        self.afree = f

    def attn(self, bs=range(NB), workers=2):
        w = [self.work, 0]
        self.scr = [[self.p.nc.dram_tensor(f"scr{k}{i}", [128, 3, 256], BF16, kind="Internal").ap() for i in range(2)]
                    for k in range(workers)]
        units = [list(bs)[i:i + 2] for i in range(0, len(bs), 2)]
        self.done = []
        return [self.attn_worker(k, units[k::workers], w) for k in range(workers)]

    def attn_worker(self, wk, units, w):
        S = Stage(self.p, f"attn{wk}")
        self.open.append(S)
        ar = lambda *s, dt=F32: self.area(w, list(s), dt)
        banks = self.bank[3 * wk:3 * wk + 3]
        oT = ar(128, 256)
        q32 = [ar(128, 256), oT]
        pq, pk = ar(128, 3, 256, dt=BF16), ar(128, 3, 256, dt=BF16)
        parts = [[x[:, i, :] for i in range(3)] for x in (pq, pk)]
        cw = self.p.counter(f's_attnw{wk}')
        Q = ar(51, 16, 256, dt=BF16)
        Kt = ar(51, 16, 256, dt=BF16)
        V = ar(128, 2 * 16, 96)
        nm = ar(128, 2, 16)
        nr = ar(128, 2, 16)
        np_ = ar(128, 2, 48, dt=BF16)
        nT = ar(48, 256, dt=BF16)
        P = [ar(128, 4, 128) for _ in range(2)]
        rc = ar(128, 16)
        o = ar(128, 128)
        cdma = self.p.counter(f"s_attnq{wk}")
        cdma2 = self.p.counter(f"s_attnm{wk}")
        tone = S.memset(Kt[32:51], 1.0, self.wfree, eng="vector")
        tone2 = S.memset(V, 0.0, self.wfree)
        tone2 = S.memset(V[:, :, 8:9], 1.0, tone2)
        f = [[self.afree, self.wfree], self.wfree, self.wfree]
        tQ = tV = tP = tm_ = to = toT = tnm = tpv = td = tdb = None
        fP = [None, None]

        def pv(i, g, k, te):
            def go():
                nonlocal tpv, to
                for h in range(4):
                    hh = 4 * g + h
                    t = S.mm(B2[:, hh * 9:hh * 9 + 96], P[k][:, h, :], V[:, 16 * i + hh, :], hh == 0, True,
                             te, tV, tone2, f[2])
                fP[k] = t
                if g == 3:
                    tpv = t
                    O = B2[:, 0:144].rearrange("p (h d) -> p h d", h=16)
                    t = S.recip(rc, O[:, :, 8], tpv, to)
                    t = S.tt(o.rearrange("p (h d) -> p h d", h=16), O[:, :, 0:8], bc(rc, 2, 8), ALU.mult, t, to)
                    f[2] = t
                    late.append(lambda: transpose(i, t))
            return go

        def transpose(i, t):
            nonlocal to
            to = t1 = S.tr(B2[:, 256:384], o, self.ident[:], t)
            f[2] = S.act(oT[:, i * 128:i * 128 + 128], B2[:, 256:384], ACT.Copy, t1, toT)
        late = []
        B0, B1, B2 = banks
        for _ in range(self.R3 * wk):
            yield
        for un in units:
            ub = slice(un[0], un[0] + 2)
            Gu = self.G[:, ub, :].rearrange("p b t -> p (b t)")
            B0, B1, B2 = banks
            t1 = S.mm(B0[:, 0:256], self.awT[0], Gu, True, True, f[0], self.tG, self.taw)
            t1 = S.mm(B0[:, 256:512], self.awT[1], Gu, True, True)
            t2 = None
            for i, b in enumerate(un):
                t2 = S.mm(B1[:, i * 128:i * 128 + 128], self.G[:, b, :], self.awT[2], True, True, f[1])
            for i in range(2):
                ta = S.act(q32[i], B0[:, 256 * i:256 * i + 256], ACT.Identity, t1, tQ, toT, bias=self.ab[:, i:i + 1],
                           scale=0.5 * (8 ** -0.5 if i == 0 else 1.0))
                pa = parts[i]
                t = S.cp(pa[0], q32[i], ta, td)
                t = S.tt(q32[i], q32[i], pa[0], ALU.subtract, t)
                t = S.cp(pa[1], q32[i], t)
                t = S.tt(q32[i], q32[i], pa[1], ALU.subtract, t)
                tQ = S.cp(pa[2], q32[i], t)
            f[0] = ta
            for i in range(2):
                tV = S.stt(V[:, 16 * i:16 * i + 16, 0:8], B1[:, i * 128:i * 128 + 128].rearrange("p (h d) -> p h d", h=16), 0.5,
                           self.bvb.rearrange("p (h d) -> p h d", h=16), ALU.mult, ALU.add, t2, tpv, tone2, self.taw)
            f[1] = tV
            yield
            sc = self.scr[wk]
            td = self.load(sc[0], pq[:], tQ, tdb, counter=cw)
            td = self.load(sc[1], pk[:], tQ, tdb, counter=cw, eng="sync")
            tdb = []
            for dst, s_, row, lo, hi in ((Kt, 1, 0, 0, 0), (Kt, 1, 1, 0, 0), (Kt, 1, 2, 0, 0), (Kt, 1, 3, 1, 1),
                                         (Kt, 1, 4, 1, 1), (Kt, 1, 5, 2, 2), (Q, 0, 0, 0, 2), (Q, 0, 3, 0, 1), (Q, 0, 5, 0, 0)):
                for q in range(lo, hi + 1):
                    r = row + q - lo
                    src = sc[s_].rearrange("(h d) q t -> q d h t", d=8)[q]
                    tdb = self.load(dst[8 * r:8 * r + 8], src, td, tone, tpv, counter=cdma)
            tk = tdb
            for _ in range(self.R1):
                yield
            n = 0
            for i, b in enumerate(un):
                for g in range(4):
                    Bk = banks[n % 2]
                    S.mm(Bk[:], self.identb[:], self.bS[:, 4 * g:4 * g + 4, :].rearrange("p h k -> p (h k)"), True, False,
                         f[n % 2], self.taw, self.tIb)
                    for h in range(4):
                        t = S.mm(Bk[:, h * 128:h * 128 + 128], Q[0:48, 4 * g + h, i * 128:i * 128 + 128],
                                 Kt[0:48, 4 * g + h, i * 128:i * 128 + 128], False, True, tk)
                    f[n % 2] = tmx = S.red(nm[:, i, 4 * g:4 * g + 4], Bk[:].rearrange("p (h k) -> p h k", h=4), ALU.max, t, tnm)
                    n += 1
                    if n % 2 == 0:
                        yield
            t = S.ts(nm, nm, -1.0, None, ALU.mult, None, tmx)
            t = S.cp(np_[:, :, 0:16], nm, t, tnm)
            t = S.tt(nr, nm, np_[:, :, 0:16], ALU.subtract, t)
            t = S.cp(np_[:, :, 16:32], nr, t)
            t = S.tt(nr, nr, np_[:, :, 16:32], ALU.subtract, t)
            t = S.cp(np_[:, :, 32:48], nr, t)
            for _ in range(self.R5):
                yield
            Bb = B2[:].bitcast(BF16)
            for i in range(2):
                t1 = S.tr(Bb[0:48, i * 128:i * 128 + 128], np_[:, i, :], self.identb[:], t, f[2], self.tIb)
            tnm = t1
            f[2] = t = S.act(nT, Bb[0:48, 0:256], ACT.Copy, t1, tm_)
            for q in range(3):
                tm_ = self.load(Q[48 + q:49 + q, :, :], nT[16 * q:16 * q + 16, :], t, tpv, counter=cdma2)
            for _ in range(self.R2):
                yield
            n = 0
            behind = None
            for i, b in enumerate(un):
                for g in range(4):
                    Bk = banks[n % 2]
                    for k in range(3):
                        S.mm(Bk[:], self.identb[:], self.bT[k][:, 4 * g:4 * g + 4, :].rearrange("p h q -> p (h q)"),
                             k == 0, False, f[n % 2])
                    for h in range(4):
                        t = S.mm(Bk[:, h * 128:h * 128 + 128], Kt[:, 4 * g + h, i * 128:i * 128 + 128],
                                 Q[:, 4 * g + h, i * 128:i * 128 + 128], False, True, tk, tm_)
                    f[n % 2] = te = S.act(P[n % 2].rearrange("p h q -> p (h q)"), Bk[:], ACT.Exp, t, fP[n % 2])
                    if late:
                        late.pop()()
                    if behind:
                        behind()
                    behind = pv(i, g, n % 2, te)
                    n += 1
                    yield
            behind()
            for _ in range(self.R4):
                yield
            late.pop()()
            yield
            toT = t = S.mm(B2[:, 0:256], self.awT[3], oT, True, True, f[2])
            Xu = self.X[:, ub, :].rearrange("p b t -> p (b t)")
            f[2] = S.stt(Xu, B2[:, 0:256], self.ab[:, 3:4], Xu, ALU.add, ALU.add, t, self.tX)
            self.done.append(f[2])
            yield

    def all(self):
        self.load_x()
        self.stages = []
        self.mamba_prep()
        run(self.gru())
        self.wfree = [self.tX, self.tG]

        def go(gens):
            run(*gens)
            e = [s.end() for s in self.open]
            self.open = []
            return e
        e = go(self.mamba())
        self.tX = self.done
        self.wfree = e
        self.tGfree = e
        self.cond2_prep()
        e = go(self.cond2())
        self.tG = self.done
        self.wfree = e
        self.cattfree = e
        e = go(self.moe(0))
        self.tX = self.done
        self.wfree = self.tGfree = self.moefree = e
        run((self.lstm(0), 1), (self.attn_prep(), 1))
        e = go(self.attn())
        self.tX = self.done
        self.wfree = self.tGfree = e
        run(self.lstm(1))
        e = go(self.moe(1))
        fin = Stage(self.p, "fin")
        fin.put("sync", lambda e: e.nop(), self.done)

    def one(self, stage, dbg):
        t1 = self.load(self.X[:], self.I["dX"])
        t2 = self.load(self.G[:], self.I["dG"])
        self.tX, self.tG, self.tGfree = [t1], [t2], [t2]
        if stage == "gru":
            run(self.gru())
        elif stage.startswith("lstm"):
            run(self.lstm(int(stage[-1])))
        elif stage == "mamba":
            self.mamba_prep(); run(*self.mamba()); self.tX = self.done
        elif stage == "cond2":
            self.cond2_prep(); run(*self.cond2()); self.tG = self.done
        elif stage == "moe0":
            run(*self.moe(0)); self.tX = self.done
        elif stage == "attn1":
            run(self.attn_prep()); run(*self.attn()); self.tX = self.done
        elif stage == "moe1":
            run(*self.moe(1)); self.tX = self.tX + self.done
        ts = [self.load(dbg[0], self.X[:], self.tX), self.load(dbg[1], self.G[:], self.tG)]
        fin = Stage(self.p, "fin")
        fin.put("sync", lambda e: e.nop(), ts)


def host_consts():
    import numpy as np
    oh = np.zeros((32, 512), np.float32)
    for j in range(255):
        oh[bucket(j - 127), j] = 1.0
        oh[bucket(j - 127), 256 + 254 - j] = 1.0
    return {"onehot": oh}


def bucket(n):
    import numpy as np
    if n < 16:
        return max(n, 0)
    v = np.log(np.float32(n) / np.float32(16)).astype(np.float32) / np.float32(np.log(128 / 16)) * np.float32(16)
    return min(16 + int(v), 31)


_INS = ['x', 'cond_1024', 'L0_cond_W_z', 'L0_cond_U_z', 'L0_cond_C_z', 'L0_cond_b_z', 'L0_cond_W_r', 'L0_cond_U_r',
        'L0_cond_C_r', 'L0_cond_b_r', 'L0_cond_W', 'L0_cond_U', 'L0_cond_C', 'L0_cond_b', 'L0_attn_W_in',
        'L0_attn_conv_w', 'L0_attn_conv_b', 'L0_attn_dt_bias', 'L0_attn_A_log', 'L0_attn_D', 'L0_attn_init_states',
        'L0_attn_norm_w', 'L0_attn_W_out', 'L0_attn_W_nl', 'L0_attn_b_nl', 'L0_cond2_WQ_w', 'L0_cond2_WQ_b',
        'L0_cond2_WK_w', 'L0_cond2_WK_b', 'L0_cond2_WV_w', 'L0_cond2_WV_b', 'L0_cond2_WO_w', 'L0_cond2_WO_b',
        'L0_ffn_router_kernel_DE', 'L0_ffn_kernel_gating_EDF', 'L0_ffn_kernel_up_EDF', 'L0_ffn_kernel_down_EFD',
        'L1_cond_Wx', 'L1_cond_Wh', 'L1_cond_b', 'L1_attn_wq', 'L1_attn_bq', 'L1_attn_wk', 'L1_attn_bk', 'L1_attn_wv',
        'L1_attn_bv', 'L1_attn_wo', 'L1_attn_bo', 'L1_attn_rel_bias', 'L1_cond2_Wx', 'L1_cond2_Wh', 'L1_cond2_b',
        'L1_ffn_sw1', 'L1_ffn_sw2', 'L1_ffn_sw3', 'L1_ffn_ew1', 'L1_ffn_ew2', 'L1_ffn_ew3', 'L1_ffn_rw', 'L1_ffn_rb']


def kernel(**inputs):
    import numpy as _np
    import concourse.bacc as _bacc
    from concourse import mybir as _mybir
    from concourse.bass_utils import run_bass_kernel_spmd as _run

    nc = _bacc.Bacc("TRN2", target_bir_lowering=False, num_devices=1)
    arrays, args = {}, {}
    data = {name: inputs[name] for name in _INS}
    data.update(host_consts())
    for name, v in data.items():
        a = _np.ascontiguousarray(v)
        arrays[f"in_{name}"] = a
        args[name] = nc.dram_tensor(f"in_{name}", a.shape, _mybir.dt.from_np(a.dtype), kind="ExternalInput").ap()
    out = nc.dram_tensor("out_0", (NB, T, D), F32, kind="ExternalOutput").ap()
    program(nc, args, out)
    r = _run(nc, [arrays], core_ids=[0])
    return r.results[0]["out_0"]
```

```python
import concourse.bass as bass
from concourse import mybir
from contextlib import ExitStack

F32 = mybir.dt.float32
F32R = mybir.dt.float32r
BF16 = mybir.dt.bfloat16
ALU = mybir.AluOpType
ACT = mybir.ActivationFunctionType
AX = mybir.AxisListType


class Tok:

    def __init__(self, sem, step):
        self.sem, self.step, self.used, self.value = sem, step, False, None


class Counter:

    def __init__(self, prog, name):
        self.h = prog.ctx.enter_context(prog.nc.semaphore(name))
        self.count = 0


class Prog:

    ENG = ("tensor", "scalar", "vector", "gpsimd", "sync")

    def __init__(self, nc, ctx):
        self.nc, self.ctx = nc, ctx
        self.q = {e: [] for e in self.ENG}

    def sb(self, name, shape, dt=F32):
        return self.ctx.enter_context(self.nc.sbuf_tensor(name, shape, dt))

    def bank(self, name):
        return self.ctx.enter_context(self.nc.psum_tensor(name, [128, 512], F32))

    def counter(self, name):
        return Counter(self, name)

    def put(self, eng, counter, fn, waits, step=1):
        tok = Tok(counter, step)
        flat = []

        def take(w):
            if isinstance(w, (list, tuple)):
                for x in w:
                    take(x)
            elif w is not None:
                w.used = True
                flat.append(w)
        take(waits)
        if step == 16:
            tok.used = True
        self.q[eng].append((fn, flat, tok))
        return tok

    def emit(self):
        for e in self.ENG:
            for fn, waits, tok in self.q[e]:
                if tok.used:
                    tok.sem.count += tok.step
                    tok.value = tok.sem.count
        block = self.ctx.enter_context(self.nc.Block())
        for e in self.ENG:
            def body(eng, e=e):
                seen = {}
                for fn, waits, tok in self.q[e]:
                    need = {}
                    for w in waits:
                        if w.value > need.get(w.sem, 0):
                            need[w.sem] = w.value
                    for s, v in need.items():
                        if v > seen.get(s, 0):
                            eng.wait_ge(s.h, v)
                            seen[s] = v
                    ins = fn(eng)
                    if tok.used:
                        ins.then_inc(tok.sem.h, tok.step)
            blocks = {"tensor": block.tensor, "scalar": block.scalar, "vector": block.vector,
                            "gpsimd": block.gpsimd, "sync": block.sync}
            blocks[e](body)


class Stage:

    def __init__(self, p, name):
        self.p, self.name, self.c, self.latest = p, name, {}, {}

    def put(self, eng, fn, waits):
        if eng not in self.c:
            self.c[eng] = self.p.counter(f"s_{self.name}_{eng}")
        t = self.latest[eng] = self.p.put(eng, self.c[eng], fn, waits)
        return t

    def end(self):
        return list(self.latest.values())

    def mm(self, out, lhsT, rhs, start, stop, *waits):
        return self.put("tensor", lambda e: e.matmul(out, lhsT, rhs, start=start, stop=stop, skip_group_check=True), waits)

    def tr(self, out, in_, ident, *waits):
        return self.put("tensor", lambda e: e.transpose(out, in_, ident), waits)

    def act(self, out, in_, func, *waits, bias=0.0, scale=1.0):
        return self.put("scalar", lambda e: e.activation(out, in_, func, bias=bias, scale=scale), waits)

    def actsum(self, out, in_, func, total, *waits):
        return self.put("scalar", lambda e: e.activation(out, in_, func, accum_out=total), waits)

    def tt(self, out, a, b, op, *waits, eng="vector"):
        return self.put(eng, lambda e: e.tensor_tensor(out, a, b, op), waits)

    def ts(self, out, a, s1, s2, op0, op1, *waits, eng="vector"):
        if op1 is None:
            return self.put(eng, lambda e: e.tensor_scalar(out, a, s1, None, op0), waits)
        return self.put(eng, lambda e: e.tensor_scalar(out, a, s1, s2, op0, op1), waits)

    def stt(self, out, a, s, b, op0, op1, *waits):
        return self.put("vector", lambda e: e.scalar_tensor_tensor(out=out, in0=a, scalar=s, in1=b, op0=op0, op1=op1), waits)

    def cp(self, out, a, *waits, eng="vector"):
        return self.put(eng, lambda e: e.tensor_copy(out, a), waits)

    def red(self, out, a, op, *waits):
        return self.put("vector", lambda e: e.tensor_reduce(out, a, axis=AX.X, op=op), waits)

    def recip(self, out, a, *waits):
        return self.put("vector", lambda e: e.reciprocal(out, a), waits)

    def memset(self, out, v, *waits, eng="gpsimd"):
        return self.put(eng, lambda e: e.memset(out, v), waits)

    def sel(self, out, in_, op, fill, base, pattern, cm, *waits):
        return self.put("gpsimd", lambda e: e.affine_select(out=out, in_=in_, compare_op=op, fill=fill, base=base,
                                                            pattern=pattern, channel_multiplier=cm), waits)


def run(*lanes):
    lanes = [list(x) if isinstance(x, tuple) else [x, 1] for x in lanes]
    while lanes:
        for l in list(lanes):
            for _ in range(l[1]):
                try:
                    next(l[0])
                except StopIteration:
                    lanes.remove(l)
                    break

NB, T, D = 32, 128, 128
N = NB * T


def bc(ap, axis, n):
    a = ap.unsqueeze(axis)
    shape = list(a.shape)
    shape[axis] = n
    return a.broadcast_to(shape)


def program(nc, I, out, only=None, dbg=None):
    ctx = ExitStack()
    with ctx:
        p = Prog(nc, ctx)
        K = Kernel(p, I, out)
        K.consts()
        if only is None:
            K.all()
        else:
            K.one(only, dbg)
        p.emit()


class Kernel:
    def __init__(self, p, I, out):
        self.p, self.I, self.out = p, I, out
        sb = p.sb
        self.X = sb("X", [128, NB, T])
        self.G = sb("G", [128, NB, T])
        self.bank = [p.bank(f"B{i}") for i in range(8)]
        self.tX = None
        self.tG = None
        self.ndma = 0
        self.lt = None
        self.rev = None
        self.h3 = None
        self.open = []
        self.moefree = None
        self.cattfree = None
        self.wr = [[sb(f"wr{i}{j}", [128, 768], F32R) for j in range(2)] for i in range(2)]
        self.gr = [[sb(f"gr{i}{j}", [128, 512], F32R) for j in range(2)] for i in range(2)]
        self.hr = [[sb(f"hr{i}{j}", [128, 512], F32R) for j in range(2)] for i in range(4)]
        self.cout = p.counter('s_out')
        self.tGfree = None
        self.work = sb("work", [128, 74 * 256])
        self.catt = sb("catt", [128, 36 * 256])
        self.wfree = []
        self.NT = 5
        self.CY = 4
        self.WY = 2
        self.VC = (3, 7)
        self.LD = 2
        self.R1, self.R2, self.R3, self.R4, self.R5 = 7, 3, 14, 1, 1
        self.lag2 = 1

    def area(self, base, shape, dt=F32):
        n = 1
        for s in shape[1:]:
            n *= s
        words = n if dt == F32 else (n + 1) // 2
        t, at = base
        assert at + words <= t.shape[1], (at, words, t.shape)
        base[1] = at + words
        v = t[0:shape[0], at:at + words]
        if dt != F32:
            v = v.bitcast(dt)
        if len(shape) == 3:
            v = v.rearrange("p (a b) -> p a b", b=shape[2])
        elif len(shape) == 4:
            v = v.rearrange("p (a b c) -> p a b c", b=shape[2], c=shape[3])
        return v

    def mm3(self, S, out, a, b, start, stop, *waits):
        S.mm(out, a[0], b[0], start, False, *waits)
        S.mm(out, a[0], b[1], False, False)
        return S.mm(out, a[1], b[0], False, stop)

    def load(self, dst, src, *waits, eng="sync", counter=None):
        if counter is None:
            self.ndma += 1
            counter = self.p.counter(f"s_ld{self.ndma}")
        return self.p.put(eng, counter, lambda e: e.dma_start(dst, src), waits, 16)

    def loads(self, pairs, *waits, eng="sync"):
        self.ndma += 1
        c = self.p.counter(f"s_ld{self.ndma}")
        for d, s in pairs:
            t = self.load(d, s, *waits, eng=eng, counter=c)
        return t

    def consts(self):
        p, I = self.p, self.I
        S = self.S0 = Stage(p, "const")
        sb = p.sb
        self.ident = sb("ident", [128, 128])
        self.identb = sb("identb", [128, 128], BF16)
        t = S.memset(self.ident[:], 0.0)
        self.tI = S.sel(self.ident[:], self.ident[:], ALU.not_equal, 1.0, 0, [[-1, 128]], 1, t)
        self.tIb = S.cp(self.identb[:], self.ident[:], self.tI, eng="gpsimd")
        self.tri = sb("tri", [128, 128])
        self.triq = sb("triq", [128, 128])
        self.low = sb("low", [128, 128])
        self.ones = sb("ones", [128, 128])
        t1 = S.memset(self.ones[:], 1.0)
        t = S.sel(self.tri[:], self.ones[:], ALU.is_ge, 0.0, 0, [[1, 128]], -1, t1)
        t2 = S.sel(self.low[:], self.ones[:], ALU.is_gt, 0.0, 0, [[-1, 128]], 1, t1)
        t3 = S.ts(self.triq[:], self.tri[:], 0.25, None, ALU.mult, None, t, eng="gpsimd")
        self.tTri = t3
        self.cond = sb("condt", [32, 128])
        self.condT = sb("condT", [128, 32])
        self.condT2 = sb("condT2", [128, 32])
        tl = self.load(self.cond[:], I["cond_1024"])
        B = self.bank[0]
        t = S.tr(B[:, 0:32], self.cond[:], self.ident[0:32, 0:32], tl, self.tI)
        self.tcond = S.act(self.condT[:], B[:, 0:32], ACT.Copy, t)
        self.tcond2 = S.act(self.condT2[:], B[:, 0:32], ACT.Copy, t, scale=2.0)
        self.tcond = self.tcond2
        self.gw = sb("gw", [128, 9, 128])
        self.gb = sb("gb", [128, 3])
        ws = ["L0_cond_W_z", "L0_cond_W_r", "L0_cond_W", "L0_cond_U_z", "L0_cond_U_r", "L0_cond_U",
              "L0_cond_C_z", "L0_cond_C_r", "L0_cond_C"]
        self.lgw = self.loads([(self.gw[:, i, :], I[n]) for i, n in enumerate(ws)] +
                              [(self.gb[:, i:i + 1], I[n].rearrange("(p o) -> p o", o=1))
                               for i, n in enumerate(["L0_cond_b_z", "L0_cond_b_r", "L0_cond_b"])])

    def load_x(self):
        S, I = self.S0, self.I
        w = [self.work, 0]
        xt = self.area(w, [128, NB, D])
        tok = []
        for u in range(4):
            tok.append(self.load(xt[:, u * 8:u * 8 + 8, :], I["x"][u * 8:u * 8 + 8].rearrange("b t d -> t b d"),
                                 eng="sync" if u % 2 else "scalar"))
        cur = {}
        for u in range(8):
            B = self.bank[2 + u % 4]
            for j in range(4):
                t = S.tr(B[:, j * 128:(j + 1) * 128], xt[:, 4 * u + j, :], self.ident[:], tok[u // 2], self.tI, cur.get(u % 4))
            dst = self.X[:, 4 * u:4 * u + 4, :].rearrange("p b t -> p (b t)")
            if u % 2:
                cur[u % 4] = S.cp(dst, B[:], t)
            else:
                cur[u % 4] = S.act(dst, B[:], ACT.Copy, t)
        self.tX = list(cur.values())
        self.wfree = self.tX

    def gru(self, banks=(6, 7), zbanks=(4, 5)):
        p, I = self.p, self.I
        S = Stage(p, "gru")
        gw, gb = self.gw, self.gb
        V = p.sb("gV", [128, 3, 32])
        tw = []
        for i in (0, 1, 3, 4, 5, 6, 7):
            tw.append(S.ts(gw[:, i, :], gw[:, i, :], 0.5, None, ALU.mult, None, self.lgw))
        tw = [tw[-1], S.ts(gb[:, 0:2], gb[:, 0:2], 0.5, None, ALU.mult, None, self.lgw)]
        B = self.bank[banks[0]]
        for g in range(3):
            t = S.mm(B[:, g * 32:g * 32 + 32], gw[:, 6 + g, :], self.condT[:], True, True, tw, self.tcond)
        for g in range(3):
            tV = S.act(V[:, g, :], B[:, g * 32:g * 32 + 32], ACT.Identity, t, bias=gb[:, g:g + 1])
        h = [p.sb(f"gh{i}", [128, 32]) for i in range(2)]
        th = p.sb("gth", [128, 2, 32])
        hh = p.sb("ghh", [128, 32])
        rh = p.sb("grh", [128, 32])
        zz = p.sb("gz", [128, 32])
        aa = p.sb("ga", [128, 32])
        zh = p.sb("gzh", [128, 32])
        th_ = S.memset(h[1][:], 0.0, eng="vector")
        free = [[tV, self.wfree], self.wfree]

        def pre(q):
            BR, BZ = self.bank[banks[q % 2]], self.bank[zbanks[q % 2]]
            R3 = BR[:, 0:256].rearrange("p (s g b) -> p s g b", s=4, g=2)
            Z3 = BZ[:, 0:128].rearrange("p (s b) -> p s b", s=4)
            xq = self.X[:, :, 4 * q:4 * q + 4].rearrange("p b s -> p s b")
            S.mm(BR[:, 0:256].rearrange("p (s c) -> p s c", s=4), self.ident[:],
                 bc(V[:, 1:3, :].rearrange("p g b -> p (g b)"), 1, 4), True, False, tV, self.tI, free[q % 2])
            S.mm(Z3, self.ident[:], bc(V[:, 0, :], 1, 4), True, False)
            yield
            for out, g in ((R3[:, :, 0, :], 1), (R3[:, :, 1, :], 2), (Z3, 0)):
                S.mm(out, gw[:, g, :], xq, False, False, tw, self.tX)
                if g:
                    yield
            yield
        for _ in pre(0):
            pass
        thm = th_
        tz0 = tz_ = tcopy = tzh = None
        gcopy = [None, None]
        for t in range(T):
            if t % 4 == 0 and t + 4 < T:
                ahead = pre(t // 4 + 1)
            q = (t // 4) % 2
            B, BZ = self.bank[banks[q]], self.bank[zbanks[q]]
            o, oz = (t % 4) * 64, (t % 4) * 32
            hp, hn = h[(t + 1) % 2][:], h[t % 2][:]
            m = self.mmh(S, B, o, gw[:, 4, :], hp, thm)
            mz = self.mmh(S, BZ, oz, gw[:, 3, :], hp)
            a1 = S.act(th[:, 1, :], B[:, o:o + 32], ACT.Tanh, m, thm)
            a0 = S.act(th[:, 0, :], BZ[:, oz:oz + 32], ACT.Tanh, mz, thm)
            trh = S.stt(rh[:], th[:, 1, :], 1.0, hp, ALU.add, ALU.mult, a1, thm)
            m = self.mmh(S, B, o + 32, gw[:, 5, :], rh[:], trh)
            if t + 4 < T or t % 4:
                next(ahead, None)
            a2 = S.act(hh[:], B[:, o + 32:o + 64], ACT.Tanh, m, tzh)
            tz_ = S.ts(zz[:], th[:, 0, :], 0.5, 0.5, ALU.mult, ALU.add, a0)
            t1 = S.tt(aa[:], zz[:], hp, ALU.mult, tz_)
            t1 = S.tt(aa[:], hp, aa[:], ALU.subtract, t1)
            tzh = S.tt(zh[:], zz[:], hh[:], ALU.mult, a2)
            thm = S.tt(hn, zh[:], aa[:], ALU.add, tzh, t1, gcopy[t % 2])
            free[q] = a2
            gcopy[t % 2] = S.cp(self.G[:, :, t], hn, thm, self.tGfree, eng="gpsimd")
            yield
        self.tG = gcopy

    def lstm(self, li, banks=(6, 7), obanks=(4, 5)):
        p, I = self.p, self.I
        S = Stage(p, f"lstm{li}")
        pre_ = "L1_cond" if li == 0 else "L1_cond2"
        if self.lt is None:
            self.lt = dict(lw=p.sb("lw", [128, 8, 128]), b3=p.sb("lb3", [128, 128], BF16), b4=p.sb("lb4", [4, 128]),
                           r4=p.sb("lr4", [4, 128]), q4=p.sb("lq4", [4, 128], BF16),
                           ind=p.sb("lind", [128, 4, 4, 32], BF16), H=[p.sb(f"lH{i}", [128, 32]) for i in range(2)],
                           Dc=p.sb("lD", [128, 32]), th=p.sb("lth", [128, 4, 32]), tc=p.sb("ltc", [128, 32]),
                           pp=p.sb("lp", [128, 32]), qq=p.sb("lq", [128, 32]))
            self.lfree = None
        lt, lfree = self.lt, self.lfree
        lw, b3, b4, r4, q4, ind, H = lt["lw"], lt["b3"], lt["b4"], lt["r4"], lt["q4"], lt["ind"], lt["H"]
        Dc, th, tc, pp, qq = lt["Dc"], lt["th"], lt["tc"], lt["pp"], lt["qq"]
        ld = self.loads([(lw[:, 0:4, :], I[pre_ + "_Wx"].rearrange("k (g e) -> k g e", g=4)),
                         (lw[:, 4:8, :], I[pre_ + "_Wh"].rearrange("k (g e) -> k g e", g=4)),
                         (b4[:, :], I[pre_ + "_b"].rearrange("(g e) -> g e", g=4))], lfree)
        tw = [S.ts(lw[:, 0:3, :], lw[:, 0:3, :], 0.5, None, ALU.mult, None, ld, eng="gpsimd"),
              S.ts(lw[:, 4:7, :], lw[:, 4:7, :], 0.25, None, ALU.mult, None, ld, eng="gpsimd"),
              S.ts(lw[:, 7, :], lw[:, 7, :], 0.5, None, ALU.mult, None, ld, eng="gpsimd")]
        t = S.ts(b4[:], b4[:], self.half3(S), None, ALU.mult, None, ld, self.thalf)
        z = S.memset(b3[:], 0.0, lfree)
        t1 = S.cp(b3[0:4, :], b4[:], t, z)
        t2 = S.tt(r4[:], b4[:], b3[0:4, :], ALU.subtract, t1)
        t3 = S.cp(b3[32:36, :], r4[:], t2)
        t4 = S.cp(q4[:], r4[:], t2)
        t5 = S.tt(r4[:], r4[:], q4[:], ALU.subtract, t4, t3)
        t6 = S.cp(b3[64:68, :], r4[:], t5)
        z = S.memset(ind[:], 0.0, lfree)
        for base in (0, 32, 64):
            v = ind[base:base + 4]
            z = S.sel(v, v, ALU.not_equal, 1.0, 0, [[0, 4], [-1, 4], [0, 32]], 1, z)
        tb = [t3, t6, z]
        tD = S.memset(Dc[:], 0.0, z)
        free = [self.wfree, self.wfree]

        def pre(q):
            BF, BO = self.bank[banks[q % 2]], self.bank[obanks[q % 2]]
            F3 = BF[:, 0:256].rearrange("p (s g b) -> p s g b", s=4, g=2)
            O3 = BO[:, 0:256].rearrange("p (s g b) -> p s g b", s=4, g=2)
            xq = self.X[:, :, 4 * q:4 * q + 4].rearrange("p b s -> p s b")
            S.mm(F3, b3[0:68, :], ind[0:68, :, 0:4:3, :], True, False, tb, free[q % 2])
            S.mm(O3, b3[0:68, :], ind[0:68, :, 1:3, :], True, False)
            for out, g in ((F3[:, :, 0, :], 0), (F3[:, :, 1, :], 3), (O3[:, :, 0, :], 1), (O3[:, :, 1, :], 2)):
                S.mm(out, lw[:, g, :], xq, False, False, tw, self.tX)
                yield
        yield
        for _ in pre(0):
            pass
        thm = S.cp(H[1][:], self.condT2[:], lfree, self.tcond2)
        ttc = None
        gcopy = [None, None]
        for t in range(T):
            if t % 4 == 0 and t + 4 < T:
                ahead = pre(t // 4 + 1)
            q = (t // 4) % 2
            B, BO = self.bank[banks[q]], self.bank[obanks[q]]
            o = (t % 4) * 64
            hp, hn = H[(t + 1) % 2][:], H[t % 2][:]
            mf = self.mmh(S, BO, o, lw[:, 5, :], hp, thm)
            for i, g in enumerate((0, 3)):
                m = self.mmh(S, B, o + 32 * i, lw[:, 4 + g, :], hp)
            af = S.act(th[:, 2, :], BO[:, o:o + 32], ACT.Tanh, mf, thm)
            mo = self.mmh(S, BO, o + 32, lw[:, 6, :], hp, af)
            if t + 4 < T or t % 4:
                next(ahead, None)
            a1 = S.act(th[:, 0:2, :].rearrange("p g b -> p (g b)"), B[:, o:o + 64], ACT.Tanh, m, thm)
            ao = S.act(th[:, 3, :], BO[:, o + 32:o + 64], ACT.Tanh, mo, thm)
            t2 = S.stt(qq[:], th[:, 2, :], 1.0, Dc[:], ALU.add, ALU.mult, tD, af)
            t1 = S.stt(pp[:], th[:, 0, :], 1.0, th[:, 1, :], ALU.add, ALU.mult, a1)
            tD = S.stt(Dc[:], qq[:], 0.5, pp[:], ALU.mult, ALU.add, t1, t2, ttc)
            ttc = S.act(tc[:], Dc[:], ACT.Tanh, tD, thm, scale=0.5)
            thm = S.stt(hn, th[:, 3, :], 1.0, tc[:], ALU.add, ALU.mult, ttc, ao, gcopy[t % 2])
            free[q] = [a1, ao]
            gcopy[t % 2] = S.cp(self.G[:, :, t], hn, thm, self.tGfree, eng="gpsimd")
            yield
        self.tG = gcopy
        self.lfree = S.end()

    def mmh(self, S, B, o, w, h, *waits):
        for j in range(0, 128, 32):
            t = S.mm(B[j:j + 32, o:o + 32], w[:, j:j + 32], h, False, True, *waits)
        return t

    def half3(self, S):
        if self.h3 is None:
            self.h3 = self.p.sb("h3", [4, 1])
            t = self.S0.memset(self.h3[:], 0.5)
            self.thalf = self.S0.sel(self.h3[:], self.h3[:], ALU.not_equal, 1.0, -3, [[0, 1]], 1, t)
        return self.h3[:]

    def mamba_prep(self):
        p, I = self.p, self.I
        sb = p.sb
        S = Stage(p, "mprep")
        self.win = sb("win", [128, 648])
        self.wout = sb("wout", [128, 2, 128])
        self.wnl = sb("wnl", [128, 128])
        self.bnl = sb("bnl", [128, 1])
        self.nw = sb("nw", [128, 2])
        self.cw = sb("cw", [128, 3, 16])
        self.cb = sb("cb", [128, 3])
        self.dtb = sb("dtb", [128, 8])
        self.alog = sb("alog", [128, 8])
        self.dcol = sb("dcol", [128, 2])
        self.dg = sb("dg", [128, 2, 128])
        self.h0 = sb("h0", [128, 2, 64])
        self.h0T = sb("h0T", [64, 256])
        pairs = [(self.win[:], I["L0_attn_W_in"]),
                 (self.wout[:], I["L0_attn_W_out"].rearrange("(c p) n -> p c n", p=128)),
                 (self.wnl[:], I["L0_attn_W_nl"]),
                 (self.bnl[:], I["L0_attn_b_nl"].rearrange("(p o) -> p o", o=1)),
                 (self.cw[:], I["L0_attn_conv_w"].rearrange("(c p) k -> p c k", p=128)),
                 (self.dtb[:], bc(I["L0_attn_dt_bias"], 0, 128)),
                 (self.alog[:], bc(I["L0_attn_A_log"], 0, 128)),
                 (self.h0[:], I["L0_attn_init_states"].rearrange("(c h) q n -> (h q) c n", c=2))]
        for c in range(2):
            pairs.append((self.nw[:, c:c + 1], I["L0_attn_norm_w"][c * 128:c * 128 + 128].rearrange("(p o) -> p o", o=1)))
            for j in range(4):
                pairs.append((self.dcol[32 * j:32 * j + 32, c:c + 1],
                              bc(I["L0_attn_D"][4 * c + j:4 * c + j + 1], 0, 32)))
        for c in range(3):
            pairs.append((self.cb[:, c:c + 1], I["L0_attn_conv_b"][c * 128:c * 128 + 128].rearrange("(p o) -> p o", o=1)))
        ld = self.loads(pairs)
        for _ in range(8):
            yield
        for c in range(2):
            t = S.ts(self.wout[:, c, :], self.wout[:, c, :], self.nw[:, c:c + 1], None, ALU.mult, None, ld)
        t = S.ts(self.dcol[:], self.dcol[:], 0.5, None, ALU.mult, None, ld)
        for c in range(2):
            t = S.ts(self.dg[:, c, :], self.ident[:], self.dcol[:, c:c + 1], None, ALU.mult, None, t, self.tI)
        self.tap = self.area([self.work, 74 * 256 - 3 * self.NT * 128], [128, 3 * self.NT, 128])
        for c in range(3):
            for k in range(self.NT):
                tg = S.ts(self.tap[:, c * self.NT + k, :], self.ident[:], self.cw[:, c, k:k + 1], None, ALU.mult, None,
                          ld, self.tI)
                if k % 2:
                    yield
        t = [t, tg]
        B = self.bank[1]
        for c in range(2):
            tm = S.tr(B[0:64, c * 128:c * 128 + 128], self.h0[:, c, :], self.ident[:], ld, self.tI)
        t2 = S.act(self.h0T[:], B[0:64, 0:256], ACT.Copy, tm, scale=0.5)
        t3 = S.act(self.alog[:], self.alog[:], ACT.Exp, ld)
        t4 = S.ts(self.alog[:], self.alog[:], -1.0, None, ALU.mult, None, t3)
        self.tmw = [t, t2, t4, ld]
        self.tb1 = t2

    def mamba_dt(self, bs=range(NB)):
        p = self.p
        S = Stage(p, "mdt")
        n0, n = bs[0], len(bs)
        c = [self.catt, 6144]
        self.adt, self.dth, self.ec, self.q1, self.q2, self.q3 = (self.area(c, [128, NB, 8]) for _ in range(6))
        B = self.bank[0]
        s = slice(n0, n0 + n)
        P = B[:, 0:8 * n].rearrange("p (b h) -> p b h", h=8)
        for i, b in enumerate(bs):
            tm = S.mm(P[:, i, :], self.G[:, b, :], self.win[:, 640:648], True, True, self.tG, self.tmw)
        x, e, z, q = self.dth[:, s, :], self.q1[:, s, :], self.q2[:, s, :], self.q3[:, s, :]
        t = S.tt(x, P, bc(self.dtb[:], 1, n), ALU.add, tm)
        t = S.stt(e, x, -1.0, x, ALU.mult, ALU.min, t)
        t = S.act(e, e, ACT.Exp, t)
        yield
        t = S.ts(z, e, 2.0, None, ALU.add, None, t)
        t = S.recip(z, z, t)
        yield
        t = S.tt(z, z, e, ALU.mult, t)
        t = S.tt(e, z, z, ALU.mult, t)
        t = S.ts(q, e, 1 / 19, 1 / 17, ALU.mult, ALU.add, t)
        for k in (15, 13, 11, 9, 7, 5, 3, 1):
            t = S.tt(q, q, e, ALU.mult, t)
            t = S.ts(q, q, 1.0 / k, None, ALU.add, None, t)
            yield
        t = S.tt(q, q, z, ALU.mult, t)
        t = S.ts(x, x, 0.0, 0.5, ALU.max, ALU.mult, t)
        t = S.tt(x, x, q, ALU.add, t)
        a = self.adt[:, s, :]
        yield
        t = S.tt(a, x, bc(self.alog[:], 1, n), ALU.mult, t)
        t = S.ts(a, a, 2.0, None, ALU.mult, None, t)
        P2 = B[:, 256:256 + 8 * n].rearrange("p (b h) -> p b h", h=8)
        yield
        tm = S.mm(P2, self.tri[:], a, True, True, t, self.tTri)
        t2 = S.act(self.ec[:, s, :], P2, ACT.Exp, tm)
        self.tdt = [t, t2]

    def mamba(self, bs=range(NB), workers=2):
        self.tdt = None
        w = [self.work, 0]
        units = [list(bs)[i:i + 4] for i in range(0, len(bs), 4)]
        self.cvb = [self.area(w, [128, 3, 512]) for _ in range(3)]
        self.c0b = [self.area(w, [128, 512]) for _ in range(3)]
        self.cvready, self.cvfree = {}, {}
        gens = [self.mamba_conv(units, w), (self.mamba_dt(bs), 2)]
        gens += [self.mamba_worker(k, units, w) for k in range(workers)]
        self.done = []
        return gens

    def mamba_conv(self, units, w):
        S = Stage(self.p, "mconv")
        self.open.append(S)
        ar = lambda *s, dt=F32: self.area(w, list(s), dt)
        XP = [ar(128, 4, 144) for _ in range(3)]
        th = [ar(128, 512) for _ in range(2)]
        NT = self.NT
        BI, BT = self.bank[6], self.bank[7]
        fI = fT = self.wfree
        fX = [S.memset(x[:, :, 0:16], 0.0, self.wfree) for x in XP]
        fth = [None, None]
        n = 0
        pend = None
        for u, un in enumerate(units):
            while u >= 3 and u - 3 not in self.cvfree:
                yield
            Gu = self.G[:, un[0]:un[0] + 4, :].rearrange("p b t -> p (b t)")
            cv, C0 = self.cvb[u % 3], self.c0b[u % 3]
            fcv = self.cvfree.get(u - 3, self.wfree)
            tks = []
            for c in range(3):
                X, th_ = XP[n % 3], th[n % 2]
                t = S.mm(BI[:], self.win[:, 256 + c * 128:384 + c * 128], Gu, True, True, fI, self.tG, self.tmw)
                fI = tx = S.act(X[:, :, 16:144], BI[:].rearrange("p (b t) -> p b t", b=4), ACT.Copy, t, fX[n % 3])
                yield
                for k in range(NT):
                    t = S.mm(BT[:], self.tap[:, c * NT + k, :], X[:, :, 1 + k:129 + k], k == 0, k == NT - 1, tx, fT)
                acc = cv[:, c, :].rearrange("p (b t) -> p b t", b=4)
                fT = t = S.act(cv[:, c, :], BT[:], ACT.Identity, t, fcv, bias=self.cb[:, c:c + 1])
                if pend:
                    pend()
                yield
                th2 = [t, t]
                for k in range(NT, 16):
                    for i in range(2):
                        b2 = slice(2 * i, 2 * i + 2)
                        th2[i] = S.stt(acc[:, b2, :], X[:, b2, 1 + k:129 + k], self.cw[:, c, k:k + 1], acc[:, b2, :],
                                       ALU.mult, ALU.add, th2[i])
                    if (k - NT) % self.CY == self.CY - 1:
                        yield
                t = th2
                fX[n % 3] = t

                def silu(t=t, c=c, th_=th_, n=n, cv=cv, C0=C0, u=u, tks=tks, fcv=fcv):
                    ta = S.act(th_, cv[:, c, :], ACT.Tanh, t, fth[n % 2], scale=0.5)
                    if c < 2:
                        t1 = S.stt(cv[:, c, :], th_, 1.0, cv[:, c, :], ALU.add, ALU.mult, ta)
                    else:
                        t1 = S.stt(C0[0:64, :], th_[64:128, :], 1.0, cv[64:128, c, :], ALU.add, ALU.mult, ta, fcv)
                        t1 = S.stt(cv[0:64, c, :], th_[0:64, :], 1.0, cv[0:64, c, :], ALU.add, ALU.mult, ta)
                    fth[n % 2] = t1
                    tks.append(t1)
                    if c == 2:
                        self.cvready[u] = tks
                pend = silu
                n += 1
            if u + 1 == len(units):
                pend()
            yield

    def mamba_worker(self, wk, units, w):
        p = self.p
        S = Stage(p, f"mamba{wk}")
        self.open.append(S)
        ar = lambda *s, dt=F32: self.area(w, list(s), dt)
        B0, B1, B2 = self.bank[3 * wk:3 * wk + 3]
        wc = [self.catt, wk * 3072]
        E = [self.area(wc, [128, 8, 128]) for _ in range(2)]
        zt = [self.area(wc, [128, 256]) for _ in range(2)]
        xdt = ar(128, 256)
        cbm = ar(128, 128)
        y4 = ar(128, 4, 256)
        sq = ar(128, 256)
        ss = ar(128, 4)
        yT = ar(128, 2, 512)
        tm1 = ar(128, 512)
        while self.tdt is None:
            yield
        fb = [[self.tdt, self.wfree], [self.tb1, self.wfree], self.wfree]
        tE = tY = None
        tyT = ttm = trs = t_yT = tss = None
        fE, fz = [None, None], [None, None]
        seq = [b for u in range(wk, len(units), 2) for b in units[u]]
        ahead = {}

        def decay(n):
            b, k = seq[n], n % 2
            e, z = E[k], zt[k]
            ef = e.rearrange("p h t -> p (h t)")
            t = S.tt(e, bc(self.tri[:], 1, 8), bc(self.adt[:, b, :], 2, 128), ALU.mult, self.tdt, fE[k], eng="gpsimd")
            yield
            t1 = S.mm(B1[:], self.low[:], ef[:, 0:512], True, True, t, fb[1])
            t2 = S.mm(B2[:], self.low[:], ef[:, 512:1024], True, True, fb[2])
            e1 = S.act(ef[:, 0:512], B1[:], ACT.Exp, t1)
            e2 = S.act(ef[:, 512:1024], B2[:], ACT.Exp, t2)
            fb[1], fb[2] = e1, e2
            yield
            t = S.mm(B1[:, 0:256], self.G[:, b, :], self.win[:, 0:256], True, True, fb[1])
            t = S.act(z, B1[:, 0:256], ACT.Tanh, t, fz[k], scale=0.5)
            fb[1] = tz = S.stt(z, z, 1.0, B1[:, 0:256], ALU.add, ALU.mult, t)
            ahead[n] = [e1, e2, tz]
            yield
        for _ in decay(0):
            yield
        n = -1
        for u in range(wk, len(units), 2):
            un = units[u]
            while u not in self.cvready:
                yield
            tth = [self.cvready[u], self.wfree]
            cv, C0 = self.cvb[u % 3], self.c0b[u % 3]
            ub = slice(un[0], un[0] + 4)
            Gu = self.G[:, ub, :].rearrange("p b t -> p (b t)")
            for j, b in enumerate(un):
                ts_ = slice(j * 128, j * 128 + 128)
                n += 1
                nxt = decay(n + 1) if n + 1 < len(seq) else iter(())
                e, k = E[n % 2], n % 2
                e1, e2, tz = ahead.pop(n)
                S.mm(B2[:, 256:384], cv[0:64, 2, ts_], C0[0:64, ts_], True, True, tth, fb[2])
                for c in range(2):
                    t = S.tr(B2[:, c * 128:c * 128 + 128], cv[:, c, ts_], self.ident[:], tth, self.tI)
                tcbm = S.tt(cbm[:], B2[:, 256:384], self.triq[:], ALU.mult, t, tE, self.tTri)
                txd = S.tt(xdt[:].rearrange("p (h q) -> p h q", h=8), B2[:, 0:256].rearrange("p (h q) -> p h q", h=8),
                           bc(self.dth[:, b, :], 2, 32), ALU.mult, t, tY)
                fb[2] = [tcbm, txd]
                next(nxt, None)
                tE = S.tt(e, e, bc(cbm[:], 1, 8), ALU.mult, e1, e2, tcbm, eng="gpsimd")
                yield
                next(nxt, None)
                yield
                for c in range(2):
                    S.mm(B0[:, c * 128:c * 128 + 128], cv[:, c, ts_], self.dg[:, c, :], c == 0, False, fb[0])
                S.mm(B0[:, 256:512], C0[0:64, ts_], self.h0T[:], False, False)
                yield
                next(nxt, None)
                for h in range(8):
                    for r in range(0, 128, 32):
                        t = S.mm(B0[r:r + 32, h * 32:h * 32 + 32], e[:, h, r:r + 32], xdt[:, h * 32:h * 32 + 32],
                                 False, True, tE, txd)
                fE[k] = tY = t
                y = y4[:, j, :]
                y3 = y.rearrange("p (h q) -> p h q", h=8)
                t = S.tt(y3, B0[:, 256:512].rearrange("p (h q) -> p h q", h=8), bc(self.ec[:, b, :], 2, 32), ALU.mult,
                         t, self.tdt, t_yT)
                t = S.tt(y, y, B0[:, 0:256], ALU.add, t)
                fb[0] = t
                fz[k] = t_y = S.tt(y, y, zt[k], ALU.mult, t, tz)
                tss = S.actsum(sq[:], y, ACT.Square, ss[:, j:j + 1], t_y, trs, tss)
                yield
            self.cvfree[u] = tY
            t = S.ts(ss[:], ss[:], 1 / 256, 4e-5, ALU.mult, ALU.add, tss)
            t = S.recip(ss[:], ss[:], t)
            t = S.act(ss[:], ss[:], ACT.Sqrt, t)
            for j in range(4):
                trs = S.ts(y4[:, j, :], y4[:, j, :], ss[:, j:j + 1], None, ALU.mult, None, t, t_y)
            yield
            yield
            for h in range(2):
                for j in (2 * h, 2 * h + 1):
                    for c in range(2):
                        t = S.tr(B2[:, (j % 2) * 256 + c * 128:(j % 2) * 256 + c * 128 + 128], y4[:, j, c * 128:c * 128 + 128],
                                 self.ident[:], trs, fb[2])
                t_yT = t
                fb[2] = S.act(yT[:, :, h * 256:h * 256 + 256].rearrange("p c (j t) -> p j c t", j=2),
                              B2[:].rearrange("p (j c t) -> p j c t", j=2, c=2), ACT.Copy, t, tyT)
            t = fb[2]
            yield
            for c in range(2):
                tw_ = S.mm(B0[:], self.wout[:, c, :], yT[:, c, :], c == 0, c == 1, t, fb[0], self.tmw)
            tyT = tw_
            t1 = S.act(tm1[:], B0[:], ACT.Square, tw_, ttm)
            t1 = S.ts(tm1[:], tm1[:], 1.0, None, ALU.add, None, t1)
            yield
            t1 = S.recip(tm1[:], tm1[:], t1)
            t1 = S.act(tm1[:], tm1[:], ACT.Sqrt, t1)
            for _ in range(self.WY):
                yield
            t1 = S.tt(tm1[:], tm1[:], B0[:], ALU.mult, t1)
            fb[0] = t1
            yield
            t2 = S.mm(B1[:], self.wnl[:], tm1[:], True, True, t1, fb[1])
            ttm = t2
            Xu = self.X[:, ub, :].rearrange("p b t -> p (b t)")
            t3 = S.stt(Xu, B1[:], self.bnl[:], Xu, ALU.add, ALU.add, t2, self.tX)
            fb[1] = t3
            t4 = S.tt(Xu, Xu, Gu, ALU.add, t3, eng="gpsimd")
            self.done.append(t4)
            yield

    def cond2_biases(self):
        p, I = self.p, self.I
        self.ckc = p.sb("ckc", [128, 2, 8])[:]
        self.bo = p.sb("cbo", [128, 1])[:]
        self.bv = p.sb("cbv", [128, 8])
        row = lambda v: v.rearrange("(p o) -> p o", o=1)
        self.tcb = self.loads([(self.bo, row(I["L0_cond2_WO_b"]))] +
                              [(d[:, c:c + 1], row(I[n][c * 128:c * 128 + 128]))
                               for c in range(8) for d, n in ((self.ckc[:, 0, :], "L0_cond2_WQ_b"),
                                                              (self.ckc[:, 1, :], "L0_cond2_WK_b"),
                                                              (self.bv, "L0_cond2_WV_b"))])

    def cond2_prep(self, banks=(0, 1)):
        p, I = self.p, self.I
        S = Stage(p, "cprep")
        ca = [self.catt, 0]
        ar = lambda *s, dt=F32: self.area(ca, list(s), dt)
        self.WQ, self.WK, self.WO = ar(128, 8, 128), ar(128, 8, 128), ar(128, 8, 128)
        self.Gak = ar(128, NB, 16)
        self.cak = ar(128, NB, 16)
        self.avo = ar(16, NB, 128)
        self.a0 = [ar(16, 512) for _ in range(2)]
        w = [self.work, 54 * 256]
        WV = self.area(w, [128, 8, 128])
        akb = self.area(w, [128, 8, 2, 32])
        avb = self.area(w, [128, 8, 2, 32])
        wqT = self.area(w, [128, 8, 128])
        bqb = self.area(w, [128, 8, 128])
        avt = self.area([self.work, 8416], [64, 8, 128])
        bv = self.bv
        self.blk = p.sb("blk", [128, 2])
        self.selc = p.sb("selc", [48, 16, 64], BF16)
        W = lambda n: I[n].rearrange("k (c m) -> k c m", c=8)
        col = lambda n: I[n].rearrange("(c p) -> p c", p=128)
        lv = [self.load(self.WK, W("L0_cond2_WK_w"), self.wfree, eng="scalar"),
              self.load(WV, W("L0_cond2_WV_w"), self.wfree), self.tcb]
        ld = [lv, self.load(self.WO, I["L0_cond2_WO_w"].rearrange("(c p) n -> p c n", p=128), self.wfree),
              self.load(self.WQ, W("L0_cond2_WQ_w"), self.wfree, eng="scalar")]
        z = S.memset(akb, 0.0, self.wfree)
        z2 = S.memset(avb, 0.0, self.wfree)
        t = S.sel(self.blk[:], self.ones[:, 0:2], ALU.is_ge, 0.0, 0, [[-64, 2]], 1, self.tI, self.tIb, self.tTri)
        self.tblk = S.sel(self.blk[:], self.blk[:], ALU.is_ge, 0.0, 63, [[64, 2]], -1, t)
        t = S.memset(self.selc[:], 0.0)
        for part in range(3):
            t = S.sel(self.selc[:], self.selc[:], ALU.not_equal, 1.0, -16 * part, [[-1, 16], [0, 64]], 1, t)
        self.tsel = t
        B0, B1 = self.bank[banks[0]], self.bank[banks[1]]
        for c in range(8):
            S.mm(B0[:, c * 32:c * 32 + 32], self.WK[:, c, :], self.condT[:], True, True, lv, self.tcond, self.wfree)
            t = S.mm(B0[:, 256 + c * 32:288 + c * 32], WV[:, c, :], self.condT[:], True, True)
        for i in range(2):
            r = slice(64 * i, 64 * i + 64)
            for d, o, b_, zz in ((akb, 0, self.ckc[:, 1, :], z), (avb, 256, bv[:], z2)):
                t1 = S.tt(d[r, :, i, :], B0[r, o:o + 256].rearrange("p (c b) -> p c b", c=8), bc(b_[r], 2, 32), ALU.add,
                          t, zz)
        f0 = t1
        f = [f0, None]
        for g in range(2):
            Bk = (B0, B1)[g]
            for i in range(4):
                c = 4 * g + i
                t = S.mm(Bk[0:64, i * 128:i * 128 + 128], avb[:, c].rearrange("p i b -> p (i b)"), self.WO[:, c, :],
                         True, True, f[g], f0, ld, self.wfree)
            f[g] = S.act(avt[:, 4 * g:4 * g + 4, :].rearrange("p c m -> p (c m)"), Bk[0:64, :], ACT.Copy, t)
        self.tavo = self.loads([(self.avo[2 * c + i:2 * c + i + 1, :, :], avt[32 * i:32 * i + 32, c, :])
                                for c in range(8) for i in range(2)], f)
        f0, f1 = [f0, f[0]], f[1]
        for g in range(2):
            for i in range(4):
                t = S.tr(B1[:, i * 128:i * 128 + 128], self.WQ[:, 4 * g + i, :], self.ident[:], ld, self.tI, f1, self.wfree)
            f1 = S.act(wqT[:, 4 * g:4 * g + 4, :].rearrange("p c m -> p (c m)"), B1[:], ACT.Copy, t)
        tb = S.cp(bqb, bc(self.ckc[:, 0, :], 2, 128), ld)
        for c in range(8):
            t = S.mm(B0[:, c * 64:c * 64 + 64], wqT[:, c, :], akb[:, c].rearrange("p i b -> p (i b)"), True, True, f0, f1)
        t2 = S.act(self.Gak.rearrange("p b (c i) -> p c i b", c=8), B0[:].rearrange("p (c i b) -> p c i b", c=8, i=2),
                   ACT.Copy, t)
        for c in range(8):
            t = S.mm(B1[:, c * 64:c * 64 + 64], bqb[:, c, :], akb[:, c].rearrange("p i b -> p (i b)"), True, True, f1, tb)
        t3 = S.act(self.cak.rearrange("p b (c i) -> p c i b", c=8), B1[:].rearrange("p (c i b) -> p c i b", c=8, i=2),
                   ACT.Copy, t)
        self.wqk = [[self.hr[2 * i + h] for h in range(2)] for i in range(2)]
        tw = []
        for i, W_ in enumerate((self.WQ, self.WK)):
            for h in range(2):
                x, d = W_[:, 4 * h:4 * h + 4, :].rearrange("p c m -> p (c m)"), self.wqk[i][h]
                t = S.act(d[0][:], x, ACT.Copy, ld)
                tw.append(S.tt(d[1][:], x, d[0][:].bitcast(F32), ALU.subtract, t))
        self.tcw = [ld, t2, t3, tw]
        self.wlow = self.wfree
        self.wfree = self.wfree + [f, t2, t3]
        self.tb0, self.tb1 = t2, t3

    def cond2(self, bs=range(NB), workers=2):
        w = [self.work, 0]
        units = [list(bs)[i:i + 4] for i in range(0, len(bs), 4)]
        self.done = []
        return [self.cond2_worker(k, units[k::workers], w) for k in range(workers)]

    def cond2_worker(self, wk, units, w):
        S = Stage(self.p, f"cond2{wk}")
        free = self.wfree if wk else self.wlow
        self.open.append(S)
        ar = lambda *s, dt=F32: self.area(w, list(s), dt)
        Bs = self.bank[3 * wk + 2]
        ring = [self.bank[i] for i in (3 * wk, 3 * wk + 1, 6 + wk)]
        KP = ar(128, 8, 4, 130)
        pr = [ar(128, 512) for i in range(5)]
        sc = ar(128, 64, 4)
        m = ar(128, 64)
        sm = ar(128, 64)
        R = ar(128, 64, 4)
        A = ar(128, 4 * 3, 48, dt=BF16)
        AT = ar(48, 3, 512, dt=BF16)
        a0 = self.a0[wk]
        att = [ar(128, 512) for i in range(2)]
        tpad = S.memset(KP[:, :, :, 0:1], 0.0, free)
        tpad = S.memset(KP[:, :, :, 129:130], 0.0, free, tpad)
        fs = [self.tb0, self.tb1, self.tcw, free]
        fr = [fs] * 3
        r_ = 0
        fKP = [free] * 8
        fpr = [free] * 5
        x = 0
        tex = tA = tAT = ta0 = None
        xr, fxr = self.gr[wk], None
        fatt = [self.tavo, self.tavo]
        for _ in range(self.lag2 * wk):
            yield
        for un in units:
            ub = slice(un[0], un[0] + 4)
            Xu = self.X[:, ub, :].rearrange("p b t -> p (b t)")
            t = S.act(xr[0][:], Xu, ACT.Copy, self.tX, fxr)
            txr = [t, S.tt(xr[1][:], Xu, xr[0][:].bitcast(F32), ALU.subtract, t)]
            S3 = Bs[:, 0:256].rearrange("p (b h j) -> p b h j", b=4, h=16)
            for i, b in enumerate(un):
                for r in range(0, 128, 32):
                    t = S.mm(S3[r:r + 32, i, :, 0], self.X[:, b, r:r + 32], self.Gak[:, b, :], i == 0, False,
                             fs, self.tcw, self.tX)
            for c in range(8):
                iq, ik = r_ % 3, (r_ + 1) % 3
                r_ += 2
                Bq, Bk = ring[iq], ring[ik]
                wq, wk_ = ([x[:, c % 4 * 128:c % 4 * 128 + 128] for x in w_[c // 4]] for w_ in self.wqk)
                tk = self.mm3(S, Bk[:], wk_, [x[:] for x in xr], True, True, fr[ik], txr, self.tcw, self.tX)
                tq = self.mm3(S, Bq[:], wq, [x[:] for x in xr], True, True, fr[iq])
                fxr = tq
                fr[ik] = tk = S.act(KP[:, c, :, 1:129], Bk[:].rearrange("p (b t) -> p b t", b=4), ACT.Identity, tk, fKP[c],
                                bias=self.ckc[:, 1, c:c + 1])
                yield
                tp, xs = [], []
                for j in range(3):
                    x = (x + 1) % 5
                    xs.append(x)
                    fr[iq] = S.stt(pr[x].rearrange("p (b t) -> p b t", b=4), Bq[:].rearrange("p (b t) -> p b t", b=4),
                               self.ckc[:, 0, c:c + 1], KP[:, c, :, j:j + 128], ALU.add, ALU.mult, tq, tk, fpr[x], tpad)
                    tp.append(fr[iq])
                yield
                for j in range(3):
                    for i in range(4):
                        for r in range(0, 128, 32):
                            ts = S.mm(S3[r:r + 32, i, 2 * c:2 * c + 2, j + 1],
                                      pr[xs[j]][:, i * 128 + r:i * 128 + r + 32], self.blk[:], False, False,
                                      tp[j], self.tblk)
                    fpr[xs[j]] = ts
                yield
            S4 = sc.rearrange("p (b h) j -> p b h j", b=4)
            t = S.act(sc, S3.rearrange("p b h j -> p (b h) j"), ACT.Copy, ts, tA)
            t = S.tt(S4[:, :, :, 0], S4[:, :, :, 0], self.cak[:, ub, :], ALU.add, t)
            fs = t
            t = S.red(m, sc, ALU.max, t)
            t = S.tt(sc, sc, bc(m, 2, 4), ALU.subtract, t)
            t = S.act(sc, sc, ACT.Exp, t, scale=0.125)
            t = S.red(sm, sc, ALU.add, t)
            t = S.recip(sm, sm, t)
            t = S.tt(sc, sc, bc(sm, 2, 4), ALU.mult, t)
            Av = A.rearrange("p (b j) (q h) -> p b j q h", b=4, q=3)
            Sv = sc.rearrange("p (b h) j -> p b j h", b=4)
            Rb = R.rearrange("p x y -> p (x y)").rearrange("p (b j h) -> p b j h", b=4, j=4)
            A3, S3_, R3 = (lambda k: Av[:, :, :, k, :]), Sv[:, :, 1:4, :], Rb[:, :, 1:4, :]
            ta = S.cp(A3(0), S3_, t, tAT)
            tb = S.tt(R3, S3_, A3(0), ALU.subtract, ta)
            ta = S.cp(A3(1), R3, tb)
            tb = S.tt(R3, R3, A3(1), ALU.subtract, ta)
            tA = S.cp(A3(2), R3, tb)
            yield
            yield
            for i in range(4):
                t1 = S.tr(Bs[0:16, i * 128:i * 128 + 128], Sv[:, i, 0, :], self.ident[:], t, self.tI)
            ta0 = S.act(a0, Bs[0:16, :], ACT.Copy, t1, ta0)
            fs = ta0
            tAT_r = []
            for j in range(3):
                k = r_ % 3
                r_ += 1
                Bt = ring[k][:].bitcast(BF16)
                for i in range(4):
                    t1 = S.tr(Bt[0:48, i * 128:i * 128 + 128], Av[:, i, j, :, :].rearrange("p q h -> p (q h)"),
                              self.identb[:], tA, self.tIb, fr[k])
                fr[k] = S.act(AT[:, j, :], Bt[0:48, 0:512], ACT.Copy, t1, tAT)
                tAT_r.append(fr[k])
            yield
            for i, b in enumerate(un):
                to = S.mm(Bs[:, i * 128:i * 128 + 128], self.avo[:, b, :], a0[:, i * 128:i * 128 + 128], i == 0, False,
                          ta0, fs, self.tavo)
            tex = to
            late = []

            def wo(c, av, t):
                def go():
                    nonlocal to
                    fatt[c % 2] = to = S.mm(Bs[:], self.WO[:, c, :], av, False, c == 7, t)
                return go
            for c in range(8):
                prods, xs = [], []
                for j in range(3):
                    x = (x + 1) % 5
                    xs.append(x)
                    k = r_ % 3
                    r_ += 1
                    Bb, fb = ring[k], fr[k]
                    t1 = S.mm(Bb[:], self.selc[:, 2 * c:2 * c + 2, :].rearrange("p h d -> p (h d)"), AT[:, j, :], True, True,
                              tAT_r, self.tsel, fb)
                    tAT = t1
                    t2 = S.tt(pr[x].rearrange("p (b t) -> p b t", b=4), Bb[:].rearrange("p (b t) -> p b t", b=4),
                              KP[:, c, :, j:j + 128], ALU.mult, t1, fpr[x])
                    prods.append(t2)
                    fr[k] = t2
                    if j < 2:
                        yield
                if len(late) > 1:
                    late.pop(0)()
                fKP[c] = t2
                av = att[c % 2]
                u0, u1, u2 = (pr[v] for v in xs)
                t3 = S.tt(av, u0, u1, ALU.add, prods[1], fatt[c % 2], eng="gpsimd")
                fpr[xs[0]] = fpr[xs[1]] = t3
                t3 = S.tt(av, av, u2, ALU.add, t3, prods[2], eng="vector" if c in self.VC else "gpsimd")
                fpr[xs[2]] = t3
                late.append(wo(c, av, t3))
                yield
            for g in late:
                g()
                yield
            t = S.act(self.G[:, ub, :].rearrange("p b t -> p (b t)"), Bs[:], ACT.Identity, to, self.tGfree, bias=self.bo)
            fs = t
            self.done.append(t)
            yield

    def moe_load(self, li):
        I, E = self.I, 8 + li
        self.wraw = self.area([self.catt, 0], [128, E, 768])
        ng, nu, nd = (("L0_ffn_kernel_gating_EDF", "L0_ffn_kernel_up_EDF", "L0_ffn_kernel_down_EFD"),
                      ("L1_ffn_ew1", "L1_ffn_ew2", "L1_ffn_ew3"))[li]
        self.rw = self.p.sb(f"rw{li}", [128, 8])
        self.rb = self.p.sb(f"rb{li}", [128, 8])
        self.trw = self.loads([(self.rw[:], I[("L0_ffn_router_kernel_DE", "L1_ffn_rw")[li]])] +
                              ([(self.rb[:], bc(I["L1_ffn_rb"], 0, 128))] if li else []))
        self.twe = []
        for e in range(E):
            g, u, d = (I[ng][e], I[nu][e], I[nd][e]) if e < 8 else (I["L1_ffn_sw1"], I["L1_ffn_sw2"], I["L1_ffn_sw3"])
            self.twe.append(self.loads([(self.wraw[:, e, 0:256], g), (self.wraw[:, e, 256:512], u),
                                        (self.wraw[:, e, 512:768].rearrange("p (c d) -> p c d", c=2),
                                         d.rearrange("(c f) d -> f c d", c=2))],
                                       self.moefree, eng=("sync", "scalar")[e % 2] if li == 0 else "sync"))

    def moe_route(self, li, bs, bank, w):
        p = self.p
        S = Stage(p, f"route{li}")
        self.open.append(S)
        n = len(bs)
        ar = lambda *s, dt=F32: self.area(w, list(s), dt)
        if self.rev is None:
            self.rev = p.sb("rev", [128, 8])
            for e in range(8):
                self.trev = self.S0.memset(self.rev[:, e:e + 1], float(8 - e), eng="vector")
            self.selw = p.sb("selw", [24, 8, 128], BF16)
            t = self.S0.memset(self.selw[:], 0.0, self.tI)
            for part in range(3):
                t = self.S0.sel(self.selw[:], self.selw[:], ALU.not_equal, 1.0, -8 * part, [[-1, 8], [0, 128]], 1, t)
            self.tselw = t
        pr, f1, f2, mk = (ar(128, n, 8) for _ in range(4))
        m1, m2, q1, q2 = (ar(128, n) for _ in range(4))
        Wp = ar(128, n, 24, dt=BF16)
        WT = ar(24, n * 128, dt=BF16)
        B = self.bank[bank]
        P = B[:, 0:8 * n].rearrange("p (b e) -> p b e", e=8)
        for i, b in enumerate(bs):
            t = S.mm(P[:, i, :], self.G[:, b, :], self.rw[:], True, True, self.tG, self.trw, self.wfree)
        if li:
            t = S.stt(pr, P, 0.5, bc(self.rb[:], 1, n), ALU.mult, ALU.add, t, self.wfree)
        else:
            t = S.cp(pr, P, t, self.wfree)
        t = S.red(m1, pr, ALU.max, t)
        t = S.tt(pr, pr, bc(m1, 2, 8), ALU.subtract, t)
        t = S.act(pr, pr, ACT.Exp, t)
        t = S.red(m1, pr, ALU.add, t)
        t = S.recip(m1, m1, t)
        t = S.tt(pr, pr, bc(m1, 2, 8), ALU.mult, t)
        for k, (m, f, q) in enumerate(((m1, f1, q1), (m2, f2, q2))):
            t = S.red(m, pr, ALU.max, t)
            t = S.tt(mk, pr, bc(m, 2, 8), ALU.is_equal, t)
            t = S.tt(mk, mk, bc(self.rev[:], 1, n), ALU.mult, t, self.trev)
            t = S.red(q, mk, ALU.max, t)
            t = S.tt(f, mk, bc(q, 2, 8), ALU.is_equal, t)
            if k == 0:
                t = S.stt(pr, f, -4.0, pr, ALU.mult, ALU.add, t)
        if li:
            t = S.tt(q1, m1, m2, ALU.add, t)
            t = S.recip(q1, q1, t)
            t1 = S.tt(m1, m1, q1, ALU.mult, t)
            t2 = S.tt(m2, m2, q1, ALU.mult, t)
        else:
            t = S.tt(q1, m2, m1, ALU.subtract, t)
            t = S.act(q1, q1, ACT.Exp, t)
            t = S.ts(q2, q1, 1.0, None, ALU.add, None, t)
            t1 = S.recip(m1, q2, t)
            t2 = S.tt(m2, q1, m1, ALU.mult, t1)
        t = S.tt(f1, f1, bc(m1, 2, 8), ALU.mult, t1, t2)
        t = S.tt(f2, f2, bc(m2, 2, 8), ALU.mult, t)
        t = S.tt(f1, f1, f2, ALU.add, t)
        t = S.cp(Wp[:, :, 0:8], f1, t)
        t = S.tt(f1, f1, Wp[:, :, 0:8], ALU.subtract, t)
        t = S.cp(Wp[:, :, 8:16], f1, t)
        t = S.tt(f1, f1, Wp[:, :, 8:16], ALU.subtract, t)
        t = S.cp(Wp[:, :, 16:24], f1, t)
        Bb = B[:].bitcast(BF16)
        f = None
        for i0 in range(0, n, 8):
            for i in range(8):
                tm = S.tr(Bb[0:24, i * 128:i * 128 + 128], Wp[:, i0 + i, :], self.identb[:], t, self.tIb, f)
            f = S.act(WT[:, i0 * 128:i0 * 128 + 1024], Bb[0:24, :], ACT.Copy, tm)
        self.tWT = [f]
        return WT

    def moe(self, li, bs=range(NB)):
        self.moe_load(li)
        self.done = []
        return [self.moe_lane(li, bs)]

    def moe_lane(self, li, bs):
        w = [self.work, 0]
        ar = lambda *s, dt=F32: self.area(w, list(s), dt)
        WT = self.moe_route(li, bs, 5, w)
        yield
        S = Stage(self.p, f"moe{li}")
        self.open.append(S)
        sg = [ar(128, 512) for _ in range(2)]
        pu = [ar(128, 512) for _ in range(2)]
        NH = len(self.hr)
        hh = [ar(128, 512) for _ in range(NH)]
        ot = ar(128, 512)
        og = ar(128, 512)
        wr, gr, hr = self.wr, self.gr, self.hr
        bank = self.bank
        BG, BU, BO, BW = bank[0:2], bank[2:4], bank[4:6], bank[6:8]
        fG, fU = [self.wfree] * 2, [self.wfree] * 2
        fW = [self.wfree] * 2
        fO = [[self.wfree, self.tWT]] * 2
        fwr = [self.moefree] * 2
        fgr = [self.moefree] * 2
        fh, fhr, fsg, fpu = [self.wfree] * NH, [self.moefree] * NH, [self.wfree] * 2, [self.wfree] * 2
        tot = None
        E = 8 + li
        units = [list(bs)[i:i + 4] for i in range(0, len(bs), 4)]
        groups = [units[i:i + 2] for i in range(0, len(units), 2)]
        flat = lambda T_, un: T_[:, un[0]:un[0] + 4, :].rearrange("p b t -> p (b t)")

        def split(n):
            d, x = wr[n % 2], self.wraw[:, n % E, :]
            t = S.act(d[0][:], x, ACT.Copy, self.twe[n % E], fwr[n % 2])
            return [t, S.tt(d[1][:], x, d[0][:].bitcast(F32), ALU.subtract, t)]

        late = []

        def down(e, fc, q, k, th, un, n):
            nonlocal tot
            first, last = (e == 0 and fc == 0), (e == E - 1 and fc == 1)
            wd = [x[:, 512 + fc * 128:640 + fc * 128] for x in wr[n % 2]]
            B = BO[q]
            t = self.mm3(S, B[:], wd, [x[:] for x in hr[k]], first, last, th, fO[q] if first else None)
            fhr[k] = t
            if q == 1 and fc == 1:
                fwr[n % 2] = t
            if last:
                Xu = flat(self.X, un)
                if not li:
                    fO[q] = S.tt(Xu, Xu, B[:], ALU.add, t, self.tX)
                    self.done.append(fO[q])
                else:
                    t2 = S.tt(ot, Xu, B[:], ALU.add, t, self.tX, tot)
                    for i in range(4):
                        t3 = S.tr(B[:, i * 128:i * 128 + 128], ot[:, i * 128:i * 128 + 128], self.ident[:], t2, self.tI)
                    tot = t3
                    fO[q] = S.act(og, B[:], ACT.Copy, t3, self.done[-1] if self.done else None)
                    self.done.append(self.load(self.out[un[0]:un[0] + 4].rearrange("b t d -> t b d"),
                                               og.rearrange("p (b d) -> p b d", b=4), fO[q], counter=self.cout))
        def part(e, fc, q, m, t3, un, n):
            def go():
                t4 = S.act(hr[m][0][:], hh[m], ACT.Copy, t3, fhr[m])
                fh[m] = t5 = S.tt(hr[m][1][:], hh[m], hr[m][0][:].bitcast(F32), ALU.subtract, t4, eng="gpsimd")
                late.append((e, fc, q, m, [t4, t5], un, n))
            return go
        parts = []
        k = n = 0
        tw = split(0)
        for gi, grp in enumerate(groups):
            tg = []
            for q, un in enumerate(grp):
                t = S.act(gr[q][0][:], flat(self.G, un), ACT.Copy, self.tG, fgr[q])
                tg.append([t, S.tt(gr[q][1][:], flat(self.G, un), gr[q][0][:].bitcast(F32), ALU.subtract, t)])
            for e in range(E):
                a = wr[n % 2]
                twn = tw
                for q, un in enumerate(grp):
                    b = [x[:] for x in gr[q]]
                    u = 2 * gi + q
                    if e < 8:
                        W_ = BW[q]
                        tW = S.mm(W_[:], self.selw[:, e, :], WT[:, u * 512:u * 512 + 512], True, True, self.tWT,
                                  self.tselw, fW[q])
                    for fc in range(2):
                        i, m = k % 2, k % NH
                        G_, U_ = BG[i], BU[i]
                        c = slice(fc * 128, fc * 128 + 128)
                        cu = slice(256 + fc * 128, 384 + fc * 128)
                        t1 = self.mm3(S, G_[:], [x[:, c] for x in a], b, True, True, fG[i], twn, tg[q])
                        fG[i] = t1 = S.act(sg[i], G_[:], ACT.Silu, t1, fsg[i], scale=0.5 if li else 1.0)
                        t2 = self.mm3(S, U_[:], [x[:, cu] for x in a], b, True, True, fU[i])
                        fgr[q] = t2
                        if e < 8:
                            fsg[i] = fW[q] = t3 = S.tt(pu[i], sg[i], W_[:], ALU.mult, t1, tW, fpu[i])
                            src = pu[i]
                        else:
                            src, t3 = sg[i], t1
                        if li:
                            t3 = S.stt(hh[m], U_[:], 0.5, src, ALU.mult, ALU.mult, t2, t3, fh[m])
                        else:
                            t3 = S.tt(hh[m], U_[:], src, ALU.mult, t2, t3, fh[m])
                        fU[i] = fpu[i] = t3
                        if e == 8:
                            fsg[i] = t3
                        if parts:
                            parts.pop()()
                        parts.append(part(e, fc, q, m, t3, un, n))
                        if len(late) > self.LD:
                            down(*late.pop(0))
                        k += 1
                        if q == 1 and fc == 0 and n + 1 < E * len(groups):
                            tw = split(n + 1)
                        yield
                n += 1
        parts.pop()()
        while late:
            down(*late.pop(0))
        yield

    def attn_prep(self, bank=0, waits=None):
        p, I = self.p, self.I
        S = Stage(p, "aprep")
        ca = [self.catt, 0]
        ar = lambda *s, dt=F32: self.area(ca, list(s), dt)
        self.awT = [ar(128, 128) for _ in range(4)]
        self.ab = ar(128, 4)
        self.bvb = ar(128, 128)
        self.bS = ar(128, 16, 128, dt=BF16)
        self.bT = [ar(128, 16, 128, dt=BF16) for _ in range(3)]
        raw = ar(128, 4, 128)
        oh = ar(96, 512)
        ohb = ar(96, 512, dt=BF16)
        rel = ar(96, 16)
        relb = ar(96, 16, dt=BF16)
        bf = ar(128, 16, 32)
        self.aP = [ar(128, 4, 128) for _ in range(4)]
        col = lambda n: I[n].rearrange("(p o) -> p o", o=1)
        ld = self.loads([(raw[:, i, :], I["L1_attn_w" + c]) for i, c in enumerate("qkvo")] +
                        [(self.ab[:, 0:1], col("L1_attn_bq")), (self.ab[:, 1:2], col("L1_attn_bk")),
                         (self.ab[:, 3:4], col("L1_attn_bo")), (self.bvb, bc(I["L1_attn_bv"], 0, 128))] +
                         [(oh[32 * i:32 * i + 32], I["onehot"]) for i in range(3)] +
                        [(rel[32 * i:32 * i + 32], I["L1_attn_rel_bias"]) for i in range(3)], self.cattfree, eng="scalar")
        B = self.bank[bank]
        for _ in range(6):
            yield
        for i in range(4):
            t = S.tr(B[:, i * 128:i * 128 + 128], raw[:, i, :], self.ident[:], ld, self.tI, waits, self.tcond)
        for i in range(4):
            f = S.act(self.awT[i], B[:, i * 128:i * 128 + 128], ACT.Copy, t)
        t0 = S.ts(self.ab[:, 0:1], self.ab[:, 0:1], 8 ** -0.5, None, ALU.mult, None, ld)
        tr_ = ld
        for i in range(3):
            for j in range(i, 3):
                r = slice(32 * j, 32 * j + 32)
                tr_ = S.cp(relb[r], rel[r], tr_)
                if j > i:
                    tr_ = S.tt(rel[r], rel[r], relb[r], ALU.subtract, tr_)
        tr_ = [tr_, S.cp(ohb, oh, ld)]
        tw = [f, t0, ld]
        tb = None
        yield
        for g in range(4):
            for q in range(32):
                o = 256 + 127 - (32 * g + q)
                t = S.mm(B[:, q * 16:q * 16 + 16], ohb[:, o:o + 128], relb, True, True, tr_, f)
            o3 = bf.rearrange("p h q -> p q h")
            t = S.act(o3, B[:].rearrange("p (q h) -> p q h", h=16), ACT.Copy, t, tb)
            f = t
            v = [x[:, :, 32 * g:32 * g + 32] for x in self.bT]
            t = S.cp(v[0], bf, t)
            t = S.tt(bf, bf, v[0], ALU.subtract, t)
            t = S.cp(v[1], bf, t)
            t = S.tt(bf, bf, v[1], ALU.subtract, t)
            tb = S.cp(v[2], bf, t)
            yield
        for g in range(4):
            for k in range(32):
                o = 127 - (32 * g + k)
                t = S.mm(B[:, k * 16:k * 16 + 16], ohb[:, o:o + 128], relb, True, True, f)
            f = S.act(self.bS[:, :, 32 * g:32 * g + 32].rearrange("p h k -> p k h"),
                      B[:].rearrange("p (k h) -> p k h", h=16), ACT.Copy, t)
            yield
        self.taw = tw + [tb, f]
        self.afree = f

    def attn(self, bs=range(NB), workers=2):
        w = [self.work, 0]
        self.scr = [[self.p.nc.dram_tensor(f"scr{k}{i}", [128, 3, 256], BF16, kind="Internal").ap() for i in range(2)]
                    for k in range(workers)]
        units = [list(bs)[i:i + 2] for i in range(0, len(bs), 2)]
        self.done = []
        return [self.attn_worker(k, units[k::workers], w) for k in range(workers)]

    def attn_worker(self, wk, units, w):
        S = Stage(self.p, f"attn{wk}")
        self.open.append(S)
        ar = lambda *s, dt=F32: self.area(w, list(s), dt)
        banks = self.bank[3 * wk:3 * wk + 3]
        oT = ar(128, 256)
        q32 = [ar(128, 256), oT]
        pq, pk = ar(128, 3, 256, dt=BF16), ar(128, 3, 256, dt=BF16)
        parts = [[x[:, i, :] for i in range(3)] for x in (pq, pk)]
        cw = self.p.counter(f's_attnw{wk}')
        Q = ar(51, 16, 256, dt=BF16)
        Kt = ar(51, 16, 256, dt=BF16)
        V = ar(128, 2 * 16, 96)
        nm = ar(128, 2, 16)
        nr = ar(128, 2, 16)
        np_ = ar(128, 2, 48, dt=BF16)
        nT = ar(48, 256, dt=BF16)
        P = [self.aP[2 * wk + i] for i in range(2)]
        rc = ar(128, 16)
        o = ar(128, 128)
        cdma = self.p.counter(f"s_attnq{wk}")
        cdma2 = self.p.counter(f"s_attnm{wk}")
        tone = S.memset(Kt[32:51], 1.0, self.wfree, eng="vector")
        tone2 = S.memset(V, 0.0, self.wfree)
        tone2 = S.memset(V[:, :, 8:9], 1.0, tone2)
        f = [[self.afree, self.wfree], self.wfree, self.wfree]
        tQ = tV = tP = tm_ = to = toT = tnm = tpv = td = tdb = None
        fP = [None, None]

        def pv(i, g, k, te):
            def go():
                nonlocal tpv, to
                for h in range(4):
                    hh = 4 * g + h
                    t = S.mm(B2[:, hh * 9:hh * 9 + 96], P[k][:, h, :], V[:, 16 * i + hh, :], hh == 0, True,
                             te, tV, tone2, f[2])
                fP[k] = t
                if g == 3:
                    tpv = t
                    O = B2[:, 0:144].rearrange("p (h d) -> p h d", h=16)
                    t = S.recip(rc, O[:, :, 8], tpv, to)
                    t = S.tt(o.rearrange("p (h d) -> p h d", h=16), O[:, :, 0:8], bc(rc, 2, 8), ALU.mult, t, to)
                    f[2] = t
                    late.append(lambda: transpose(i, t))
            return go

        def transpose(i, t):
            nonlocal to
            to = t1 = S.tr(B2[:, 256:384], o, self.ident[:], t)
            f[2] = S.act(oT[:, i * 128:i * 128 + 128], B2[:, 256:384], ACT.Copy, t1, toT)
        late = []
        B0, B1, B2 = banks
        for _ in range(self.R3 * wk):
            yield
        for un in units:
            ub = slice(un[0], un[0] + 2)
            Gu = self.G[:, ub, :].rearrange("p b t -> p (b t)")
            B0, B1, B2 = banks
            t1 = S.mm(B0[:, 0:256], self.awT[0], Gu, True, True, f[0], self.tG, self.taw)
            t1 = S.mm(B0[:, 256:512], self.awT[1], Gu, True, True)
            t2 = None
            for i, b in enumerate(un):
                t2 = S.mm(B1[:, i * 128:i * 128 + 128], self.G[:, b, :], self.awT[2], True, True, f[1])
            for i in range(2):
                ta = S.act(q32[i], B0[:, 256 * i:256 * i + 256], ACT.Identity, t1, tQ, toT, bias=self.ab[:, i:i + 1],
                           scale=0.5 * (8 ** -0.5 if i == 0 else 1.0))
                pa = parts[i]
                t = S.cp(pa[0], q32[i], ta, td)
                t = S.tt(q32[i], q32[i], pa[0], ALU.subtract, t)
                t = S.cp(pa[1], q32[i], t)
                t = S.tt(q32[i], q32[i], pa[1], ALU.subtract, t)
                tQ = S.cp(pa[2], q32[i], t)
            f[0] = ta
            for i in range(2):
                tV = S.stt(V[:, 16 * i:16 * i + 16, 0:8], B1[:, i * 128:i * 128 + 128].rearrange("p (h d) -> p h d", h=16), 0.5,
                           self.bvb.rearrange("p (h d) -> p h d", h=16), ALU.mult, ALU.add, t2, tpv, tone2, self.taw)
            f[1] = tV
            yield
            sc = self.scr[wk]
            td = self.load(sc[0], pq[:], tQ, tdb, counter=cw)
            td = self.load(sc[1], pk[:], tQ, tdb, counter=cw, eng="sync")
            tdb = []
            for dst, s_, row, lo, hi in ((Kt, 1, 0, 0, 0), (Kt, 1, 1, 0, 0), (Kt, 1, 2, 0, 0), (Kt, 1, 3, 1, 1),
                                         (Kt, 1, 4, 1, 1), (Kt, 1, 5, 2, 2), (Q, 0, 0, 0, 2), (Q, 0, 3, 0, 1), (Q, 0, 5, 0, 0)):
                for q in range(lo, hi + 1):
                    r = row + q - lo
                    src = sc[s_].rearrange("(h d) q t -> q d h t", d=8)[q]
                    tdb = self.load(dst[8 * r:8 * r + 8], src, td, tone, tpv, counter=cdma)
            tk = tdb
            for _ in range(self.R1):
                yield
            n = 0
            for i, b in enumerate(un):
                for g in range(4):
                    Bk = banks[n % 2]
                    S.mm(Bk[:], self.identb[:], self.bS[:, 4 * g:4 * g + 4, :].rearrange("p h k -> p (h k)"), True, False,
                         f[n % 2], self.taw, self.tIb)
                    for h in range(4):
                        t = S.mm(Bk[:, h * 128:h * 128 + 128], Q[0:48, 4 * g + h, i * 128:i * 128 + 128],
                                 Kt[0:48, 4 * g + h, i * 128:i * 128 + 128], False, True, tk)
                    f[n % 2] = tmx = S.red(nm[:, i, 4 * g:4 * g + 4], Bk[:].rearrange("p (h k) -> p h k", h=4), ALU.max, t, tnm)
                    n += 1
                    if n % 2 == 0:
                        yield
            t = S.ts(nm, nm, -1.0, None, ALU.mult, None, tmx)
            t = S.cp(np_[:, :, 0:16], nm, t, tnm)
            t = S.tt(nr, nm, np_[:, :, 0:16], ALU.subtract, t)
            t = S.cp(np_[:, :, 16:32], nr, t)
            t = S.tt(nr, nr, np_[:, :, 16:32], ALU.subtract, t)
            t = S.cp(np_[:, :, 32:48], nr, t)
            for _ in range(self.R5):
                yield
            Bb = B2[:].bitcast(BF16)
            for i in range(2):
                t1 = S.tr(Bb[0:48, i * 128:i * 128 + 128], np_[:, i, :], self.identb[:], t, f[2], self.tIb)
            tnm = t1
            f[2] = t = S.act(nT, Bb[0:48, 0:256], ACT.Copy, t1, tm_)
            for q in range(3):
                tm_ = self.load(Q[48 + q:49 + q, :, :], nT[16 * q:16 * q + 16, :], t, tpv, counter=cdma2)
            for _ in range(self.R2):
                yield
            n = 0
            behind = None
            for i, b in enumerate(un):
                for g in range(4):
                    Bk = banks[n % 2]
                    for k in range(3):
                        S.mm(Bk[:], self.identb[:], self.bT[k][:, 4 * g:4 * g + 4, :].rearrange("p h q -> p (h q)"),
                             k == 0, False, f[n % 2])
                    for h in range(4):
                        t = S.mm(Bk[:, h * 128:h * 128 + 128], Kt[:, 4 * g + h, i * 128:i * 128 + 128],
                                 Q[:, 4 * g + h, i * 128:i * 128 + 128], False, True, tk, tm_)
                    f[n % 2] = te = S.act(P[n % 2].rearrange("p h q -> p (h q)"), Bk[:], ACT.Exp, t, fP[n % 2])
                    if late:
                        late.pop()()
                    if behind:
                        behind()
                    behind = pv(i, g, n % 2, te)
                    n += 1
                    yield
            behind()
            for _ in range(self.R4):
                yield
            late.pop()()
            yield
            toT = t = S.mm(B2[:, 0:256], self.awT[3], oT, True, True, f[2])
            Xu = self.X[:, ub, :].rearrange("p b t -> p (b t)")
            f[2] = S.stt(Xu, B2[:, 0:256], self.ab[:, 3:4], Xu, ALU.add, ALU.add, t, self.tX)
            self.done.append(f[2])
            yield

    def all(self):
        self.load_x()
        self.stages = []
        prep = self.mamba_prep()
        next(prep)
        self.cond2_biases()
        run(self.gru(), prep)
        self.wfree = [self.tX, self.tG]

        def go(gens):
            run(*gens)
            e = [s.end() for s in self.open]
            self.open = []
            return e
        e = go(self.mamba())
        self.tX = self.done
        self.wfree = e
        self.tGfree = e
        self.cond2_prep()
        e = go(self.cond2())
        self.tG = self.done
        self.wfree = e
        self.moefree = e
        e = go(self.moe(0))
        self.tX = self.done
        self.wfree = self.tGfree = self.cattfree = e
        run((self.lstm(0), 1), (self.attn_prep(), 1))
        e = go(self.attn())
        self.tX = self.done
        self.wfree = self.tGfree = self.moefree = e
        run(self.lstm(1))
        e = go(self.moe(1))
        fin = Stage(self.p, "fin")
        fin.put("sync", lambda e: e.nop(), self.done)

    def one(self, stage, dbg):
        t1 = self.load(self.X[:], self.I["dX"])
        t2 = self.load(self.G[:], self.I["dG"])
        self.tX, self.tG, self.tGfree = [t1], [t2], [t2]
        if stage == "gru":
            run(self.gru())
        elif stage.startswith("lstm"):
            run(self.lstm(int(stage[-1])))
        elif stage == "mamba":
            run(self.mamba_prep()); run(*self.mamba()); self.tX = self.done
        elif stage == "cond2":
            self.cond2_biases(); self.cond2_prep(); run(*self.cond2()); self.tG = self.done
        elif stage == "moe0":
            run(*self.moe(0)); self.tX = self.done
        elif stage == "attn1":
            run(self.attn_prep()); run(*self.attn()); self.tX = self.done
        elif stage == "moe1":
            run(*self.moe(1)); self.tX = self.tX + self.done
        ts = [self.load(dbg[0], self.X[:], self.tX), self.load(dbg[1], self.G[:], self.tG)]
        fin = Stage(self.p, "fin")
        fin.put("sync", lambda e: e.nop(), ts)


def host_consts():
    import numpy as np
    oh = np.zeros((32, 512), np.float32)
    for j in range(255):
        oh[bucket(j - 127), j] = 1.0
        oh[bucket(j - 127), 256 + 254 - j] = 1.0
    return {"onehot": oh}


def bucket(n):
    import numpy as np
    if n < 16:
        return max(n, 0)
    v = np.log(np.float32(n) / np.float32(16)).astype(np.float32) / np.float32(np.log(128 / 16)) * np.float32(16)
    return min(16 + int(v), 31)


_INS = ['x', 'cond_1024', 'L0_cond_W_z', 'L0_cond_U_z', 'L0_cond_C_z', 'L0_cond_b_z', 'L0_cond_W_r', 'L0_cond_U_r',
        'L0_cond_C_r', 'L0_cond_b_r', 'L0_cond_W', 'L0_cond_U', 'L0_cond_C', 'L0_cond_b', 'L0_attn_W_in',
        'L0_attn_conv_w', 'L0_attn_conv_b', 'L0_attn_dt_bias', 'L0_attn_A_log', 'L0_attn_D', 'L0_attn_init_states',
        'L0_attn_norm_w', 'L0_attn_W_out', 'L0_attn_W_nl', 'L0_attn_b_nl', 'L0_cond2_WQ_w', 'L0_cond2_WQ_b',
        'L0_cond2_WK_w', 'L0_cond2_WK_b', 'L0_cond2_WV_w', 'L0_cond2_WV_b', 'L0_cond2_WO_w', 'L0_cond2_WO_b',
        'L0_ffn_router_kernel_DE', 'L0_ffn_kernel_gating_EDF', 'L0_ffn_kernel_up_EDF', 'L0_ffn_kernel_down_EFD',
        'L1_cond_Wx', 'L1_cond_Wh', 'L1_cond_b', 'L1_attn_wq', 'L1_attn_bq', 'L1_attn_wk', 'L1_attn_bk', 'L1_attn_wv',
        'L1_attn_bv', 'L1_attn_wo', 'L1_attn_bo', 'L1_attn_rel_bias', 'L1_cond2_Wx', 'L1_cond2_Wh', 'L1_cond2_b',
        'L1_ffn_sw1', 'L1_ffn_sw2', 'L1_ffn_sw3', 'L1_ffn_ew1', 'L1_ffn_ew2', 'L1_ffn_ew3', 'L1_ffn_rw', 'L1_ffn_rb']


def kernel(**inputs):
    import numpy as _np
    import concourse.bacc as _bacc
    from concourse import mybir as _mybir
    from concourse.bass_utils import run_bass_kernel_spmd as _run

    nc = _bacc.Bacc("TRN2", target_bir_lowering=False, num_devices=1)
    arrays, args = {}, {}
    data = {name: inputs[name] for name in _INS}
    data.update(host_consts())
    for name, v in data.items():
        a = _np.ascontiguousarray(v)
        arrays[f"in_{name}"] = a
        args[name] = nc.dram_tensor(f"in_{name}", a.shape, _mybir.dt.from_np(a.dtype), kind="ExternalInput").ap()
    out = nc.dram_tensor("out_0", (NB, T, D), F32, kind="ExternalOutput").ap()
    program(nc, args, out)
    r = _run(nc, [arrays], core_ids=[0])
    return r.results[0]["out_0"]
```
